# Optimizing a Trainium2 kernel written in Bass

```python
import numpy as np
import jax
import jax.numpy as jnp

def _softmax(x, axis=-1):
    return jax.nn.softmax(x, axis=axis)

def _gelu(x):
    return jax.nn.gelu(x, approximate=True)

def _silu(x):
    return jax.nn.silu(x)

def _sigmoid(x):
    return jax.nn.sigmoid(x)

def _layernorm(x, axis=-1, eps=1e-05):
    m = jnp.mean(x, axis=axis, keepdims=True)
    v = jnp.var(x, axis=axis, keepdims=True)
    return (x - m) / jnp.sqrt(v + eps)

def _scatter_add(tgt, idx, src, axis=0):
    return tgt.at[idx].add(src)

def _segment_sum(src, seg, n):
    return jax.ops.segment_sum(src, seg, n)
kernel_name = 'mk_gps_d1_gnn_r8_9ed1d5'

def setup_inputs(seed: int=0):
    np.random.seed(seed)
    _w = jnp.asarray

    def _rec_inputs():
        import jax
        import jax.numpy as jnp
        _gk = jax.random.key(seed)
        x = -7.329e-05 + 0.9999 * jax.random.normal(jax.random.fold_in(_gk, 1), (1250, 1024), jnp.float32)
        src = jax.random.randint(jax.random.fold_in(_gk, 2), (40000,), 0, 1250, jnp.int32)
        dst = jax.random.randint(jax.random.fold_in(_gk, 3), (40000,), 0, 1250, jnp.int32)
        _o = jnp.argsort(dst, stable=True)
        src = src[_o]
        dst = dst[_o]
        return (x, src, dst)
    x, src, dst = _rec_inputs()

    def _L0_gnn_setup():
        import jax, jax.numpy as jnp
        import numpy as np
        N = 6250
        E = 100000
        D_IN = 1024
        D_HID = 512
        D_B = 256
        N_LAYERS = 3
        LN_EPS = 1e-05

        def layernorm(x, g, b):
            m = jnp.mean(x, axis=-1, keepdims=True)
            v = jnp.mean((x - m) ** 2, axis=-1, keepdims=True)
            return (x - m) * jax.lax.rsqrt(v + LN_EPS) * g + b
        key = jax.random.key(seed)
        ks = jax.random.split(key, 16)
        s = 0.02
        inp = {'x': jax.random.normal(ks[0], (N, D_IN), dtype=jnp.float32), 'edge_index': jax.random.randint(ks[1], (2, E), 0, N, dtype=jnp.int32), 'ln_in_g': jnp.ones((D_IN,), jnp.float32), 'ln_in_b': jnp.zeros((D_IN,), jnp.float32), 'W1': jax.random.normal(ks[2], (D_IN, D_HID), jnp.float32) * s, 'b1': jnp.zeros((D_HID,), jnp.float32), 'W2': jax.random.normal(ks[3], (D_HID, D_B), jnp.float32) * s, 'b2': jnp.zeros((D_B,), jnp.float32), 'layer_Wa': jax.random.normal(ks[4], (N_LAYERS, D_B, D_B), jnp.float32) * s, 'layer_ba': jnp.zeros((N_LAYERS, D_B), jnp.float32), 'layer_Wb': jax.random.normal(ks[5], (N_LAYERS, D_B, D_B), jnp.float32) * s, 'layer_bb': jnp.zeros((N_LAYERS, D_B), jnp.float32), 'layer_ng': jnp.ones((N_LAYERS, D_B), jnp.float32), 'layer_nb': jnp.zeros((N_LAYERS, D_B), jnp.float32), 'Wd1': jax.random.normal(ks[6], (D_B, D_HID), jnp.float32) * s, 'bd1': jnp.zeros((D_HID,), jnp.float32), 'Wd2': jax.random.normal(ks[7], (D_HID, D_IN), jnp.float32) * s, 'bd2': jnp.zeros((D_IN,), jnp.float32), 'out_g': jnp.ones((D_IN,), jnp.float32), 'out_b': jnp.zeros((D_IN,), jnp.float32)}
        return inp
    _L0_gnn_all = _L0_gnn_setup()
    _L0_gnn_in = {k: v for k, v in _L0_gnn_all.items() if k in ('ln_in_g', 'ln_in_b', 'W1', 'b1', 'W2', 'b2', 'layer_Wa', 'layer_ba', 'layer_Wb', 'layer_bb', 'layer_ng', 'layer_nb', 'Wd1', 'bd1', 'Wd2', 'bd2', 'out_g', 'out_b')}
    del _L0_gnn_all

    def _L0_mix_setup():
        import jax, jax.numpy as jnp
        import numpy as np
        key = jax.random.key(seed)
        k1, k2, k3 = jax.random.split(key, 3)
        B, S, D = (4, 512, 1024)
        inner = 1024
        x = jax.random.normal(k1, (B, S, D), dtype=jnp.float32)
        w_qkv = jax.random.normal(k2, (D, 3 * inner), dtype=jnp.float32) * (1.0 / np.sqrt(D))
        w_out = jax.random.normal(k3, (inner, D), dtype=jnp.float32) * (1.0 / np.sqrt(inner))
        b_out = jnp.zeros((D,), dtype=jnp.float32)
        return {'x': x, 'w_qkv': w_qkv, 'w_out': w_out, 'b_out': b_out}
    _L0_mix_all = _L0_mix_setup()
    _L0_mix_in = {k: v for k, v in _L0_mix_all.items() if k in ('w_qkv', 'w_out', 'b_out')}
    del _L0_mix_all

    def _L0_ffn_setup():
        import jax, jax.numpy as jnp
        import numpy as np
        TOP_K = 8
        key = jax.random.key(seed)
        k1, k2, k3, k4, k5 = jax.random.split(key, 5)
        B, S, D, F, E = (2, 256, 1024, 768, 64)
        return {'hidden_states': jax.random.normal(k1, (B, S, D), dtype=jnp.float32), 'gate_w': jax.random.normal(k2, (E, D), dtype=jnp.float32) * 0.02, 'w_gate': jax.random.normal(k3, (E, F, D), dtype=jnp.float32) * 0.02, 'w_up': jax.random.normal(k4, (E, F, D), dtype=jnp.float32) * 0.02, 'w_down': jax.random.normal(k5, (E, D, F), dtype=jnp.float32) * 0.02}
    _L0_ffn_all = _L0_ffn_setup()
    _L0_ffn_in = {k: v for k, v in _L0_ffn_all.items() if k in ('gate_w', 'w_gate', 'w_up', 'w_down')}
    del _L0_ffn_all
    return {'x': x, 'src': src, 'dst': dst, 'L0_gnn_ln_in_g': _L0_gnn_in['ln_in_g'], 'L0_gnn_ln_in_b': _L0_gnn_in['ln_in_b'], 'L0_gnn_W1': _L0_gnn_in['W1'], 'L0_gnn_b1': _L0_gnn_in['b1'], 'L0_gnn_W2': _L0_gnn_in['W2'], 'L0_gnn_b2': _L0_gnn_in['b2'], 'L0_gnn_layer_Wa': _L0_gnn_in['layer_Wa'], 'L0_gnn_layer_ba': _L0_gnn_in['layer_ba'], 'L0_gnn_layer_Wb': _L0_gnn_in['layer_Wb'], 'L0_gnn_layer_bb': _L0_gnn_in['layer_bb'], 'L0_gnn_layer_ng': _L0_gnn_in['layer_ng'], 'L0_gnn_layer_nb': _L0_gnn_in['layer_nb'], 'L0_gnn_Wd1': _L0_gnn_in['Wd1'], 'L0_gnn_bd1': _L0_gnn_in['bd1'], 'L0_gnn_Wd2': _L0_gnn_in['Wd2'], 'L0_gnn_bd2': _L0_gnn_in['bd2'], 'L0_gnn_out_g': _L0_gnn_in['out_g'], 'L0_gnn_out_b': _L0_gnn_in['out_b'], 'L0_mix_w_qkv': _L0_mix_in['w_qkv'], 'L0_mix_w_out': _L0_mix_in['w_out'], 'L0_mix_b_out': _L0_mix_in['b_out'], 'L0_ffn_gate_w': _L0_ffn_in['gate_w'], 'L0_ffn_w_gate': _L0_ffn_in['w_gate'], 'L0_ffn_w_up': _L0_ffn_in['w_up'], 'L0_ffn_w_down': _L0_ffn_in['w_down']}

def reference(x, src, dst, L0_gnn_ln_in_g, L0_gnn_ln_in_b, L0_gnn_W1, L0_gnn_b1, L0_gnn_W2, L0_gnn_b2, L0_gnn_layer_Wa, L0_gnn_layer_ba, L0_gnn_layer_Wb, L0_gnn_layer_bb, L0_gnn_layer_ng, L0_gnn_layer_nb, L0_gnn_Wd1, L0_gnn_bd1, L0_gnn_Wd2, L0_gnn_bd2, L0_gnn_out_g, L0_gnn_out_b, L0_mix_w_qkv, L0_mix_w_out, L0_mix_b_out, L0_ffn_gate_w, L0_ffn_w_gate, L0_ffn_w_up, L0_ffn_w_down):
    import jax
    import jax.numpy as jnp

    def _L0_gnn_ref(x, edge_index, ln_in_g, ln_in_b, W1, b1, W2, b2, layer_Wa, layer_ba, layer_Wb, layer_bb, layer_ng, layer_nb, Wd1, bd1, Wd2, bd2, out_g, out_b):
        import jax, jax.numpy as jnp
        import numpy as np
        N = 6250
        E = 100000
        D_IN = 1024
        D_HID = 512
        D_B = 256
        N_LAYERS = 3
        LN_EPS = 1e-05

        def layernorm(x, g, b):
            m = jnp.mean(x, axis=-1, keepdims=True)
            v = jnp.mean((x - m) ** 2, axis=-1, keepdims=True)
            return (x - m) * jax.lax.rsqrt(v + LN_EPS) * g + b
        n = x.shape[0]
        src, dst = (edge_index[0], edge_index[1])
        h = layernorm(x, ln_in_g, ln_in_b)
        h = jax.nn.relu(h @ W1 + b1)
        h = h @ W2 + b2
        for i in range(N_LAYERS):
            agg = jax.ops.segment_sum(h[src], dst, num_segments=n)
            z = h + agg
            z = jax.nn.relu(z @ layer_Wa[i] + layer_ba[i])
            z = z @ layer_Wb[i] + layer_bb[i]
            z = jax.nn.relu(layernorm(z, layer_ng[i], layer_nb[i]))
            h = h + z
        delta = jax.nn.relu(h @ Wd1 + bd1) @ Wd2 + bd2
        return layernorm(x + delta, out_g, out_b)

    def _L0_mix_ref(x, w_qkv, w_out, b_out):
        import jax, jax.numpy as jnp
        import numpy as np
        B, S, D = x.shape
        H, Dh = (16, 64)
        qkv = x @ w_qkv
        q, k, v = jnp.split(qkv, 3, axis=-1)
        reshape = lambda t: t.reshape(B, S, H, Dh).transpose(0, 2, 1, 3)
        q, k, v = (reshape(q), reshape(k), reshape(v))
        q = jax.nn.elu(q) + 1.0
        k = jax.nn.elu(k) + 1.0
        kv = jnp.einsum('bhnd,bhne->bhde', k, v)
        z = jnp.sum(k, axis=-2, keepdims=True)
        numerator = jnp.einsum('bhnd,bhde->bhne', q, kv)
        denominator = jnp.sum(q * z, axis=-1, keepdims=True) + 1e-06
        out = numerator / denominator
        out = out.transpose(0, 2, 1, 3).reshape(B, S, H * Dh)
        return out @ w_out + b_out

    def _L0_ffn_ref(hidden_states, gate_w, w_gate, w_up, w_down):
        import jax, jax.numpy as jnp
        import numpy as np
        TOP_K = 8
        B, S, D = hidden_states.shape
        E = gate_w.shape[0]
        x = hidden_states.reshape(-1, D)
        logits = x.astype(jnp.float32) @ gate_w.astype(jnp.float32).T
        scores = jax.nn.softmax(logits, axis=-1)
        topk_w, topk_ids = jax.lax.top_k(scores, TOP_K)
        topk_w = topk_w / (topk_w.sum(axis=-1, keepdims=True) + 1e-20)
        flat_ids = topk_ids.reshape(-1)
        sort_idx = jnp.argsort(flat_ids)
        sorted_tokens = x[sort_idx // TOP_K]
        group_sizes = jnp.zeros((E,), jnp.int32).at[flat_ids].add(1)
        g = jax.lax.ragged_dot(sorted_tokens, jnp.swapaxes(w_gate, 1, 2), group_sizes)
        u = jax.lax.ragged_dot(sorted_tokens, jnp.swapaxes(w_up, 1, 2), group_sizes)
        h = jax.nn.silu(g) * u
        out = jax.lax.ragged_dot(h, jnp.swapaxes(w_down, 1, 2), group_sizes)
        unsorted = jnp.zeros_like(out).at[sort_idx].set(out)
        y = (unsorted.reshape(B * S, TOP_K, D) * topk_w[..., None]).sum(axis=1)
        return y.reshape(B, S, D)
    edge_index = jnp.stack([src, dst])
    xn = _layernorm(x, axis=-1)
    x = x + _L0_gnn_ref(xn, edge_index, L0_gnn_ln_in_g, L0_gnn_ln_in_b, L0_gnn_W1, L0_gnn_b1, L0_gnn_W2, L0_gnn_b2, L0_gnn_layer_Wa, L0_gnn_layer_ba, L0_gnn_layer_Wb, L0_gnn_layer_bb, L0_gnn_layer_ng, L0_gnn_layer_nb, L0_gnn_Wd1, L0_gnn_bd1, L0_gnn_Wd2, L0_gnn_bd2, L0_gnn_out_g, L0_gnn_out_b) + _L0_mix_ref(xn[None], L0_mix_w_qkv, L0_mix_w_out, L0_mix_b_out)[0]
    x = x + _L0_ffn_ref(_layernorm(x, axis=-1)[None], L0_ffn_gate_w, L0_ffn_w_gate, L0_ffn_w_up, L0_ffn_w_down)[0]
    return x

_drawn_inputs = setup_inputs


def setup_inputs(seed=0):
    import zlib

    import numpy as np

    out = dict(_drawn_inputs(seed))
    spreads = {'L0_gnn_ln_in_g': (1.0, 0.6),
     'L0_gnn_ln_in_b': (0.0, 0.8),
     'L0_gnn_b1': (0.0, 2.0),
     'L0_gnn_b2': (0.0, 1.141),
     'L0_gnn_layer_ba': (0.0, 2.0),
     'L0_gnn_layer_bb': (0.0, 2.0),
     'L0_gnn_layer_ng': (1.0, 0.6),
     'L0_gnn_layer_nb': (0.0, 0.8),
     'L0_gnn_bd1': (0.0, 0.489),
     'L0_gnn_bd2': (0.0, 0.1),
     'L0_gnn_out_g': (1.0, 0.2),
     'L0_gnn_out_b': (0.0, 0.1),
     'L0_mix_b_out': (0.0, 0.1)}
    factors = {'L0_gnn_W1': 5.076, 'L0_mix_w_qkv': 3.939, 'L0_mix_w_out': 4.091}
    for name, (base, spread) in spreads.items():
        noise = np.random.default_rng([zlib.crc32(name.encode()), seed]).standard_normal(out[name].shape)
        drawn = base * np.exp(spread * noise) if base else spread * noise
        out[name] = jnp.asarray(drawn.astype(out[name].dtype))
    for name, factor in factors.items():
        out[name] = (out[name] * factor).astype(out[name].dtype)
    return out
```

```python
from contextlib import ExitStack

import concourse.bass as bass
from concourse import mybir

F32 = mybir.dt.float32
BF16 = mybir.dt.bfloat16
I32 = mybir.dt.int32
I16 = mybir.dt.int16
ALU = mybir.AluOpType
ACT = mybir.ActivationFunctionType
AX = mybir.AxisListType.X
RMAX = bass.bass_isa.ReduceOp.max

P = 128
N, D = 1250, 1024
TP = 125
T = N // TP
DC = D // P
HID, DB = 512, 256
HC, BC = HID // P, DB // P
LAYERS = 3
HEADS, DH = 16, 64
PAIRS = HEADS // 2
E, TOPK, F = 64, 8, 768
FC, FH = F // P, F // 2
EDGES = 40000
CE = 125
CHUNKS = EDGES // CE
EP = 32
PAIRQ = CHUNKS // 2 // EP
NPAIR = CHUNKS // 2
SPANS = ((0, 418), (418, 416), (834, 416))
UNIT = 256
KB = DC * UNIT
MAXB = E + (N * TOPK - E) // P + 1
TAB = 2 * P
BMAX = (N + P - 1) // P
PADROWS = P
EPS = 1e-5

ROWS = {}
_at = 0
for _name, _n in (("b2", DB), ("bb", LAYERS * DB), ("ng", LAYERS * DB), ("nb", LAYERS * DB),
                  ("bd2", D), ("og", D), ("ob", D), ("bo", D)):
    ROWS[_name] = (_at, _n)
    _at += _n
ROWLEN = _at
COLS = {}
_at = 0
for _name, _n in (("g", DC), ("b", DC), ("b1", HC), ("ba", LAYERS * BC), ("bd1", HC)):
    COLS[_name] = (_at, _n)
    _at += _n
COLLEN = _at


class Names:
    pass


def memory(nc, ctx):
    def sb(name, shape, dt=F32):
        return ctx.enter_context(nc.sbuf_tensor(name, shape, dt))

    m = Names()
    m.ps = ctx.enter_context(nc.psum_tensor("ps", [P, 8, 512], F32))
    arena = sb("arena", [P, 2 * 3 * DC * F])
    m.arena = arena
    r0, r1, r2, r3 = 0, 12500, 22500, 30692

    def view(at, *shape):
        n = 1
        for s in shape:
            n *= s
        v = arena[:, at:at + n]
        if len(shape) == 2:
            return v.rearrange("p (a b) -> p a b", a=shape[0])
        if len(shape) == 3:
            return v.rearrange("p (a b c) -> p a b c", a=shape[0], b=shape[1])
        return v

    m.view = view
    m.xnT = view(r0, DC, N)
    m.adjT = view(r0, T, N)
    m.wout = view(r0, DC, D)
    m.wd2 = view(r0 + DC * D, HC, D)
    m.h0T = view(r1, DC, N)
    m.qT = view(r1, DC, N)
    m.w1 = view(r2, DC, HID)
    m.w2 = view(r2 + DC * HID, HC, DB)
    m.unit = [view(r2 + s * KB, DC, UNIT) for s in range(4)]
    m.wab = view(r2, 2 * LAYERS * BC, DB)
    m.zz = view(r2 + 4096, T, DB)
    m.hT = view(r2, BC, N)
    m.wd1 = view(r2 + 2500, BC, HID)
    m.tile = [view(r2 + 2500 + 1024 + i * D, D) for i in range(4)]
    m.row = [view(r3 + i * D, D) for i in range(6)]
    m.h1T = view(r3, HC, N)
    m.kvm = view(r3, PAIRS, P)
    m.zm = view(r3 + 1024, PAIRS, P)
    m.kt = [view(r3 + 2048 + i * UNIT, UNIT) for i in range(2)]
    m.vt = [view(r3 + 2560 + i * UNIT, UNIT) for i in range(2)]
    m.tmp = [view(r3 + 3072 + i * 418, 418) for i in range(3)]
    m.zT = view(r3, BC, N)
    m.aT = view(r3 + 2500, BC, N)
    m.dT = view(r3, HC, N)
    m.edge = [view(r3 + i * CHUNKS, CHUNKS) for i in range(4)]
    m.dstrow = view(r3 + 4 * CHUNKS, PAIRQ, 2 * CE)
    m.dstrowf = view(r3 + 4 * CHUNKS + 1250, PAIRQ, 2 * CE)
    m.hot = [view(r3 + 4000 + i * 700, 625) for i in range(2)]
    m.hotd = [view(r3 + 5400 + i * 64, 63) for i in range(2)]
    q = DC * F
    m.wgate = [view(s * 3 * q, DC, F) for s in range(2)]
    m.wup = [view(s * 3 * q + q, DC, F) for s in range(2)]
    m.wdown = [view(s * 3 * q + 2 * q, FC, D) for s in range(2)]

    work = sb("work", [P, ROWLEN])
    m.rows = work
    m.h = sb("h", [P, T, DB])
    m.xg = work[:, 0:1024]
    m.xT = work[:, 1024:2048].rearrange("p (c n) -> p c n", c=DC)
    m.hx = work[:, 2048:2816]
    m.hxT = work[:, 2816:3584].rearrange("p (c n) -> p c n", c=FC)
    m.ex = work[:, 3584:4352]
    m.yo = work[:, 4352:5376]
    m.oh = work[:, 5376:6016].bitcast(BF16).rearrange("p (t s) -> p t s", t=T)
    m.cols = sb("cols", [P, COLLEN])
    m.ident = sb("ident", [P, P])
    m.before = sb("before", [P, TP], BF16)
    m.ones = sb("ones", [P, P], BF16)
    m.onesf = sb("onesf", [P, P])
    m.zeros = sb("zeros", [P, 512], BF16)
    m.iota = sb("iota", [P, BMAX * P])
    m.iota16 = sb("iota16", [P, N], I16)
    m.pos = sb("pos", [P, 4])
    m.stats = sb("stats", [P, 12])
    m.mv = sb("mv", [P, 3, T, 2])
    m.ve = sb("ve", [P, T])
    m.rs = sb("rs", [P, T])
    m.mr = sb("mr", [P, T, 2])
    m.nt = sb("nt", [P, T])
    m.gatew = sb("gatew", [P, DC, E])
    m.logit = sb("logit", [P, T, E])
    m.score = view(0, T, E)
    m.rep = view(T * E, T, E)
    m.top = sb("top", [P, T, TOPK])
    m.sc = sb("sc", [P, 4, T])
    m.mask = sb("mask", [P, T, E], BF16)
    m.mprev = sb("mprev", [P, T + 1, E], BF16)
    hs = m.h[:, :, :].rearrange("p t f -> p (t f)")
    m.place = hs[:, 0:T * E].rearrange("p (t e) -> p t e", t=T)
    m.sel = hs[:, T * E:4 * T * E].bitcast(BF16).rearrange("p (t e k) -> p t e k", t=T, e=E)
    m.cnt = sb("cnt", [P, 8, E])
    m.tabp = sb("tabp", [P, 2, 2], I32)
    m.tab = sb("tab", [1, TAB * 2], I32)
    m.nbi = sb("nbi", [P, 2, E], I32)
    m.tot = sb("tot", [P, 1], I32)
    m.rng = sb("rng", [P, 8, 2 * T])
    m.rngh = sb("rngh", [P, T, 2, PAIRQ])
    m.rngi = sb("rngi", [P, 3, T], I32)
    m.sw = sb("sw", [P, T, 6], BF16)
    m.selc = sb("selc", [P, 6])
    m.wpart = sb("wpart", [P, 1])
    m.meta = sb("meta", [P, 3, 3])
    m.metai = m.meta[:, :, :].bitcast(I32)
    m.idx = sb("idx", [P, 2], I32)
    return m


def build(nc, x, srcT, dstT, dst, cols, rows, w1, w2, wa, wb, wd1, wd2, wqkv, wout, gatew,
          wg, wu, wd, out):
    ctx = ExitStack()
    with ctx:
        m = memory(nc, ctx)
        xn2 = nc.dram_tensor("xn2", [N + PADROWS, D], F32, kind="Internal").ap()
        acc = nc.dram_tensor("acc", [N + PADROWS, D], F32, kind="Internal").ap()
        tabd = nc.dram_tensor("tabd", [TAB, 2], I32, kind="Internal").ap()
        w = Names()
        w.w1_in, w.w2_in, w.rows_in, w.cols_in, w.gatew_in, w.made = (
            ctx.enter_context(nc.semaphore(n)) for n in ("w1_in", "w2_in", "rows_in", "cols_in", "gatew_in", "made"))
        normalise(nc, m, w, x, cols, rows, w1, w2, gatew)
        encode(nc, m, w)
        attention(nc, m, wqkv)
        adjacency(nc, m, srcT, dstT, dst)
        messages(nc, m, wa, wb)
        combine(nc, m, w, x, wd1, wd2, wout, xn2, acc)
        route(nc, m, tabd)
        experts(nc, m, wg, wu, wd, xn2, acc, out)


def row(m, name, i=0, n=None):
    at, size = ROWS[name]
    n = n or size
    return m.rows[0:TP, at + i * n:at + (i + 1) * n]


def col(m, name, i):
    return m.cols[:, COLS[name][0] + i:COLS[name][0] + i + 1]


def inverse_root(dve, act_ready, act_done, n, var, ve, y, t):
    nc_v = dve
    nc_v.tensor_scalar(ve, var, EPS, None, ALU.add).then_inc(act_ready, 1)
    dve.wait_ge(act_done, n)
    nc_v.reciprocal(y, y)
    dve.drain()
    nc_v.tensor_tensor(t, y, y, ALU.mult)
    dve.drain()
    nc_v.tensor_tensor(t, t, ve, ALU.mult)
    dve.drain()
    nc_v.tensor_scalar(t, t, -0.5, 1.5, ALU.mult, ALU.add)
    dve.drain()
    nc_v.tensor_tensor(y, y, t, ALU.mult)
    dve.drain()


def normalise(nc, m, w, x, cols, rows, w1, w2, gatew):
    with ExitStack() as ctx:
        def sem(name):
            return ctx.enter_context(nc.semaphore(name))
        x_in = [sem("x_in0"), sem("x_in1")]
        var_ready, root_done, xn_ready, xh_ready = sem("var_ready"), sem("root_done"), sem("xn_ready"), sem("xh_ready")
        xn_turned, xh_turned, xn_kept, xh_kept = sem("xn_turned"), sem("xh_turned"), sem("xn_kept"), sem("xh_kept")
        xin, xn, xh = m.row[0:2], m.row[2:4], m.row[4:6]
        block = ctx.enter_context(nc.Block())

        @block.sync
        def _(sp):
            sp.dma_start(m.cols[:], cols).then_inc(w.cols_in, 16)
            sp.dma_start(m.w1, w1.rearrange("(c p) n -> p c n", p=P)).then_inc(w.w1_in, 16)
            sp.dma_start(m.w2, w2.rearrange("(c p) n -> p c n", p=P)).then_inc(w.w2_in, 16)
            sp.dma_start(m.rows[0:TP, :], rows.to_broadcast([TP, ROWLEN])).then_inc(w.rows_in, 16)
            sp.dma_start(m.gatew[:], gatew.rearrange("p (c e) -> p c e", c=DC)).then_inc(w.gatew_in, 16)

        @block.gpsimd
        def _(pool):
            for t in range(2):
                pool.dma_start(xin[t][0:TP, :], x[t * TP:(t + 1) * TP, :]).then_inc(x_in[t], 16)
            nc.gpsimd.memset(m.ident[:], 0.0)
            nc.gpsimd.memset(m.before[:], 1.0)
            nc.gpsimd.memset(m.ones[:], 1.0)
            nc.gpsimd.memset(m.onesf[:], 1.0)
            nc.gpsimd.memset(m.zeros[:], 0.0)
            pool.drain()
            nc.gpsimd.affine_select(out=m.ident[:], in_=m.ident[:], compare_op=ALU.not_equal, fill=1.0,
                                    base=0, pattern=[[-1, P]], channel_multiplier=1)
            nc.gpsimd.affine_select(out=m.before[:], in_=m.before[:], compare_op=ALU.is_gt, fill=0.0,
                                    base=0, pattern=[[1, TP]], channel_multiplier=-1)
            nc.gpsimd.iota(m.iota[:], pattern=[[1, BMAX * P]], base=0, channel_multiplier=0,
                           allow_small_or_imprecise_dtypes=True)
            nc.gpsimd.iota(m.iota16[:], pattern=[[1, N]], base=0, channel_multiplier=0,
                           allow_small_or_imprecise_dtypes=True)
            nc.gpsimd.iota(m.pos[:, 0:1], pattern=[[1, 1]], base=0, channel_multiplier=1,
                           allow_small_or_imprecise_dtypes=True)
            nc.gpsimd.iota(m.pos[:, 1:2], pattern=[[1, 1]], base=P, channel_multiplier=1,
                           allow_small_or_imprecise_dtypes=True)
            nc.gpsimd.iota(m.pos[:, 2:3], pattern=[[1, 1]], base=N, channel_multiplier=1,
                           allow_small_or_imprecise_dtypes=True)
            nc.gpsimd.iota(m.pos[:, 3:4], pattern=[[1, 1]], base=-N, channel_multiplier=-1,
                           allow_small_or_imprecise_dtypes=True).then_inc(w.made, 1)
            for t in range(2, T):
                pool.wait_ge(xn_ready, t - 1)
                pool.dma_start(xin[t % 2][0:TP, :], x[t * TP:(t + 1) * TP, :]).then_inc(x_in[t % 2], 16)

        @block.vector
        def _(dve):
            for t in range(T):
                s = t % 2
                dve.wait_ge(x_in[s], 16 * (t // 2 + 1))
                src = xin[s]
                for which, dest, ready in ((0, xn[s], xn_ready), (1, xh[s], xh_ready)):
                    for i in range(2):
                        nc.vector.bn_stats(m.stats[0:TP, 6 * i:6 * i + 6], src[0:TP, 512 * i:512 * i + 512])
                    dve.drain()
                    nc.vector.bn_aggr(m.mv[0:TP, which, t, :], m.stats[0:TP, :])
                    dve.drain()
                    inverse_root(nc.vector, var_ready, root_done, 2 * t + which + 1, m.mv[0:TP, which, t, 1:2],
                                 m.ve[0:TP, t:t + 1], m.rs[0:TP, t:t + 1], m.nt[0:TP, t:t + 1])
                    if which == 0:
                        nc.vector.tensor_copy(m.mr[0:TP, t, 0:1], m.mv[0:TP, 0, t, 0:1])
                        nc.vector.tensor_copy(m.mr[0:TP, t, 1:2], m.rs[0:TP, t:t + 1])
                    if t >= 2:
                        dve.wait_ge(xn_turned if which == 0 else xh_turned, t - 1)
                    nc.vector.tensor_scalar(dest[0:TP, :], src[0:TP, :], m.mv[0:TP, which, t, 0:1],
                                            m.rs[0:TP, t:t + 1], ALU.subtract, ALU.mult).then_inc(ready, 1)
                    dve.drain()
                    src = dest

        @block.tensor
        def _(pe):
            pe.wait_ge(w.made, 1)
            for t in range(T):
                for src, ready, kept, turned, b0 in ((xn[t % 2], xn_ready, xn_kept, xn_turned, 0),
                                                     (xh[t % 2], xh_ready, xh_kept, xh_turned, 2)):
                    pe.wait_ge(ready, t + 1)
                    if t:
                        pe.wait_ge(kept, t)
                    for c in range(DC):
                        mm = nc.tensor.transpose(m.ps[:, b0 + c // 4, (c % 4) * TP:(c % 4 + 1) * TP],
                                                 src[0:TP, c * P:(c + 1) * P], m.ident[0:TP, 0:TP])
                    mm.then_inc(turned, 1)

        @block.scalar
        def _(act):
            act.wait_ge(w.cols_in, 16)
            for t in range(T):
                act.wait_ge(var_ready, 2 * t + 1)
                nc.scalar.activation(m.rs[0:TP, t:t + 1], m.ve[0:TP, t:t + 1], ACT.Sqrt).then_inc(root_done, 1)
                act.wait_ge(var_ready, 2 * t + 2)
                nc.scalar.activation(m.rs[0:TP, t:t + 1], m.ve[0:TP, t:t + 1], ACT.Sqrt).then_inc(root_done, 1)
                act.wait_ge(xn_turned, t + 1)
                for i in range(2):
                    a = nc.scalar.activation(m.xnT[:, 4 * i:4 * i + 4, t * TP:(t + 1) * TP],
                                             m.ps[:, i, 0:4 * TP].rearrange("p (c n) -> p c n", c=4), ACT.Copy)
                a.then_inc(xn_kept, 1)
                act.wait_ge(xh_turned, t + 1)
                for c in range(DC):
                    a = nc.scalar.activation(m.h0T[:, c, t * TP:(t + 1) * TP],
                                             m.ps[:, 2 + c // 4, (c % 4) * TP:(c % 4 + 1) * TP],
                                             ACT.Identity, bias=col(m, "b", c), scale=col(m, "g", c))
                a.then_inc(xh_kept, 1)


def encode(nc, m, w):
    with ExitStack() as ctx:
        def sem(name):
            return ctx.enter_context(nc.semaphore(name))
        h1_done, h1_kept, h_done, h_kept = sem("h1_done"), sem("h1_kept"), sem("h_done"), sem("h_kept")
        groups = [(hb, s) for hb in range(HC) for s in range(len(SPANS))]
        block = ctx.enter_context(nc.Block())

        @block.tensor
        def _(pe):
            pe.wait_ge(w.w1_in, 16)
            for g, (hb, s) in enumerate(groups):
                at, n = SPANS[s]
                if g >= 4:
                    pe.wait_ge(h1_kept, g - 3)
                for c in range(DC):
                    mm = nc.tensor.matmul(m.ps[:, g % 4, 0:n], m.w1[:, c, hb * P:(hb + 1) * P],
                                          m.h0T[:, c, at:at + n], start=(c == 0), stop=(c == DC - 1))
                mm.then_inc(h1_done, 1)
            pe.wait_ge(w.w2_in, 16)
            pe.wait_ge(h1_kept, len(groups))
            for t in range(T):
                if t >= 4:
                    pe.wait_ge(h_kept, t - 3)
                for c in range(HC):
                    mm = nc.tensor.matmul(m.ps[0:TP, 4 + t % 4, 0:DB], m.h1T[:, c, t * TP:(t + 1) * TP],
                                          m.w2[:, c, :], start=(c == 0), stop=(c == HC - 1))
                mm.then_inc(h_done, 1)

        @block.scalar
        def _(act):
            for g, (hb, s) in enumerate(groups):
                at, n = SPANS[s]
                act.wait_ge(h1_done, g + 1)
                nc.scalar.activation(m.h1T[:, hb, at:at + n], m.ps[:, g % 4, 0:n], ACT.Relu,
                                     bias=col(m, "b1", hb)).then_inc(h1_kept, 1)

        @block.vector
        def _(dve):
            dve.wait_ge(w.rows_in, 16)
            for t in range(T):
                dve.wait_ge(h_done, t + 1)
                nc.vector.tensor_tensor(m.h[0:TP, t, :], m.ps[0:TP, 4 + t % 4, 0:DB], row(m, "b2"),
                                        ALU.add).then_inc(h_kept, 1)


def attention(nc, m, wqkv):
    QU = D // UNIT
    order = list(range(QU)) + [v for i in range(QU) for v in (QU + i, 2 * QU + i)]
    NS = len(SPANS)
    q_groups = [(u, cb, s) for u in range(QU) for cb in range(UNIT // P) for s in range(NS)]
    G = len(q_groups)
    BANKS = 6
    steps = [(i, t) for i in range(QU) for t in range(T)]

    with ExitStack() as ctx:
        def sem(name):
            return ctx.enter_context(nc.semaphore(name))
        unit_in = [sem(f"unit_in{s}") for s in range(4)]
        unit_used, proj_done, cut, exped = sem("unit_used"), sem("proj_done"), sem("cut"), sem("exped")
        q_kept, k_kept, v_kept = sem("q_kept"), sem("k_kept"), sem("v_kept")
        kv_step, kv_kept, cleared = sem("kv_step"), sem("kv_kept"), sem("cleared")
        nd_done, nd_kept = sem("nd_done"), sem("nd_kept")
        block = ctx.enter_context(nc.Block())

        @block.sync
        def _(sp):
            for n, u in enumerate(order):
                if n >= 4:
                    sp.wait_ge(unit_used, n - 3 if n - 4 < QU else (n - 4 - QU) // 2 * 2 + 2 + QU)
                sp.dma_start(m.unit[n % 4], wqkv[:, u * UNIT:(u + 1) * UNIT].rearrange("(c p) n -> p c n", p=P)
                             ).then_inc(unit_in[n % 4], 16)

        @block.tensor
        def _(pe):
            for g, (u, cb, s) in enumerate(q_groups):
                at, n = SPANS[s]
                pe.wait_ge(unit_in[u % 4], 16)
                if g >= BANKS:
                    pe.wait_ge(q_kept, g - BANKS + 1)
                for c in range(DC):
                    mm = nc.tensor.matmul(m.ps[:, g % BANKS, 0:n], m.unit[u % 4][:, c, cb * P:(cb + 1) * P],
                                          m.xnT[:, c, at:at + n], start=(c == 0), stop=(c == DC - 1))
                mm.then_inc(proj_done, 1)
                if cb == UNIT // P - 1 and s == NS - 1:
                    pe.drain().then_inc(unit_used, 1)

            def accumulate(n):
                i, t = steps[n]
                pe.wait_ge(k_kept, n + 1)
                pe.wait_ge(v_kept, n + 1)
                if t == 0 and i >= 2:
                    pe.wait_ge(kv_kept, i - 1)
                bank = 6 + i % 2
                for pr in range(2):
                    nc.tensor.matmul(m.ps[:, bank, pr * P:(pr + 1) * P], m.kt[n % 2][0:TP, pr * P:(pr + 1) * P],
                                     m.vt[n % 2][0:TP, pr * P:(pr + 1) * P],
                                     start=(t == 0 and pr == 0), stop=(t == T - 1), skip_group_check=True)
                    mm = nc.tensor.matmul(m.ps[:, bank, 2 * P + pr:2 * P + pr + 1],
                                          m.kt[n % 2][0:TP, pr * P:(pr + 1) * P], m.onesf[0:TP, 0:1],
                                          start=False, stop=(t == T - 1), skip_group_check=True)
                mm.then_inc(kv_step, 1)

            for n, (i, t) in enumerate(steps):
                slots = [(QU + 2 * i) % 4, (QU + 2 * i + 1) % 4]
                for j in range(2):
                    g = G + 2 * n + j
                    if t == 0:
                        pe.wait_ge(unit_in[slots[j]], 16 * ((QU + 2 * i + j) // 4 + 1))
                    if g - BANKS < G:
                        pe.wait_ge(q_kept, g - BANKS + 1)
                    else:
                        pe.wait_ge((k_kept, v_kept)[j], (g - BANKS - G) // 2 + 1)
                    for c in range(DC):
                        mm = nc.tensor.matmul(m.ps[0:TP, g % BANKS, 0:UNIT], m.xnT[:, c, t * TP:(t + 1) * TP],
                                              m.unit[slots[j]][:, c, :], start=(c == 0), stop=(c == DC - 1))
                    mm.then_inc(proj_done, 1)
                if t == T - 1:
                    pe.drain().then_inc(unit_used, 2)
                if n:
                    accumulate(n - 1)
            accumulate(len(steps) - 1)
            pe.wait_ge(kv_kept, QU)
            pe.wait_ge(q_kept, G)
            pe.wait_ge(v_kept, len(steps))
            for g in range(PAIRS * NS):
                pr, s = divmod(g, NS)
                at, n = SPANS[s]
                if g >= 3:
                    pe.wait_ge(nd_kept, g - 2)
                b = 2 * (g % 3)
                nc.tensor.matmul(m.ps[:, b, 0:n], m.kvm[:, pr, :], m.qT[:, pr, at:at + n], start=True, stop=True)
                nc.tensor.matmul(m.ps[:, b + 1, 0:n], m.zm[:, pr, :], m.qT[:, pr, at:at + n],
                                 start=True, stop=True).then_inc(nd_done, 1)

        @block.scalar
        def _(act):
            for g, (u, cb, s) in enumerate(q_groups):
                n = SPANS[s][1]
                act.wait_ge(cut, g + 1)
                nc.scalar.activation(m.tmp[g % 2][:, 0:n], m.tmp[g % 2][:, 0:n], ACT.Exp).then_inc(exped, 1)
            for n, (i, t) in enumerate(steps):
                act.wait_ge(cut, G + n + 1)
                nc.scalar.activation(m.tmp[n % 2][0:TP, 0:UNIT], m.tmp[n % 2][0:TP, 0:UNIT],
                                     ACT.Exp).then_inc(exped, 1)
                act.wait_ge(proj_done, G + 2 * n + 2)
                if n >= 2:
                    act.wait_ge(kv_step, n - 1)
                nc.scalar.activation(m.vt[n % 2][0:TP, :], m.ps[0:TP, (G + 2 * n + 1) % BANKS, 0:UNIT],
                                     ACT.Copy).then_inc(v_kept, 1)

        @block.vector
        def _(dve):
            nc.vector.memset(m.kvm, 0.0)
            nc.vector.memset(m.zm, 0.0)
            dve.drain()

            def finish_q(g):
                u, cb, s = q_groups[g]
                at, n = SPANS[s]
                dve.wait_ge(exped, g + 1)
                nc.vector.scalar_tensor_tensor(m.qT[:, 2 * u + cb, at:at + n], m.ps[:, g % BANKS, 0:n], 0.0,
                                               m.tmp[g % 2][:, 0:n], ALU.max, ALU.add).then_inc(q_kept, 1)

            for g, (u, cb, s) in enumerate(q_groups):
                n = SPANS[s][1]
                dve.wait_ge(proj_done, g + 1)
                if g >= 2:
                    dve.drain()
                nc.vector.tensor_scalar(m.tmp[g % 2][:, 0:n], m.ps[:, g % BANKS, 0:n], 0.0, None,
                                        ALU.min).then_inc(cut, 1)
                if g:
                    finish_q(g - 1)
            finish_q(G - 1)
            dve.drain()

            def finish_k(n):
                dve.wait_ge(exped, G + n + 1)
                if n >= 2:
                    dve.wait_ge(kv_step, n - 1)
                nc.vector.scalar_tensor_tensor(m.kt[n % 2][0:TP, :], m.ps[0:TP, (G + 2 * n) % BANKS, 0:UNIT], 0.0,
                                               m.tmp[n % 2][0:TP, 0:UNIT], ALU.max, ALU.add).then_inc(k_kept, 1)
                i, t = steps[n]
                if t == T - 1:
                    dve.wait_ge(kv_step, n + 1)
                    bank = 6 + i % 2
                    for pr in range(2):
                        for hd in range(2):
                            a, b = hd * DH, (hd + 1) * DH
                            nc.vector.tensor_copy(m.kvm[a:b, 2 * i + pr, a:b],
                                                  m.ps[a:b, bank, pr * P + a:pr * P + b])
                            v = nc.vector.tensor_scalar(m.zm[a:b, 2 * i + pr, a:b], m.onesf[a:b, 0:DH],
                                                        m.ps[a:b, bank, 2 * P + pr:2 * P + pr + 1], None, ALU.mult)
                    v.then_inc(kv_kept, 1)

            for n, (i, t) in enumerate(steps):
                dve.wait_ge(proj_done, G + 2 * n + 1)
                dve.drain()
                nc.vector.tensor_scalar(m.tmp[n % 2][0:TP, 0:UNIT], m.ps[0:TP, (G + 2 * n) % BANKS, 0:UNIT],
                                        0.0, None, ALU.min).then_inc(cut, 1)
                if n:
                    finish_k(n - 1)
            finish_k(len(steps) - 1)
            for g in range(PAIRS * NS):
                pr, s = divmod(g, NS)
                at, n = SPANS[s]
                b = 2 * (g % 3)
                tmp = m.tmp[g % 2][:, 0:n]
                dve.wait_ge(nd_done, g + 1)
                dve.drain()
                nc.vector.tensor_scalar(tmp, m.ps[:, b + 1, 0:n], 1e-6, None, ALU.add)
                dve.drain()
                nc.vector.reciprocal(tmp, tmp)
                dve.drain()
                nc.vector.tensor_tensor(m.qT[:, pr, at:at + n], m.ps[:, b, 0:n], tmp, ALU.mult).then_inc(nd_kept, 1)


def adjacency(nc, m, srcT, dstT, dst):
    with ExitStack() as ctx:
        def sem(name):
            return ctx.enter_context(nc.semaphore(name))
        e_in, row_in, found, ranged = sem("e_in"), sem("row_in"), sem("found"), sem("ranged")
        bounds, hot_ready, hot_free = sem("bounds"), sem("hot_ready"), sem("hot_free")
        tile_done, tile_kept, zeroed = sem("tile_done"), sem("tile_kept"), sem("zeroed")
        esrc, edst, srcf, dstf = m.edge
        hots = [v[:, :].bitcast(BF16)[0:TP, 0:N] for v in m.hot]
        hotd = [v[:, :].bitcast(BF16)[0:TP, 0:TP] for v in m.hotd]
        banks = ((0, 4), (4, 4), (8, 2))
        block = ctx.enter_context(nc.Block())

        @block.sync
        def _(sp):
            sp.dma_start(m.dstrow[0:EP, :, :].bitcast(I32),
                         dst.rearrange("(p q e) -> p q e", p=EP, q=PAIRQ)).then_inc(row_in, 16)
            sp.dma_start(esrc[0:CE, :].bitcast(I32), srcT).then_inc(e_in, 16)
            sp.dma_start(edst[0:CE, :].bitcast(I32), dstT).then_inc(e_in, 16)

        @block.gpsimd
        def _(pool):
            nc.gpsimd.iota(m.rng[0:EP, 6, 0:PAIRQ], pattern=[[1, PAIRQ]], base=1, channel_multiplier=PAIRQ,
                           allow_small_or_imprecise_dtypes=True)
            nc.gpsimd.iota(m.rng[0:EP, 7, 0:PAIRQ], pattern=[[-1, PAIRQ]], base=NPAIR, channel_multiplier=-PAIRQ,
                           allow_small_or_imprecise_dtypes=True).then_inc(found, 1)
            pool.wait_ge(found, 2)
            nc.gpsimd.partition_all_reduce(m.rng[0:EP, 3, :], m.rng[0:EP, 2, :], EP, RMAX).then_inc(ranged, 1)

        @block.vector
        def _(dve):
            dve.wait_ge(row_in, 16)
            nc.vector.tensor_copy(m.dstrowf[0:EP, :, :], m.dstrow[0:EP, :, :].bitcast(I32))
            dve.drain()
            lo, hi = m.rng[0:EP, 0, 0:PAIRQ], m.rng[0:EP, 1, 0:PAIRQ]
            nc.vector.tensor_reduce(lo, m.dstrowf[0:EP, :, :], AX, ALU.min)
            nc.vector.tensor_reduce(hi, m.dstrowf[0:EP, :, :], AX, ALU.max)
            dve.drain()
            for t in range(T):
                nc.vector.tensor_scalar(m.rngh[0:EP, t, 0, :], hi, float(t * TP), None, ALU.is_ge)
            dve.drain()
            for t in range(T):
                nc.vector.scalar_tensor_tensor(m.rngh[0:EP, t, 1, :], lo, float(t * TP + TP - 1),
                                               m.rngh[0:EP, t, 0, :], ALU.is_le, ALU.mult)
            dve.drain()
            dve.wait_ge(found, 1)
            for t in range(T):
                nc.vector.tensor_tensor(m.rngh[0:EP, t, 0, :], m.rngh[0:EP, t, 1, :], m.rng[0:EP, 6, 0:PAIRQ],
                                        ALU.mult)
            dve.drain()
            nc.vector.tensor_reduce(m.rng[0:EP, 2, 0:T], m.rngh[0:EP, :, 0, :], AX, ALU.max)
            for t in range(T):
                nc.vector.tensor_tensor(m.rngh[0:EP, t, 1, :], m.rngh[0:EP, t, 1, :], m.rng[0:EP, 7, 0:PAIRQ],
                                        ALU.mult)
            dve.drain()
            nc.vector.tensor_reduce(m.rng[0:EP, 2, T:2 * T], m.rngh[0:EP, :, 1, :], AX,
                                    ALU.max).then_inc(found, 1)
            dve.wait_ge(ranged, 1)
            end, low = m.rng[0:EP, 3, 0:T], m.rng[0:EP, 3, T:2 * T]
            first, last, count = m.rng[0:EP, 4, 0:T], m.rng[0:EP, 4, T:2 * T], m.rng[0:EP, 5, 0:T]
            nc.vector.tensor_scalar(first, low, -1.0, float(NPAIR), ALU.mult, ALU.add)
            dve.drain()
            nc.vector.tensor_scalar(first, first, float(NPAIR - 1), None, ALU.min)
            dve.drain()
            nc.vector.tensor_tensor(count, end, first, ALU.subtract)
            dve.drain()
            nc.vector.tensor_scalar(count, count, 1.0, None, ALU.max)
            nc.vector.tensor_copy(m.rngi[0:EP, 0, :], first)
            dve.drain()
            nc.vector.tensor_copy(m.rngi[0:EP, 1, :], count)
            nc.vector.tensor_tensor_scan(last, m.onesf[0:EP, 0:T], count, 0.0, ALU.mult, ALU.add)
            dve.drain()
            nc.vector.tensor_tensor(last, last, count, ALU.subtract)
            dve.drain()
            nc.vector.tensor_copy(m.rngi[0:EP, 2, :], last).then_inc(bounds, 1)
            dve.drain()
            dve.wait_ge(e_in, 32)
            nc.vector.tensor_copy(srcf[0:CE, :], esrc[0:CE, :].bitcast(I32))
            nc.vector.tensor_copy(dstf[0:CE, :], edst[0:CE, :].bitcast(I32))
            dve.drain()
            with dve.Fori(0, T) as t:
                first_pair = dve.value_load(m.rngi[0:1, 0, bass.ds(t, 1)], min_val=0, max_val=NPAIR - 1)
                pairs = dve.value_load(m.rngi[0:1, 1, bass.ds(t, 1)], min_val=1, max_val=NPAIR)
                before = dve.value_load(m.rngi[0:1, 2, bass.ds(t, 1)], min_val=0, max_val=(T - 1) * NPAIR)
                with dve.Fori(0, pairs) as j:
                    pair = dve.snap(nc.s_assert_within(
                        first_pair + j, 0, NPAIR - 1,
                        skip_runtime_bounds_check_because="the count ends at the last pair"))
                    done = dve.snap(before + j)
                    for s in range(2):
                        c = pair * 2 + s
                        dve.wait_ge(hot_free, done * 2 + s + 1)
                        nc.vector.tensor_scalar(hots[s], m.iota16[0:CE, 0:N], srcf[0:CE, bass.ds(c, 1)], None,
                                                ALU.is_equal)
                        nc.vector.tensor_scalar(hotd[s], m.iota16[0:CE, bass.ds(t * TP, TP)],
                                                dstf[0:CE, bass.ds(c, 1)], None, ALU.is_equal).then_inc(hot_ready, 1)

        @block.tensor
        def _(pe):
            pe.wait_ge(bounds, 1)
            pe.drain().then_inc(hot_free, 2)
            pe.drain().then_inc(tile_kept, 2)
            with pe.Fori(0, T // 2) as t2:
                for odd in range(2):
                    t = t2 * 2 + odd
                    pairs = pe.value_load(m.rngi[0:1, 1, bass.ds(t, 1)], min_val=1, max_val=NPAIR)
                    before = pe.value_load(m.rngi[0:1, 2, bass.ds(t, 1)], min_val=0, max_val=(T - 1) * NPAIR)
                    pe.wait_ge(tile_kept, t2 * 2 + odd + 1)
                    for b, (s0, n) in enumerate(banks):
                        nc.tensor.matmul(m.ps[0:TP, 3 * odd + b, 0:n * TP], m.zeros[0:CE, 0:TP],
                                         m.zeros[0:CE, 0:n * TP], start=True, stop=False, skip_group_check=True)
                    with pe.Fori(0, pairs) as j:
                        done = pe.snap(before + j)
                        for s in range(2):
                            pe.wait_ge(hot_ready, done * 2 + s + 1)
                            for b, (s0, n) in enumerate(banks):
                                for i in range(n):
                                    mm = nc.tensor.matmul(m.ps[0:TP, 3 * odd + b, i * TP:(i + 1) * TP],
                                                          hots[s][:, (s0 + i) * TP:(s0 + i + 1) * TP], hotd[s],
                                                          start=False, stop=False, skip_group_check=True)
                            mm.then_inc(hot_free, 1)
                    for b, (s0, n) in enumerate(banks):
                        mm = nc.tensor.matmul(m.ps[0:TP, 3 * odd + b, 0:n * TP], m.zeros[0:CE, 0:TP],
                                              m.zeros[0:CE, 0:n * TP], start=False, stop=True,
                                              skip_group_check=True)
                    mm.then_inc(tile_done, 1)

        @block.scalar
        def _(act):
            with act.Fori(0, T // 2) as t2:
                for odd in range(2):
                    act.wait_ge(tile_done, t2 * 2 + odd + 1)
                    for b, (s0, n) in enumerate(banks):
                        a = nc.scalar.activation(m.adjT[0:TP, s0:s0 + n, bass.ds((t2 * 2 + odd) * TP, TP)],
                                                 m.ps[0:TP, 3 * odd + b, 0:n * TP].rearrange("p (s d) -> p s d", s=n),
                                                 ACT.Copy)
                    a.then_inc(tile_kept, 1)

    with ExitStack() as ctx:
        block = ctx.enter_context(nc.Block())

        @block.vector
        def _(dve):
            for s in range(T):
                d = m.adjT[0:TP, s, s * TP:(s + 1) * TP]
                nc.vector.tensor_tensor(d, d, m.ident[0:TP, 0:TP], ALU.add)


def messages(nc, m, wa, wb):
    NS = len(SPANS)
    with ExitStack() as ctx:
        def sem(name):
            return ctx.enter_context(nc.semaphore(name))
        w_in, mm_done, kept, zz_done, zz_kept = sem("w_in"), sem("mm_done"), sem("kept"), sem("zz_done"), sem("zz_kept")
        var_ready, root_done, h_ready = sem("mvar_ready"), sem("mroot_done"), sem("h_ready")
        groups = [(f, s) for f in range(BC) for s in range(NS)]
        G = len(groups)
        block = ctx.enter_context(nc.Block())

        @block.sync
        def _(sp):
            sp.dma_start(m.wab[:, 0:LAYERS * BC, :], wa.rearrange("l (c p) n -> p (l c) n", p=P)).then_inc(w_in, 16)
            sp.dma_start(m.wab[:, LAYERS * BC:, :], wb.rearrange("l (c p) n -> p (l c) n", p=P)).then_inc(w_in, 16)

        @block.tensor
        def _(pe):
            pe.wait_ge(w_in, 32)
            for i in range(LAYERS):
                if i:
                    pe.wait_ge(h_ready, i)
                for g, (f, s) in enumerate(groups):
                    at, n = SPANS[s]
                    k = 2 * G * i + g
                    if k >= 4:
                        pe.wait_ge(kept, k - 3)
                    for c in range(T):
                        mm = nc.tensor.matmul(m.ps[:, k % 4, 0:n], m.h[0:TP, c, f * P:(f + 1) * P],
                                              m.adjT[0:TP, c, at:at + n], start=(c == 0), stop=(c == T - 1))
                    mm.then_inc(mm_done, 1)
                for g, (f, s) in enumerate(groups):
                    at, n = SPANS[s]
                    k = 2 * G * i + G + g
                    pe.wait_ge(kept, max(k - 3, 2 * G * i + G))
                    for c in range(BC):
                        mm = nc.tensor.matmul(m.ps[:, k % 4, 0:n], m.wab[:, i * BC + c, f * P:(f + 1) * P],
                                              m.zT[:, c, at:at + n], start=(c == 0), stop=(c == BC - 1))
                    mm.then_inc(mm_done, 1)
                pe.wait_ge(kept, 2 * G * (i + 1))
                for t in range(T):
                    k = T * i + t
                    if k >= 4:
                        pe.wait_ge(zz_kept, k - 3)
                    for c in range(BC):
                        mm = nc.tensor.matmul(m.ps[0:TP, 4 + k % 4, 0:DB], m.aT[:, c, t * TP:(t + 1) * TP],
                                              m.wab[:, (LAYERS + i) * BC + c, :], start=(c == 0), stop=(c == BC - 1))
                    mm.then_inc(zz_done, 1)

        @block.scalar
        def _(act):
            for i in range(LAYERS):
                for g, (f, s) in enumerate(groups):
                    at, n = SPANS[s]
                    k = 2 * G * i + g
                    act.wait_ge(mm_done, k + 1)
                    nc.scalar.activation(m.zT[:, f, at:at + n], m.ps[:, k % 4, 0:n], ACT.Copy).then_inc(kept, 1)
                for g, (f, s) in enumerate(groups):
                    at, n = SPANS[s]
                    k = 2 * G * i + G + g
                    act.wait_ge(mm_done, k + 1)
                    nc.scalar.activation(m.aT[:, f, at:at + n], m.ps[:, k % 4, 0:n], ACT.Relu,
                                         bias=col(m, "ba", i * BC + f)).then_inc(kept, 1)
                act.wait_ge(var_ready, i + 1)
                nc.scalar.activation(m.rs[0:TP, :], m.ve[0:TP, :], ACT.Sqrt).then_inc(root_done, 1)

        @block.vector
        def _(dve):
            for i in range(LAYERS):
                for t in range(T):
                    k = T * i + t
                    dve.wait_ge(zz_done, k + 1)
                    nc.vector.tensor_tensor(m.zz[0:TP, t, :], m.ps[0:TP, 4 + k % 4, 0:DB], row(m, "bb", i, DB),
                                            ALU.add).then_inc(zz_kept, 1)
                    dve.drain()
                    nc.vector.bn_stats(m.stats[0:TP, 0:6], m.zz[0:TP, t, :])
                    dve.drain()
                    nc.vector.bn_aggr(m.mv[0:TP, 2, t, :], m.stats[0:TP, 0:6])
                dve.drain()
                inverse_root(nc.vector, var_ready, root_done, i + 1, m.mv[0:TP, 2, :, 1], m.ve[0:TP, :],
                             m.rs[0:TP, :], m.nt[0:TP, :])
                for t in range(T):
                    nc.vector.tensor_scalar(m.zz[0:TP, t, :], m.zz[0:TP, t, :], m.mv[0:TP, 2, t, 0:1],
                                            m.rs[0:TP, t:t + 1], ALU.subtract, ALU.mult)
                dve.drain()
                z = m.zz[0:TP, :, :]
                nc.vector.tensor_tensor(z, z, row(m, "ng", i, DB).unsqueeze(1).to_broadcast([TP, T, DB]), ALU.mult)
                dve.drain()
                nc.vector.tensor_tensor(z, z, row(m, "nb", i, DB).unsqueeze(1).to_broadcast([TP, T, DB]), ALU.add)
                dve.drain()
                nc.vector.scalar_tensor_tensor(m.h[0:TP, :, :], z, 0.0, m.h[0:TP, :, :], ALU.max,
                                               ALU.add).then_inc(h_ready, 1)
                dve.drain()


def combine(nc, m, w, x, wd1, wd2, wout, xn2, acc):
    NS = len(SPANS)
    groups = [(f, s) for f in range(HC) for s in range(NS)]
    with ExitStack() as ctx:
        def sem(name):
            return ctx.enter_context(nc.semaphore(name))
        wd1_in, wbig_in, h_turned, h_kept, d_done, d_kept = (sem(n) for n in (
            "wd1_in", "wbig_in", "h_turned", "hT_kept", "d_done", "d_kept"))
        x_in, delta_done, mix_done, delta_used, mix_used = (sem(n) for n in (
            "cx_in", "delta_done", "mix_done", "delta_used", "mix_used"))
        var_ready, root_done, x1_ready, xn_ready, stored, xn_stored = (sem(n) for n in (
            "cvar_ready", "croot_done", "x1_ready", "xn2_ready", "stored", "xn_stored"))
        turned, kept, logit_done, logit_kept, pads = (sem(n) for n in (
            "cturned", "ckept", "logit_done", "logit_kept", "pads"))
        xt, u, mx, xo = m.tile
        xT = m.h[:, 0:DC // 2, :].rearrange("p a b -> p (a b)")[:, 0:DC * TP].rearrange("p (c n) -> p c n", c=DC)
        block = ctx.enter_context(nc.Block())

        @block.sync
        def _(sp):
            sp.dma_start(m.wd1, wd1.rearrange("(c p) n -> p c n", p=P)).then_inc(wd1_in, 16)
            sp.dma_start(m.wd2, wd2.rearrange("(c p) n -> p c n", p=P)).then_inc(wbig_in, 16)
            sp.dma_start(m.wout, wout.rearrange("(c p) n -> p c n", p=P)).then_inc(wbig_in, 16)
            sp.wait_ge(pads, 1)
            sp.dma_start(xn2[N:N + PADROWS, 0:512], m.zeros[:].bitcast(F32).unsqueeze(1).to_broadcast([P, 2, 256])
                         ).then_inc(stored, 16)
            sp.dma_start(xn2[N:N + PADROWS, 512:1024], m.zeros[:].bitcast(F32).unsqueeze(1).to_broadcast([P, 2, 256])
                         ).then_inc(stored, 16)
            sp.dma_start(acc[N:N + PADROWS, 0:512], m.zeros[:].bitcast(F32).unsqueeze(1).to_broadcast([P, 2, 256])
                         ).then_inc(stored, 16)
            sp.dma_start(acc[N:N + PADROWS, 512:1024], m.zeros[:].bitcast(F32).unsqueeze(1).to_broadcast([P, 2, 256])
                         ).then_inc(stored, 16)
            for t in range(T):
                sp.wait_ge(x1_ready, t + 1)
                sp.dma_start(acc[t * TP:(t + 1) * TP, :], mx[0:TP, :]).then_inc(stored, 16)
                sp.wait_ge(xn_ready, t + 1)
                sp.dma_start(xn2[t * TP:(t + 1) * TP, :], xo[0:TP, :]).then_inc(xn_stored, 16)
            sp.wait_ge(stored, 16 * (T + 4))
            sp.wait_ge(xn_stored, 16 * T)

        @block.gpsimd
        def _(pool):
            pool.drain().then_inc(pads, 1)
            for t in range(T):
                if t:
                    pool.wait_ge(x1_ready, t)
                pool.dma_start(xt[0:TP, :], x[t * TP:(t + 1) * TP, :]).then_inc(x_in, 16)

        @block.tensor
        def _(pe):
            for t in range(T):
                if t >= 4:
                    pe.wait_ge(h_kept, t - 3)
                for f in range(BC):
                    mm = nc.tensor.transpose(m.ps[:, t % 4, f * TP:(f + 1) * TP], m.h[0:TP, t, f * P:(f + 1) * P],
                                             m.ident[0:TP, 0:TP])
                mm.then_inc(h_turned, 1)
            pe.wait_ge(h_kept, T)
            pe.wait_ge(wd1_in, 16)
            for g, (f, s) in enumerate(groups):
                at, n = SPANS[s]
                if g >= 4:
                    pe.wait_ge(d_kept, g - 3)
                for c in range(BC):
                    mm = nc.tensor.matmul(m.ps[:, g % 4, 0:n], m.wd1[:, c, f * P:(f + 1) * P],
                                          m.hT[:, c, at:at + n], start=(c == 0), stop=(c == BC - 1))
                mm.then_inc(d_done, 1)
            pe.wait_ge(d_kept, len(groups))
            pe.wait_ge(wbig_in, 32)

            def router(t):
                pe.wait_ge(xn_ready, t + 1)
                if t:
                    pe.wait_ge(kept, t)
                for c in range(DC):
                    mm = nc.tensor.transpose(m.ps[:, 4 + c // 4, (c % 4) * TP:(c % 4 + 1) * TP],
                                             xo[0:TP, c * P:(c + 1) * P], m.ident[0:TP, 0:TP])
                mm.then_inc(turned, 1)
                pe.wait_ge(kept, t + 1)
                if t:
                    pe.wait_ge(logit_kept, t)
                for c in range(DC):
                    mm = nc.tensor.matmul(m.ps[0:TP, 6, 0:E], xT[:, c, :], m.gatew[:, c, :],
                                          start=(c == 0), stop=(c == DC - 1))
                mm.then_inc(logit_done, 1)

            pe.wait_ge(w.gatew_in, 16)
            for t in range(T):
                if t:
                    pe.wait_ge(delta_used, t)
                for half in range(2):
                    for c in range(HC):
                        mm = nc.tensor.matmul(m.ps[0:TP, half, :], m.dT[:, c, t * TP:(t + 1) * TP],
                                              m.wd2[:, c, half * 512:half * 512 + 512],
                                              start=(c == 0), stop=(c == HC - 1))
                mm.then_inc(delta_done, 1)
                if t:
                    pe.wait_ge(mix_used, t)
                for half in range(2):
                    for c in range(DC):
                        mm = nc.tensor.matmul(m.ps[0:TP, 2 + half, :], m.qT[:, c, t * TP:(t + 1) * TP],
                                              m.wout[:, c, half * 512:half * 512 + 512],
                                              start=(c == 0), stop=(c == DC - 1))
                mm.then_inc(mix_done, 1)
                if t:
                    router(t - 1)
            router(T - 1)

        @block.scalar
        def _(act):
            for t in range(T):
                act.wait_ge(h_turned, t + 1)
                nc.scalar.activation(m.hT[:, :, t * TP:(t + 1) * TP],
                                     m.ps[:, t % 4, 0:BC * TP].rearrange("p (f n) -> p f n", f=BC),
                                     ACT.Copy).then_inc(h_kept, 1)
            for g, (f, s) in enumerate(groups):
                at, n = SPANS[s]
                act.wait_ge(d_done, g + 1)
                nc.scalar.activation(m.dT[:, f, at:at + n], m.ps[:, g % 4, 0:n], ACT.Relu,
                                     bias=col(m, "bd1", f)).then_inc(d_kept, 1)
            for t in range(T):
                for i in range(2):
                    act.wait_ge(var_ready, 2 * t + i + 1)
                    nc.scalar.activation(m.rs[0:TP, t:t + 1], m.ve[0:TP, t:t + 1], ACT.Sqrt).then_inc(root_done, 1)
                act.wait_ge(turned, t + 1)
                if t:
                    act.wait_ge(logit_done, t)
                for i in range(2):
                    a = nc.scalar.activation(xT[:, 4 * i:4 * i + 4, :],
                                             m.ps[:, 4 + i, 0:4 * TP].rearrange("p (c n) -> p c n", c=4), ACT.Copy)
                a.then_inc(kept, 1)
                act.wait_ge(logit_done, t + 1)
                nc.scalar.activation(m.logit[0:TP, t, :], m.ps[0:TP, 6, 0:E], ACT.Copy).then_inc(logit_kept, 1)

        @block.vector
        def _(dve):
            for t in range(T):
                dve.wait_ge(x_in, 16 * (t + 1))
                xt_, u_, mx_, xo_ = (v[0:TP, :] for v in (xt, u, mx, xo))
                nc.vector.tensor_scalar(u_, xt_, m.mr[0:TP, t, 0:1], m.mr[0:TP, t, 1:2], ALU.subtract, ALU.mult)
                dve.drain()
                nc.vector.tensor_tensor(u_, u_, row(m, "bd2"), ALU.add)
                dve.drain()
                dve.wait_ge(delta_done, t + 1)
                nc.vector.tensor_tensor(u_, m.ps[0:TP, 0:2, :].rearrange("p a b -> p (a b)"), u_,
                                        ALU.add).then_inc(delta_used, 1)
                dve.drain()
                for i in range(2):
                    nc.vector.bn_stats(m.stats[0:TP, 6 * i:6 * i + 6], u_[:, 512 * i:512 * i + 512])
                dve.drain()
                nc.vector.bn_aggr(m.mv[0:TP, 0, t, :], m.stats[0:TP, :])
                dve.drain()
                inverse_root(nc.vector, var_ready, root_done, 2 * t + 1, m.mv[0:TP, 0, t, 1:2],
                             m.ve[0:TP, t:t + 1], m.rs[0:TP, t:t + 1], m.nt[0:TP, t:t + 1])
                nc.vector.tensor_scalar(u_, u_, m.mv[0:TP, 0, t, 0:1], m.rs[0:TP, t:t + 1], ALU.subtract, ALU.mult)
                dve.drain()
                nc.vector.tensor_tensor(u_, u_, row(m, "og"), ALU.mult)
                dve.drain()
                nc.vector.tensor_tensor(u_, u_, row(m, "ob"), ALU.add)
                dve.drain()
                nc.vector.tensor_tensor(u_, u_, xt_, ALU.add)
                dve.drain()
                nc.vector.tensor_tensor(u_, u_, row(m, "bo"), ALU.add)
                dve.drain()
                dve.wait_ge(mix_done, t + 1)
                dve.wait_ge(stored, 16 * (t + 4 if t else 0))
                nc.vector.tensor_tensor(mx_, m.ps[0:TP, 2:4, :].rearrange("p a b -> p (a b)"), u_,
                                        ALU.add).then_inc(mix_used, 1)
                dve.drain()
                nc.vector.bn_stats(m.stats[0:TP, 0:6], mx_[:, 0:512]).then_inc(x1_ready, 1)
                nc.vector.bn_stats(m.stats[0:TP, 6:12], mx_[:, 512:1024])
                dve.drain()
                nc.vector.bn_aggr(m.mv[0:TP, 1, t, :], m.stats[0:TP, :])
                dve.drain()
                inverse_root(nc.vector, var_ready, root_done, 2 * t + 2, m.mv[0:TP, 1, t, 1:2],
                             m.ve[0:TP, t:t + 1], m.rs[0:TP, t:t + 1], m.nt[0:TP, t:t + 1])
                if t:
                    dve.wait_ge(xn_stored, 16 * t)
                    dve.wait_ge(turned, t)
                nc.vector.tensor_scalar(xo_, mx_, m.mv[0:TP, 1, t, 0:1], m.rs[0:TP, t:t + 1], ALU.subtract,
                                        ALU.mult).then_inc(xn_ready, 1)
                dve.drain()


def route(nc, m, tabd):
    with ExitStack() as ctx:
        def sem(name):
            return ctx.enter_context(nc.semaphore(name))
        shifted, exped, masked, ranked, tabled, tab_out, tab_in = (sem(n) for n in (
            "shifted", "rexped", "masked", "ranked", "tabled", "tab_out", "tab_in"))
        HT = T // 2
        block = ctx.enter_context(nc.Block())

        def per_tile(v):
            return v[0:TP, :].unsqueeze(2).to_broadcast([TP, T, E])

        @block.scalar
        def _(act):
            act.wait_ge(shifted, 1)
            nc.scalar.activation(m.score[0:TP, :, :], m.logit[0:TP, :, :], ACT.Exp).then_inc(exped, 1)

        @block.vector
        def _(dve):
            logit, score, rep = (v[0:TP, :, :] for v in (m.logit, m.score, m.rep))
            top1, total, inv, topsum = (m.sc[:, i, :] for i in range(4))
            nc.vector.tensor_reduce(top1[0:TP, :], logit, AX, ALU.max)
            dve.drain()
            nc.vector.tensor_tensor(logit, logit, per_tile(top1), ALU.subtract).then_inc(shifted, 1)
            dve.wait_ge(exped, 1)
            nc.vector.tensor_reduce(total[0:TP, :], score, AX, ALU.add)
            dve.drain()
            nc.vector.reciprocal(inv[0:TP, :], total[0:TP, :])
            dve.drain()
            nc.vector.tensor_tensor(score, score, per_tile(inv), ALU.mult)
            dve.drain()
            for t in range(T):
                nc.vector.max(m.top[0:TP, t, :], m.score[0:TP, t, :])
            dve.drain()
            for t in range(T):
                nc.vector.match_replace(m.rep[0:TP, t, :], m.top[0:TP, t, :], m.score[0:TP, t, :], -1.0)
            dve.drain()
            nc.vector.tensor_scalar(m.mask[0:TP, :, :], rep, 0.0, None, ALU.is_lt)
            nc.vector.tensor_reduce(topsum[0:TP, :], m.top[0:TP, :, :], AX, ALU.add)
            nc.vector.memset(m.mprev[0:TP, 0, :], 0.0)
            dve.drain()
            for t in range(T):
                v = nc.vector.tensor_tensor(m.mprev[0:TP, t + 1, :], m.mprev[0:TP, t, :], m.mask[0:TP, t, :], ALU.add)
                if t == T - 1:
                    v.then_inc(masked, 1)
                dve.drain()
            nc.vector.tensor_scalar(topsum[0:TP, :], topsum[0:TP, :], 1e-20, None, ALU.add)
            dve.drain()
            nc.vector.reciprocal(inv[0:TP, :], topsum[0:TP, :])
            dve.drain()
            nc.vector.tensor_tensor(score, score, m.mask[0:TP, :, :], ALU.mult)
            dve.drain()
            nc.vector.tensor_tensor(score, score, per_tile(inv), ALU.mult)
            for t in range(T):
                nc.vector.memset(m.sel[0:TP, t, :, 0], float(t))
            nc.vector.memset(m.sel[0:TP, :, :, 2], 1.0)
            nc.vector.tensor_scalar(m.sel[0:TP, :, :, 1], m.onesf[0:TP, 0:1].unsqueeze(1).to_broadcast([TP, T, E]),
                                    m.pos[0:TP, 0:1], None, ALU.mult)
            dve.drain()
            nc.vector.tensor_copy(m.sel[0:TP, :, :, 3], score)
            dve.drain()
            nc.vector.tensor_tensor(score, score, m.sel[0:TP, :, :, 3], ALU.subtract)
            dve.drain()
            nc.vector.tensor_copy(m.sel[0:TP, :, :, 4], score)
            dve.drain()
            nc.vector.tensor_tensor(score, score, m.sel[0:TP, :, :, 4], ALU.subtract)
            dve.drain()
            nc.vector.tensor_copy(m.sel[0:TP, :, :, 5], score)
            dve.wait_ge(ranked, 1)
            for i in range(2):
                nc.vector.scalar_tensor_tensor(
                    m.place[0:TP, i * HT:(i + 1) * HT, :],
                    m.ps[0:TP, i, 0:HT * E].rearrange("p (t e) -> p t e", t=HT), 1.0,
                    m.mask[0:TP, i * HT:(i + 1) * HT, :], ALU.add, ALU.mult)
            n, nb, end, before, cmp, prod = (m.cnt[:, i, :] for i in range(6))
            nc.vector.tensor_copy(n, m.ps[:, 2, 0:E])
            dve.drain()
            nc.vector.tensor_scalar(m.place[0:TP, :, :], m.place[0:TP, :, :], -1.0, None, ALU.add)
            nc.vector.memset(nb, 1.0)
            dve.drain()
            for j in range(1, BMAX):
                nc.vector.scalar_tensor_tensor(nb, n, float(P * j), nb, ALU.is_gt, ALU.add)
                dve.drain()
            nc.vector.tensor_tensor_scan(end, m.onesf[:, 0:E], nb, 0.0, ALU.mult, ALU.add)
            dve.drain()
            nc.vector.tensor_tensor(before, end, nb, ALU.subtract)
            dve.drain()
            nc.vector.tensor_copy(m.nbi[:, 0, :], nb)
            nc.vector.tensor_copy(m.nbi[:, 1, :], before)
            nc.vector.tensor_copy(m.tot[:], end[:, E - 1:E])
            for h in range(2):
                a, s = m.cnt[:, 6, 0:1], m.cnt[:, 6, 1:2]
                dve.drain()
                nc.vector.tensor_scalar(cmp, end, m.pos[:, h:h + 1], None, ALU.is_le)
                dve.drain()
                nc.vector.tensor_reduce(a, cmp, AX, ALU.add)
                nc.vector.tensor_tensor(prod, cmp, nb, ALU.mult)
                dve.drain()
                nc.vector.tensor_reduce(s, prod, AX, ALU.add)
                nc.vector.tensor_scalar(a, a, float(E - 1), None, ALU.min)
                dve.drain()
                nc.vector.tensor_tensor(s, m.pos[:, h:h + 1], s, ALU.subtract)
                nc.vector.tensor_copy(m.tabp[:, h, 0:1], a)
                dve.drain()
                nc.vector.tensor_scalar(s, s, float(BMAX - 1), float(P), ALU.min, ALU.mult)
                dve.drain()
                nc.vector.tensor_copy(m.tabp[:, h, 1:2], s).then_inc(tabled, 1)

        @block.tensor
        def _(pe):
            pe.wait_ge(masked, 1)
            for t in range(T):
                o = m.ps[0:TP, t // HT, (t % HT) * E:(t % HT + 1) * E]
                nc.tensor.matmul(o, m.before[0:TP, 0:TP], m.mask[0:TP, t, :], start=(t % HT == 0), stop=False,
                                 skip_group_check=True)
                nc.tensor.matmul(o, m.ones[0:TP, 0:TP], m.mprev[0:TP, t, :], start=False, stop=True,
                                 skip_group_check=True)
            nc.tensor.matmul(m.ps[:, 2, 0:E], m.ones[0:TP, :], m.mprev[0:TP, T, :], start=True,
                             stop=True).then_inc(ranked, 1)

        @block.sync
        def _(sp):
            sp.wait_ge(tabled, 2)
            for h in range(2):
                sp.dma_start(tabd[h * P:(h + 1) * P, :], m.tabp[:, h, :]).then_inc(tab_out, 16)
            sp.wait_ge(tab_out, 32)
            sp.dma_start(m.tab[:], tabd.rearrange("b k -> (b k)").unsqueeze(0)).then_inc(tab_in, 16)
            sp.wait_ge(tab_in, 16)


def experts(nc, m, wg, wu, wd, xn2, acc, out):
    FOUR = 4 * P
    with ExitStack() as ctx:
        def sem(name):
            return ctx.enter_context(nc.semaphore(name))
        gate_in, up_in, down_in = ([sem(f"{n}_in{s}") for s in range(2)] for n in ("gate", "up", "down"))
        hot_ready, listed, meta_ready, gathered = sem("hot_ready"), sem("listed"), sem("meta_ready"), sem("gathered")
        x_turned, xT_ready, gu_done, exp_ready, g_used = (sem(n) for n in (
            "x_turned", "xT_ready", "gu_done", "exp_ready", "g_used"))
        h_ready, h_turned, hT_ready, down_done, y_ready, added, copied = (sem(n) for n in (
            "eh_ready", "eh_turned", "ehT_ready", "down_done", "y_ready", "added", "copied"))
        landed = sem("landed")
        block = ctx.enter_context(nc.Block())

        @block.sync
        def _(sp):
            def load(e, s):
                sp.dma_start(m.wgate[s], wg[e].rearrange("p (c f) -> p c f", c=DC)).then_inc(gate_in[s], 16)
                sp.dma_start(m.wup[s], wu[e].rearrange("p (c f) -> p c f", c=DC)).then_inc(up_in[s], 16)
                sp.dma_start(m.wdown[s], wd[e].rearrange("p (c d) -> p c d", c=FC)).then_inc(down_in[s], 16)

            def load_at(e, s):
                sp.dma_start(m.wgate[s], wg[bass.ds(e, 1)].rearrange("o p (c f) -> p (o c) f", c=DC)
                             ).then_inc(gate_in[s], 16)
                sp.dma_start(m.wup[s], wu[bass.ds(e, 1)].rearrange("o p (c f) -> p (o c) f", c=DC)
                             ).then_inc(up_in[s], 16)
                sp.dma_start(m.wdown[s], wd[bass.ds(e, 1)].rearrange("o p (c d) -> p (o c) d", c=FC)
                             ).then_inc(down_in[s], 16)

            for s in range(2):
                load(s, s)
            with sp.Fori(1, E // 2) as e2:
                for s in range(2):
                    used = sp.value_load(m.nbi[0:1, 1, bass.ds(e2 * 2 + (s - 1), 1)], min_val=0, max_val=MAXB)
                    sp.wait_ge(down_done, used)
                    load_at(e2 * 2 + s, s)
            total = sp.value_load(m.tot[0:1, 0:1], min_val=E, max_val=MAXB)
            sp.wait_ge(added, total * 16)
            sp.dma_start(out.rearrange("n d -> (n d)").rearrange("(a b) -> a b", b=1000),
                         acc[0:N, :].rearrange("n d -> (n d)").rearrange("(a b) -> a b", b=1000)
                         ).then_inc(copied, 16)
            sp.wait_ge(copied, 16)

        @block.tensor
        def _(pe):
            def make_list():
                for t in range(T):
                    mm = nc.tensor.matmul(m.ps[:, 1, 2 * P:2 * P + 6], m.oh[0:TP, t, :], m.sw[0:TP, t, :],
                                          start=(t == 0), stop=(t == T - 1))
                mm.then_inc(listed, 1)

            def turn_x():
                for c in range(DC):
                    mm = nc.tensor.transpose(m.ps[:, 6 + c // 4, (c % 4) * P:(c % 4 + 1) * P],
                                             m.xg[:, c * P:(c + 1) * P], m.ident[:])
                mm.then_inc(x_turned, 1)

            for b in range(2):
                pe.wait_ge(hot_ready, b + 1)
                make_list()
            pe.wait_ge(gathered, 16)
            turn_x()
            with pe.Fori(0, E // 2) as e2:
                for s in range(2):
                    blocks = pe.value_load(m.nbi[0:1, 0, bass.ds(e2 * 2 + s, 1)], min_val=1, max_val=BMAX)
                    before = pe.value_load(m.nbi[0:1, 1, bass.ds(e2 * 2 + s, 1)], min_val=0, max_val=MAXB)
                    with pe.Fori(0, blocks) as j:
                        k = pe.snap(before + j)
                        pe.wait_ge(xT_ready, k * 2 + 2)
                        pe.wait_ge(gate_in[s], e2 * 16 + 16)
                        for half in range(2):
                            for c in range(DC):
                                mm = nc.tensor.matmul(m.ps[:, half, 0:FH], m.xT[:, c, :],
                                                      m.wgate[s][:, c, half * FH:(half + 1) * FH],
                                                      start=(c == 0), stop=(c == DC - 1))
                            mm.then_inc(gu_done, 1)
                        pe.wait_ge(up_in[s], e2 * 16 + 16)
                        for half in range(2):
                            for c in range(DC):
                                mm = nc.tensor.matmul(m.ps[:, 2 + half, 0:FH], m.xT[:, c, :],
                                                      m.wup[s][:, c, half * FH:(half + 1) * FH],
                                                      start=(c == 0), stop=(c == DC - 1))
                            mm.then_inc(gu_done, 1)
                        pe.wait_ge(gathered, k * 16 + 32)
                        turn_x()
                        pe.wait_ge(hot_ready, k + 3)
                        pe.wait_ge(g_used, k + 2)
                        make_list()
                        pe.wait_ge(h_ready, k + 1)
                        for c in range(FC):
                            mm = nc.tensor.transpose(m.ps[:, c // 4, (c % 4) * P:(c % 4 + 1) * P],
                                                     m.hx[:, c * P:(c + 1) * P], m.ident[:])
                        mm.then_inc(h_turned, 1)
                        pe.wait_ge(hT_ready, k * 2 + 2)
                        pe.wait_ge(down_in[s], e2 * 16 + 16)
                        pe.wait_ge(y_ready, k * 2 + 2)
                        for half in range(2):
                            for c in range(FC):
                                mm = nc.tensor.matmul(m.ps[:, 4 + half, :], m.hxT[:, c, :],
                                                      m.wdown[s][:, c, half * 512:half * 512 + 512],
                                                      start=(c == 0), stop=(c == FC - 1))
                        mm.then_inc(down_done, 1)

        @block.scalar
        def _(act):
            total = act.value_load(m.tot[0:1, 0:1], min_val=E, max_val=MAXB)

            def keep_x():
                nc.scalar.activation(m.xT[:, 0:4, :], m.ps[:, 6, :].rearrange("p (c n) -> p c n", c=4),
                                     ACT.Copy).then_inc(xT_ready, 1)

            act.wait_ge(x_turned, 1)
            keep_x()
            with act.Fori(0, total) as k:
                act.wait_ge(g_used, k + 1)
                for half in range(2):
                    act.wait_ge(gu_done, k * 4 + half + 1)
                    nc.scalar.activation(m.ex[:, half * FH:(half + 1) * FH], m.ps[:, half, 0:FH], ACT.Exp,
                                         scale=-1.0).then_inc(exp_ready, 1)
                act.wait_ge(h_turned, k + 1)
                nc.scalar.activation(m.hxT[:, 0:4, :], m.ps[:, 0, :].rearrange("p (c n) -> p c n", c=4),
                                     ACT.Copy).then_inc(hT_ready, 1)
                act.wait_ge(x_turned, k + 2)
                keep_x()
                act.wait_ge(down_done, k + 1)
                act.wait_ge(meta_ready, k + 3)
                act.wait_ge(landed, k + 1)
                nc.scalar.activation(m.yo[:, 0:512], m.ps[:, 4, :], ACT.Copy,
                                     scale=m.meta[:, 2, 2:3]).then_inc(y_ready, 1)

        @block.vector
        def _(dve):
            total = dve.value_load(m.tot[0:1, 0:1], min_val=E, max_val=MAXB)

            def one_hot(b):
                e = dve.value_load(m.tab[0:1, bass.ds(b * 2, 1)], min_val=0, max_val=E - 1)
                at = dve.value_load(m.tab[0:1, bass.ds(b * 2 + 1, 1)], min_val=0, max_val=(BMAX - 1) * P)
                nc.vector.tensor_tensor(m.oh[0:TP, :, :],
                                        m.place[0:TP, :, bass.ds(e, 1)].to_broadcast([TP, T, P]),
                                        m.iota[0:TP, bass.ds(at, P)].unsqueeze(1).to_broadcast([TP, T, P]),
                                        ALU.is_equal)
                nc.vector.tensor_copy(m.sw[0:TP, :, :].unsqueeze(2),
                                      m.sel[0:TP, :, bass.ds(e, 1), :]).then_inc(hot_ready, 1)

            def take_list():
                nc.vector.tensor_copy(m.selc[:], m.ps[:, 1, 2 * P:2 * P + 6])

            def meta(first):
                c = m.selc
                nc.vector.tensor_tensor(m.wpart[:], c[:, 3:4], c[:, 4:5], ALU.add)
                if not first:
                    nc.vector.tensor_copy(m.metai[:, 2, :], m.metai[:, 1, :])
                    dve.drain()
                    nc.vector.tensor_copy(m.metai[:, 1, :], m.metai[:, 0, :])
                dve.drain()
                nc.vector.scalar_tensor_tensor(m.metai[:, 0, 0:1], c[:, 0:1], float(TP), c[:, 1:2], ALU.mult, ALU.add)
                nc.vector.tensor_scalar(m.metai[:, 0, 1:2], c[:, 2:3], m.pos[:, 3:4], m.pos[:, 2:3], ALU.mult, ALU.add)
                nc.vector.tensor_tensor(m.meta[:, 0, 2:3], m.wpart[:], c[:, 5:6], ALU.add).then_inc(meta_ready, 1)

            nc.vector.memset(m.meta[:], 0.0)
            dve.drain().then_inc(g_used, 1)
            dve.drain().then_inc(y_ready, 2)
            one_hot(0)
            dve.wait_ge(listed, 1)
            take_list()
            dve.drain()
            meta(first=True)
            one_hot(1)
            dve.wait_ge(listed, 2)
            take_list()
            dve.drain()
            dve.wait_ge(gathered, 16)
            meta(first=False)
            one_hot(2)
            dve.wait_ge(x_turned, 1)
            nc.vector.tensor_copy(m.xT[:, 4:8, :], m.ps[:, 7, :].rearrange("p (c n) -> p c n", c=4)
                                  ).then_inc(xT_ready, 1)
            with dve.Fori(0, total) as k:
                for half in range(2):
                    ex = m.ex[:, half * FH:(half + 1) * FH]
                    hx = m.hx[:, half * FH:(half + 1) * FH]
                    dve.wait_ge(exp_ready, k * 2 + half + 1)
                    nc.vector.tensor_scalar(ex, ex, 1.0, None, ALU.add)
                    dve.drain()
                    nc.vector.reciprocal(ex, ex)
                    dve.drain()
                    v = nc.vector.tensor_tensor(hx, m.ps[:, half, 0:FH], ex, ALU.mult)
                    if half:
                        v.then_inc(g_used, 1)
                    dve.drain()
                for half in range(2):
                    hx = m.hx[:, half * FH:(half + 1) * FH]
                    dve.wait_ge(gu_done, k * 4 + 3 + half)
                    v = nc.vector.tensor_tensor(hx, m.ps[:, 2 + half, 0:FH], hx, ALU.mult)
                v.then_inc(h_ready, 1)
                dve.wait_ge(h_turned, k + 1)
                take_list()
                nc.vector.tensor_copy(m.hxT[:, 4:6, :], m.ps[:, 1, 0:2 * P].rearrange("p (c n) -> p c n", c=2)
                                      ).then_inc(hT_ready, 1)
                dve.wait_ge(x_turned, k + 2)
                nc.vector.tensor_copy(m.xT[:, 4:8, :], m.ps[:, 7, :].rearrange("p (c n) -> p c n", c=4)
                                      ).then_inc(xT_ready, 1)
                dve.drain()
                dve.wait_ge(landed, k + 1)
                dve.wait_ge(y_ready, k * 2 + 2)
                meta(first=False)
                one_hot(k + 3)
                dve.wait_ge(down_done, k + 1)
                nc.vector.tensor_scalar(m.yo[:, 512:1024], m.ps[:, 5, :], m.meta[:, 2, 2:3], None,
                                        ALU.mult).then_inc(y_ready, 1)

        @block.gpsimd
        def _(pool):
            total = pool.value_load(m.tot[0:1, 0:1], min_val=E, max_val=MAXB)

            def gather():
                nc.gpsimd.tensor_tensor(m.idx[:, 0:1], m.metai[:, 0, 0:1], m.metai[:, 0, 1:2], ALU.add)
                pool.drain()
                pool.indirect_dma_start(out=m.xg, out_offset=None, in_=xn2,
                                        in_offset=bass.IndirectOffsetOnAxis(ap=m.idx[:, 0:1], axis=0)
                                        ).then_inc(gathered, 16)

            pool.sem_inc(landed, 1)
            pool.wait_ge(meta_ready, 1)
            gather()
            pool.wait_ge(meta_ready, 2)
            pool.wait_ge(x_turned, 1)
            gather()
            with pool.Fori(0, total) as k:
                pool.wait_ge(meta_ready, k + 3)
                pool.wait_ge(x_turned, k + 2)
                gather()
                pool.wait_ge(y_ready, k * 2 + 4)
                nc.gpsimd.tensor_tensor(m.idx[:, 1:2], m.metai[:, 2, 0:1], m.metai[:, 2, 1:2], ALU.add)
                pool.drain()
                pool.indirect_dma_start(out=acc, out_offset=bass.IndirectOffsetOnAxis(ap=m.idx[:, 1:2], axis=0),
                                        in_=m.yo, in_offset=None, compute_op=ALU.add).then_inc(added, 16)
                pool.wait_ge(added, k * 16 + 16)
                pool.sem_inc(landed, 1)
            pool.wait_ge(gathered, total * 16 + 32)


def kernel(x, src, dst, L0_gnn_ln_in_g, L0_gnn_ln_in_b, L0_gnn_W1, L0_gnn_b1, L0_gnn_W2, L0_gnn_b2,
           L0_gnn_layer_Wa, L0_gnn_layer_ba, L0_gnn_layer_Wb, L0_gnn_layer_bb, L0_gnn_layer_ng,
           L0_gnn_layer_nb, L0_gnn_Wd1, L0_gnn_bd1, L0_gnn_Wd2, L0_gnn_bd2, L0_gnn_out_g, L0_gnn_out_b,
           L0_mix_w_qkv, L0_mix_w_out, L0_mix_b_out, L0_ffn_gate_w, L0_ffn_w_gate, L0_ffn_w_up,
           L0_ffn_w_down):
    import numpy as np
    import concourse.bacc as bacc
    from concourse.bass_utils import run_bass_kernel_spmd

    def arr(a):
        return np.ascontiguousarray(a)

    def on_partitions(v):
        return np.asarray(v).reshape(-1, P).T

    def chunked(wt):
        wt = np.asarray(wt)
        e, n, k = wt.shape
        return arr(wt.reshape(e, n, k // P, P).transpose(0, 3, 2, 1)).reshape(e, P, k // P * n)

    cols = arr(np.concatenate([on_partitions(v) for v in (
        L0_gnn_ln_in_g, L0_gnn_ln_in_b, L0_gnn_b1, L0_gnn_layer_ba, L0_gnn_bd1)], axis=1))
    rows = arr(np.concatenate([np.asarray(v).reshape(1, -1) for v in (
        L0_gnn_b2, L0_gnn_layer_bb, L0_gnn_layer_ng, L0_gnn_layer_nb, L0_gnn_bd2, L0_gnn_out_g,
        L0_gnn_out_b, L0_mix_b_out)], axis=1))
    arrays = {
        "x": arr(x), "srcT": arr(np.asarray(src).reshape(CHUNKS, CE).T),
        "dstT": arr(np.asarray(dst).reshape(CHUNKS, CE).T), "dst": arr(dst), "cols": cols, "rows": rows,
        "w1": arr(L0_gnn_W1), "w2": arr(L0_gnn_W2), "wa": arr(L0_gnn_layer_Wa), "wb": arr(L0_gnn_layer_Wb),
        "wd1": arr(L0_gnn_Wd1), "wd2": arr(L0_gnn_Wd2), "wqkv": arr(L0_mix_w_qkv), "wout": arr(L0_mix_w_out),
        "gatew": chunked(np.asarray(L0_ffn_gate_w)[None])[0],
        "wg": chunked(L0_ffn_w_gate), "wu": chunked(L0_ffn_w_up), "wd": chunked(L0_ffn_w_down),
    }
    nc = bacc.Bacc("TRN2", target_bir_lowering=False, num_devices=1)
    args = {n: nc.dram_tensor("in_" + n, a.shape, mybir.dt.from_np(a.dtype), kind="ExternalInput").ap()
            for n, a in arrays.items()}
    out = nc.dram_tensor("out", (N, D), F32, kind="ExternalOutput").ap()
    build(nc, **args, out=out)
    r = run_bass_kernel_spmd(nc, [{"in_" + n: a for n, a in arrays.items()}], core_ids=[0])
    return r.results[0]["out"]
```

```python
from contextlib import ExitStack

import concourse.bass as bass
from concourse import mybir

F32 = mybir.dt.float32
F32R = mybir.dt.float32r
BF16 = mybir.dt.bfloat16
I32 = mybir.dt.int32
I16 = mybir.dt.int16
ALU = mybir.AluOpType
ACT = mybir.ActivationFunctionType
AX = mybir.AxisListType.X
RMAX = bass.bass_isa.ReduceOp.max

P = 128
N, D = 1250, 1024
TP = 125
T = N // TP
DC = D // P
HID, DB = 512, 256
HC, BC = HID // P, DB // P
LAYERS = 3
HEADS, DH = 16, 64
PAIRS = HEADS // 2
E, TOPK, F = 64, 8, 768
FC, FH = F // P, F // 2
EDGES = 40000
CE = 125
CHUNKS = EDGES // CE
EP = 32
PAIRQ = CHUNKS // 2 // EP
NPAIR = CHUNKS // 2
SPANS = ((0, 418), (418, 416), (834, 416))
UNIT = 256
KB = DC * UNIT
MAXB = E + (N * TOPK - E) // P + 1
BMAX = (N + P - 1) // P
TAB = MAXB + BMAX + 3
WCOLS = 3 * DC * F
PIECE = 768
PIECES = WCOLS // PIECE
MP = PIECES // 3
RAW = 6
PADROWS = P
EPS = 1e-5

ROWS = {}
_at = 0
for _name, _n in (("b2", DB), ("bb", LAYERS * DB), ("ng", LAYERS * DB), ("nb", LAYERS * DB),
                  ("bd2", D), ("og", D), ("ob", D), ("bo", D)):
    ROWS[_name] = (_at, _n)
    _at += _n
ROWLEN = _at
COLS = {}
_at = 0
for _name, _n in (("g", DC), ("b", DC), ("b1", HC), ("ba", LAYERS * BC), ("bd1", HC)):
    COLS[_name] = (_at, _n)
    _at += _n
COLLEN = _at


class Names:
    pass


def memory(nc, ctx):
    def sb(name, shape, dt=F32):
        return ctx.enter_context(nc.sbuf_tensor(name, shape, dt))

    m = Names()
    m.ps = ctx.enter_context(nc.psum_tensor("ps", [P, 8, 512], F32))
    arena_at = (nc.sbuf_base + 31) // 32 * 32
    arena = sb("arena", [P, 2 * WCOLS])
    m.arena = arena
    r0, r1, r2, r3 = 0, 12500, 22500, 30692

    def view(at, *shape):
        n = 1
        for s in shape:
            n *= s
        v = arena[:, at:at + n]
        if len(shape) == 2:
            return v.rearrange("p (a b) -> p a b", a=shape[0])
        if len(shape) == 3:
            return v.rearrange("p (a b c) -> p a b c", a=shape[0], b=shape[1])
        return v

    m.view = view
    m.xnT = view(r0, DC, N)
    m.adjT = view(r0, T, N)
    m.wout = view(r0, DC, D)
    m.wd2 = view(r0 + DC * D, HC, D)
    m.h0T = view(r1, DC, N)
    m.qT = view(r1, DC, N)
    m.w1 = view(r2, DC, HID)
    m.w2 = view(r2 + DC * HID, HC, DB)
    m.unit = [view(r2 + s * KB, DC, UNIT) for s in range(4)]
    m.wab = view(r2, 2 * LAYERS * BC, DB)
    m.zz = view(r2 + 4096, T, DB)
    m.hT = view(r2, BC, N)
    m.wd1 = view(r2 + 2500, BC, HID)
    m.tile = [view(r2 + 2500 + 1024 + i * D, D) for i in range(4)]
    m.row = [view(r3 + i * D, D) for i in range(6)]
    m.h1T = view(r3, HC, N)
    m.kvm = view(r3, PAIRS, P)
    m.zm = view(r3 + 1024, PAIRS, P)
    m.kt = [view(r3 + 2048 + i * UNIT, UNIT) for i in range(2)]
    m.vt = [view(r3 + 2560 + i * UNIT, UNIT) for i in range(2)]
    m.tmp = [view(r3 + 3072 + i * 418, 418) for i in range(3)]
    m.zT = view(r3, BC, N)
    m.aT = view(r3 + 2500, BC, N)
    m.dT = view(r3, HC, N)
    m.edge = [view(r3 + i * CHUNKS, CHUNKS) for i in range(4)]
    m.dstrow = view(r3 + 4 * CHUNKS, PAIRQ, 2 * CE)
    m.dstrowf = view(r3 + 4 * CHUNKS + 1250, PAIRQ, 2 * CE)
    m.hot = [view(r3 + 4000 + i * 700, 625) for i in range(2)]
    m.hotd = [view(r3 + 5400 + i * 64, 63) for i in range(2)]
    def placed(name, at, n):
        return nc.alloc_sbuf_tensor_at(name, [P, n], F32R, offset=at)

    def matrices(v):
        q = DC * F
        return (v[:, 0:q].rearrange("p (c f) -> p c f", c=DC), v[:, q:2 * q].rearrange("p (c f) -> p c f", c=DC),
                v[:, 2 * q:3 * q].rearrange("p (c d) -> p c d", c=FC))

    m.whi = placed("whi", arena_at, WCOLS)
    m.wlo = placed("wlo", arena_at + 4 * WCOLS, WCOLS)
    m.gate, m.up, m.down = zip(matrices(m.whi), matrices(m.wlo))
    late_at = (nc.sbuf_base + 31) // 32 * 32
    late = sb("late", [P, 11648])
    lat = [ROWLEN]

    def small(*shape, dt=F32):
        n = 1
        for q in shape:
            n *= q
        words = n // (2 if dt == BF16 else 1)
        v = late[:, lat[0]:lat[0] + words]
        lat[0] += words
        if dt != F32:
            v = v.bitcast(dt)
        if len(shape) == 2:
            return v.rearrange("p (a b) -> p a b", a=shape[0])
        if len(shape) == 3:
            return v.rearrange("p (a b c) -> p a b c", a=shape[0], b=shape[1])
        return v

    m.rows = late[:, 0:ROWLEN]
    m.h = sb("h", [P, T, DB])
    m.xg = late[:, 0:1024]
    m.ex = late[:, 1024:1792]
    m.yo = late[:, 1792:2816]
    m.oh = late[:, 2816:3456].bitcast(BF16).rearrange("p (t s) -> p t s", t=T)
    m.raw = [late[:, 3456 + i * PIECE:3456 + (i + 1) * PIECE] for i in range(RAW)]
    part = 3456 + RAW * PIECE
    m.xT = [placed(f"xT{i}", late_at + 4 * (part + i * D), D)[:, :].rearrange("p (c n) -> p c n", c=DC)
            for i in range(2)]
    m.hxT = [placed(f"hxT{i}", late_at + 4 * (part + 2 * D + i * F), F)[:, :].rearrange("p (c n) -> p c n", c=FC)
             for i in range(2)]
    m.cols = sb("cols", [P, COLLEN])
    m.ident = sb("ident", [P, P])
    m.before = sb("before", [P, TP], BF16)
    m.ones = sb("ones", [P, P], BF16)
    m.onesf = sb("onesf", [P, P])
    m.zeros = small(512, dt=BF16)
    m.iota16 = sb("iota16", [P, BMAX * P], I16)
    m.pos = sb("pos", [P, 4])
    m.stats = sb("stats", [P, 12])
    m.mv = small(3, T, 2)
    m.ve = sb("ve", [P, T])
    m.rs = sb("rs", [P, T])
    m.mr = sb("mr", [P, T, 2])
    m.nt = sb("nt", [P, T])
    m.gatew = small(DC, E)
    m.logit = small(T, E)
    m.score = view(0, T, E)
    m.rep = view(T * E, T, E)
    m.top = sb("top", [P, T, TOPK])
    m.sc = sb("sc", [P, 4, T])
    m.mask = small(T, E, dt=BF16)
    m.mprev = small(T + 1, E, dt=BF16)
    hs = m.h[:, :, :].rearrange("p t f -> p (t f)")
    m.place = hs[:, 0:T * E].rearrange("p (t e) -> p t e", t=T)
    m.sel = hs[:, T * E:4 * T * E].bitcast(BF16).rearrange("p (t e k) -> p t e k", t=T, e=E)
    m.cnt = small(8, E)
    m.tabp = sb("tabp", [P, 2, 2], I32)
    m.tab = sb("tab", [1, 2 * TAB], I32)
    m.nbi = sb("nbi", [P, 4, E], I32)
    m.tot = sb("tot", [P, 1], I32)
    m.rng = small(8, 2 * T)
    m.rngh = small(T, 2, PAIRQ)
    m.rngi = small(3, T, dt=I32)
    m.sw = sb("sw", [P, T, 6], BF16)
    m.selc = sb("selc", [P, 6])
    m.wpart = sb("wpart", [P, 1])
    m.meta = sb("meta", [P, 3, 3])
    m.metai = m.meta[:, :, :].bitcast(I32)
    m.idx = sb("idx", [P, 2], I32)
    return m


def build(nc, x, srcT, dstT, dst, cols, rows, w1, w2, wa, wb, wd1, wd2, wqkv, wout, gatew,
          weights, out):
    ctx = ExitStack()
    with ctx:
        m = memory(nc, ctx)
        xn2 = nc.dram_tensor("xn2", [N + PADROWS, D], F32, kind="Internal").ap()
        acc = nc.dram_tensor("acc", [N + PADROWS, D], F32, kind="Internal").ap()
        tabd = nc.dram_tensor("tabd", [2 * P, 2], I32, kind="Internal").ap()
        w = Names()
        w.w1_in, w.w2_in, w.rows_in, w.cols_in, w.gatew_in, w.made = (
            ctx.enter_context(nc.semaphore(n)) for n in ("w1_in", "w2_in", "rows_in", "cols_in", "gatew_in", "made"))
        normalise(nc, m, w, x, cols, rows, w1, w2, gatew)
        encode(nc, m, w)
        attention(nc, m, wqkv)
        adjacency(nc, m, srcT, dstT, dst)
        messages(nc, m, wa, wb)
        combine(nc, m, w, x, wd1, wd2, wout, xn2, acc)
        route(nc, m, tabd)
        experts(nc, m, weights, xn2, acc, out)


def row(m, name, i=0, n=None):
    at, size = ROWS[name]
    n = n or size
    return m.rows[0:TP, at + i * n:at + (i + 1) * n]


def col(m, name, i):
    return m.cols[:, COLS[name][0] + i:COLS[name][0] + i + 1]


def inverse_root(dve, act_ready, act_done, n, var, ve, y, t):
    nc_v = dve
    nc_v.tensor_scalar(ve, var, EPS, None, ALU.add).then_inc(act_ready, 1)
    dve.wait_ge(act_done, n)
    nc_v.reciprocal(y, y)
    dve.drain()
    nc_v.tensor_tensor(t, y, y, ALU.mult)
    dve.drain()
    nc_v.tensor_tensor(t, t, ve, ALU.mult)
    dve.drain()
    nc_v.tensor_scalar(t, t, -0.5, 1.5, ALU.mult, ALU.add)
    dve.drain()
    nc_v.tensor_tensor(y, y, t, ALU.mult)
    dve.drain()


def normalise(nc, m, w, x, cols, rows, w1, w2, gatew):
    with ExitStack() as ctx:
        def sem(name):
            return ctx.enter_context(nc.semaphore(name))
        x_in = [sem("x_in0"), sem("x_in1")]
        var_ready, root_done, xn_ready, xh_ready = sem("var_ready"), sem("root_done"), sem("xn_ready"), sem("xh_ready")
        xn_turned, xh_turned, xn_kept, xh_kept = sem("xn_turned"), sem("xh_turned"), sem("xn_kept"), sem("xh_kept")
        xin, xn, xh = m.row[0:2], m.row[2:4], m.row[4:6]
        block = ctx.enter_context(nc.Block())

        @block.sync
        def _(sp):
            sp.dma_start(m.cols[:], cols).then_inc(w.cols_in, 16)
            sp.dma_start(m.w1, w1.rearrange("(c p) n -> p c n", p=P)).then_inc(w.w1_in, 16)
            sp.dma_start(m.w2, w2.rearrange("(c p) n -> p c n", p=P)).then_inc(w.w2_in, 16)
            sp.dma_start(m.rows[0:TP, :], rows.to_broadcast([TP, ROWLEN])).then_inc(w.rows_in, 16)
            sp.dma_start(m.gatew, gatew.rearrange("p (c e) -> p c e", c=DC)).then_inc(w.gatew_in, 16)

        @block.gpsimd
        def _(pool):
            for t in range(2):
                pool.dma_start(xin[t][0:TP, :], x[t * TP:(t + 1) * TP, :]).then_inc(x_in[t], 16)
            nc.gpsimd.memset(m.ident[:], 0.0)
            nc.gpsimd.memset(m.before[:], 1.0)
            nc.gpsimd.memset(m.ones[:], 1.0)
            nc.gpsimd.memset(m.onesf[:], 1.0)
            nc.gpsimd.memset(m.zeros, 0.0)
            pool.drain()
            nc.gpsimd.affine_select(out=m.ident[:], in_=m.ident[:], compare_op=ALU.not_equal, fill=1.0,
                                    base=0, pattern=[[-1, P]], channel_multiplier=1)
            nc.gpsimd.affine_select(out=m.before[:], in_=m.before[:], compare_op=ALU.is_gt, fill=0.0,
                                    base=0, pattern=[[1, TP]], channel_multiplier=-1)
            nc.gpsimd.iota(m.iota16[:], pattern=[[1, BMAX * P]], base=0, channel_multiplier=0,
                           allow_small_or_imprecise_dtypes=True)
            nc.gpsimd.iota(m.pos[:, 0:1], pattern=[[1, 1]], base=0, channel_multiplier=1,
                           allow_small_or_imprecise_dtypes=True)
            nc.gpsimd.iota(m.pos[:, 1:2], pattern=[[1, 1]], base=P, channel_multiplier=1,
                           allow_small_or_imprecise_dtypes=True)
            nc.gpsimd.iota(m.pos[:, 2:3], pattern=[[1, 1]], base=N, channel_multiplier=1,
                           allow_small_or_imprecise_dtypes=True)
            nc.gpsimd.iota(m.pos[:, 3:4], pattern=[[1, 1]], base=-N, channel_multiplier=-1,
                           allow_small_or_imprecise_dtypes=True).then_inc(w.made, 1)
            for t in range(2, T):
                pool.wait_ge(xn_ready, t - 1)
                pool.dma_start(xin[t % 2][0:TP, :], x[t * TP:(t + 1) * TP, :]).then_inc(x_in[t % 2], 16)

        @block.vector
        def _(dve):
            for t in range(T):
                s = t % 2
                dve.wait_ge(x_in[s], 16 * (t // 2 + 1))
                src = xin[s]
                for which, dest, ready in ((0, xn[s], xn_ready), (1, xh[s], xh_ready)):
                    for i in range(2):
                        nc.vector.bn_stats(m.stats[0:TP, 6 * i:6 * i + 6], src[0:TP, 512 * i:512 * i + 512])
                    dve.drain()
                    nc.vector.bn_aggr(m.mv[0:TP, which, t, :], m.stats[0:TP, :])
                    dve.drain()
                    inverse_root(nc.vector, var_ready, root_done, 2 * t + which + 1, m.mv[0:TP, which, t, 1:2],
                                 m.ve[0:TP, t:t + 1], m.rs[0:TP, t:t + 1], m.nt[0:TP, t:t + 1])
                    if which == 0:
                        nc.vector.tensor_copy(m.mr[0:TP, t, 0:1], m.mv[0:TP, 0, t, 0:1])
                        nc.vector.tensor_copy(m.mr[0:TP, t, 1:2], m.rs[0:TP, t:t + 1])
                    if t >= 2:
                        dve.wait_ge(xn_turned if which == 0 else xh_turned, t - 1)
                    nc.vector.tensor_scalar(dest[0:TP, :], src[0:TP, :], m.mv[0:TP, which, t, 0:1],
                                            m.rs[0:TP, t:t + 1], ALU.subtract, ALU.mult).then_inc(ready, 1)
                    dve.drain()
                    src = dest

        @block.tensor
        def _(pe):
            pe.wait_ge(w.made, 1)
            for t in range(T):
                for src, ready, kept, turned, b0 in ((xn[t % 2], xn_ready, xn_kept, xn_turned, 0),
                                                     (xh[t % 2], xh_ready, xh_kept, xh_turned, 2)):
                    pe.wait_ge(ready, t + 1)
                    if t:
                        pe.wait_ge(kept, t)
                    for c in range(DC):
                        mm = nc.tensor.transpose(m.ps[:, b0 + c // 4, (c % 4) * TP:(c % 4 + 1) * TP],
                                                 src[0:TP, c * P:(c + 1) * P], m.ident[0:TP, 0:TP])
                    mm.then_inc(turned, 1)

        @block.scalar
        def _(act):
            act.wait_ge(w.cols_in, 16)
            for t in range(T):
                act.wait_ge(var_ready, 2 * t + 1)
                nc.scalar.activation(m.rs[0:TP, t:t + 1], m.ve[0:TP, t:t + 1], ACT.Sqrt).then_inc(root_done, 1)
                act.wait_ge(var_ready, 2 * t + 2)
                nc.scalar.activation(m.rs[0:TP, t:t + 1], m.ve[0:TP, t:t + 1], ACT.Sqrt).then_inc(root_done, 1)
                act.wait_ge(xn_turned, t + 1)
                for i in range(2):
                    a = nc.scalar.activation(m.xnT[:, 4 * i:4 * i + 4, t * TP:(t + 1) * TP],
                                             m.ps[:, i, 0:4 * TP].rearrange("p (c n) -> p c n", c=4), ACT.Copy)
                a.then_inc(xn_kept, 1)
                act.wait_ge(xh_turned, t + 1)
                for c in range(DC):
                    a = nc.scalar.activation(m.h0T[:, c, t * TP:(t + 1) * TP],
                                             m.ps[:, 2 + c // 4, (c % 4) * TP:(c % 4 + 1) * TP],
                                             ACT.Identity, bias=col(m, "b", c), scale=col(m, "g", c))
                a.then_inc(xh_kept, 1)


def encode(nc, m, w):
    with ExitStack() as ctx:
        def sem(name):
            return ctx.enter_context(nc.semaphore(name))
        h1_done, h1_kept, h_done, h_kept = sem("h1_done"), sem("h1_kept"), sem("h_done"), sem("h_kept")
        groups = [(hb, s) for hb in range(HC) for s in range(len(SPANS))]
        block = ctx.enter_context(nc.Block())

        @block.tensor
        def _(pe):
            pe.wait_ge(w.w1_in, 16)
            for g, (hb, s) in enumerate(groups):
                at, n = SPANS[s]
                if g >= 4:
                    pe.wait_ge(h1_kept, g - 3)
                for c in range(DC):
                    mm = nc.tensor.matmul(m.ps[:, g % 4, 0:n], m.w1[:, c, hb * P:(hb + 1) * P],
                                          m.h0T[:, c, at:at + n], start=(c == 0), stop=(c == DC - 1))
                mm.then_inc(h1_done, 1)
            pe.wait_ge(w.w2_in, 16)
            pe.wait_ge(h1_kept, len(groups))
            for t in range(T):
                if t >= 4:
                    pe.wait_ge(h_kept, t - 3)
                for c in range(HC):
                    mm = nc.tensor.matmul(m.ps[0:TP, 4 + t % 4, 0:DB], m.h1T[:, c, t * TP:(t + 1) * TP],
                                          m.w2[:, c, :], start=(c == 0), stop=(c == HC - 1))
                mm.then_inc(h_done, 1)

        @block.scalar
        def _(act):
            for g, (hb, s) in enumerate(groups):
                at, n = SPANS[s]
                act.wait_ge(h1_done, g + 1)
                nc.scalar.activation(m.h1T[:, hb, at:at + n], m.ps[:, g % 4, 0:n], ACT.Relu,
                                     bias=col(m, "b1", hb)).then_inc(h1_kept, 1)

        @block.vector
        def _(dve):
            dve.wait_ge(w.rows_in, 16)
            for t in range(T):
                dve.wait_ge(h_done, t + 1)
                nc.vector.tensor_tensor(m.h[0:TP, t, :], m.ps[0:TP, 4 + t % 4, 0:DB], row(m, "b2"),
                                        ALU.add).then_inc(h_kept, 1)


def attention(nc, m, wqkv):
    QU = D // UNIT
    order = list(range(QU)) + [v for i in range(QU) for v in (QU + i, 2 * QU + i)]
    NS = len(SPANS)
    q_groups = [(u, cb, s) for u in range(QU) for cb in range(UNIT // P) for s in range(NS)]
    G = len(q_groups)
    BANKS = 6
    steps = [(i, t) for i in range(QU) for t in range(T)]

    with ExitStack() as ctx:
        def sem(name):
            return ctx.enter_context(nc.semaphore(name))
        unit_in = [sem(f"unit_in{s}") for s in range(4)]
        unit_used, proj_done, cut, exped = sem("unit_used"), sem("proj_done"), sem("cut"), sem("exped")
        q_kept, k_kept, v_kept = sem("q_kept"), sem("k_kept"), sem("v_kept")
        kv_step, kv_kept, cleared = sem("kv_step"), sem("kv_kept"), sem("cleared")
        nd_done, nd_kept = sem("nd_done"), sem("nd_kept")
        block = ctx.enter_context(nc.Block())

        @block.sync
        def _(sp):
            for n, u in enumerate(order):
                if n >= 4:
                    sp.wait_ge(unit_used, n - 3 if n - 4 < QU else (n - 4 - QU) // 2 * 2 + 2 + QU)
                sp.dma_start(m.unit[n % 4], wqkv[:, u * UNIT:(u + 1) * UNIT].rearrange("(c p) n -> p c n", p=P)
                             ).then_inc(unit_in[n % 4], 16)

        @block.tensor
        def _(pe):
            for g, (u, cb, s) in enumerate(q_groups):
                at, n = SPANS[s]
                pe.wait_ge(unit_in[u % 4], 16)
                if g >= BANKS:
                    pe.wait_ge(q_kept, g - BANKS + 1)
                for c in range(DC):
                    mm = nc.tensor.matmul(m.ps[:, g % BANKS, 0:n], m.unit[u % 4][:, c, cb * P:(cb + 1) * P],
                                          m.xnT[:, c, at:at + n], start=(c == 0), stop=(c == DC - 1))
                mm.then_inc(proj_done, 1)
                if cb == UNIT // P - 1 and s == NS - 1:
                    pe.drain().then_inc(unit_used, 1)

            def accumulate(n):
                i, t = steps[n]
                pe.wait_ge(k_kept, n + 1)
                pe.wait_ge(v_kept, n + 1)
                if t == 0 and i >= 2:
                    pe.wait_ge(kv_kept, i - 1)
                bank = 6 + i % 2
                for pr in range(2):
                    nc.tensor.matmul(m.ps[:, bank, pr * P:(pr + 1) * P], m.kt[n % 2][0:TP, pr * P:(pr + 1) * P],
                                     m.vt[n % 2][0:TP, pr * P:(pr + 1) * P],
                                     start=(t == 0 and pr == 0), stop=(t == T - 1), skip_group_check=True)
                    mm = nc.tensor.matmul(m.ps[:, bank, 2 * P + pr:2 * P + pr + 1],
                                          m.kt[n % 2][0:TP, pr * P:(pr + 1) * P], m.onesf[0:TP, 0:1],
                                          start=False, stop=(t == T - 1), skip_group_check=True)
                mm.then_inc(kv_step, 1)

            for n, (i, t) in enumerate(steps):
                slots = [(QU + 2 * i) % 4, (QU + 2 * i + 1) % 4]
                for j in range(2):
                    g = G + 2 * n + j
                    if t == 0:
                        pe.wait_ge(unit_in[slots[j]], 16 * ((QU + 2 * i + j) // 4 + 1))
                    if g - BANKS < G:
                        pe.wait_ge(q_kept, g - BANKS + 1)
                    else:
                        pe.wait_ge((k_kept, v_kept)[j], (g - BANKS - G) // 2 + 1)
                    for c in range(DC):
                        mm = nc.tensor.matmul(m.ps[0:TP, g % BANKS, 0:UNIT], m.xnT[:, c, t * TP:(t + 1) * TP],
                                              m.unit[slots[j]][:, c, :], start=(c == 0), stop=(c == DC - 1))
                    mm.then_inc(proj_done, 1)
                if t == T - 1:
                    pe.drain().then_inc(unit_used, 2)
                if n:
                    accumulate(n - 1)
            accumulate(len(steps) - 1)
            pe.wait_ge(kv_kept, QU)
            pe.wait_ge(q_kept, G)
            pe.wait_ge(v_kept, len(steps))
            for g in range(PAIRS * NS):
                pr, s = divmod(g, NS)
                at, n = SPANS[s]
                if g >= 3:
                    pe.wait_ge(nd_kept, g - 2)
                b = 2 * (g % 3)
                nc.tensor.matmul(m.ps[:, b, 0:n], m.kvm[:, pr, :], m.qT[:, pr, at:at + n], start=True, stop=True)
                nc.tensor.matmul(m.ps[:, b + 1, 0:n], m.zm[:, pr, :], m.qT[:, pr, at:at + n],
                                 start=True, stop=True).then_inc(nd_done, 1)

        @block.scalar
        def _(act):
            for g, (u, cb, s) in enumerate(q_groups):
                n = SPANS[s][1]
                act.wait_ge(cut, g + 1)
                nc.scalar.activation(m.tmp[g % 2][:, 0:n], m.tmp[g % 2][:, 0:n], ACT.Exp).then_inc(exped, 1)
            for n, (i, t) in enumerate(steps):
                act.wait_ge(cut, G + n + 1)
                nc.scalar.activation(m.tmp[n % 2][0:TP, 0:UNIT], m.tmp[n % 2][0:TP, 0:UNIT],
                                     ACT.Exp).then_inc(exped, 1)
                act.wait_ge(proj_done, G + 2 * n + 2)
                if n >= 2:
                    act.wait_ge(kv_step, n - 1)
                nc.scalar.activation(m.vt[n % 2][0:TP, :], m.ps[0:TP, (G + 2 * n + 1) % BANKS, 0:UNIT],
                                     ACT.Copy).then_inc(v_kept, 1)

        @block.vector
        def _(dve):
            nc.vector.memset(m.kvm, 0.0)
            nc.vector.memset(m.zm, 0.0)
            dve.drain()

            def finish_q(g):
                u, cb, s = q_groups[g]
                at, n = SPANS[s]
                dve.wait_ge(exped, g + 1)
                nc.vector.scalar_tensor_tensor(m.qT[:, 2 * u + cb, at:at + n], m.ps[:, g % BANKS, 0:n], 0.0,
                                               m.tmp[g % 2][:, 0:n], ALU.max, ALU.add).then_inc(q_kept, 1)

            for g, (u, cb, s) in enumerate(q_groups):
                n = SPANS[s][1]
                dve.wait_ge(proj_done, g + 1)
                if g >= 2:
                    dve.drain()
                nc.vector.tensor_scalar(m.tmp[g % 2][:, 0:n], m.ps[:, g % BANKS, 0:n], 0.0, None,
                                        ALU.min).then_inc(cut, 1)
                if g:
                    finish_q(g - 1)
            finish_q(G - 1)
            dve.drain()

            def finish_k(n):
                dve.wait_ge(exped, G + n + 1)
                if n >= 2:
                    dve.wait_ge(kv_step, n - 1)
                nc.vector.scalar_tensor_tensor(m.kt[n % 2][0:TP, :], m.ps[0:TP, (G + 2 * n) % BANKS, 0:UNIT], 0.0,
                                               m.tmp[n % 2][0:TP, 0:UNIT], ALU.max, ALU.add).then_inc(k_kept, 1)
                i, t = steps[n]
                if t == T - 1:
                    dve.wait_ge(kv_step, n + 1)
                    bank = 6 + i % 2
                    for pr in range(2):
                        for hd in range(2):
                            a, b = hd * DH, (hd + 1) * DH
                            nc.vector.tensor_copy(m.kvm[a:b, 2 * i + pr, a:b],
                                                  m.ps[a:b, bank, pr * P + a:pr * P + b])
                            v = nc.vector.tensor_scalar(m.zm[a:b, 2 * i + pr, a:b], m.onesf[a:b, 0:DH],
                                                        m.ps[a:b, bank, 2 * P + pr:2 * P + pr + 1], None, ALU.mult)
                    v.then_inc(kv_kept, 1)

            for n, (i, t) in enumerate(steps):
                dve.wait_ge(proj_done, G + 2 * n + 1)
                dve.drain()
                nc.vector.tensor_scalar(m.tmp[n % 2][0:TP, 0:UNIT], m.ps[0:TP, (G + 2 * n) % BANKS, 0:UNIT],
                                        0.0, None, ALU.min).then_inc(cut, 1)
                if n:
                    finish_k(n - 1)
            finish_k(len(steps) - 1)
            for g in range(PAIRS * NS):
                pr, s = divmod(g, NS)
                at, n = SPANS[s]
                b = 2 * (g % 3)
                tmp = m.tmp[g % 2][:, 0:n]
                dve.wait_ge(nd_done, g + 1)
                dve.drain()
                nc.vector.tensor_scalar(tmp, m.ps[:, b + 1, 0:n], 1e-6, None, ALU.add)
                dve.drain()
                nc.vector.reciprocal(tmp, tmp)
                dve.drain()
                nc.vector.tensor_tensor(m.qT[:, pr, at:at + n], m.ps[:, b, 0:n], tmp, ALU.mult).then_inc(nd_kept, 1)


def adjacency(nc, m, srcT, dstT, dst):
    with ExitStack() as ctx:
        def sem(name):
            return ctx.enter_context(nc.semaphore(name))
        e_in, row_in, found, ranged = sem("e_in"), sem("row_in"), sem("found"), sem("ranged")
        bounds, hot_ready, hot_free = sem("bounds"), sem("hot_ready"), sem("hot_free")
        tile_done, tile_kept, zeroed = sem("tile_done"), sem("tile_kept"), sem("zeroed")
        esrc, edst, srcf, dstf = m.edge
        hots = [v[:, :].bitcast(BF16)[0:TP, 0:N] for v in m.hot]
        hotd = [v[:, :].bitcast(BF16)[0:TP, 0:TP] for v in m.hotd]
        banks = ((0, 4), (4, 4), (8, 2))
        block = ctx.enter_context(nc.Block())

        @block.sync
        def _(sp):
            sp.dma_start(m.dstrow[0:EP, :, :].bitcast(I32),
                         dst.rearrange("(p q e) -> p q e", p=EP, q=PAIRQ)).then_inc(row_in, 16)
            sp.dma_start(esrc[0:CE, :].bitcast(I32), srcT).then_inc(e_in, 16)
            sp.dma_start(edst[0:CE, :].bitcast(I32), dstT).then_inc(e_in, 16)

        @block.gpsimd
        def _(pool):
            nc.gpsimd.iota(m.rng[0:EP, 6, 0:PAIRQ], pattern=[[1, PAIRQ]], base=1, channel_multiplier=PAIRQ,
                           allow_small_or_imprecise_dtypes=True)
            nc.gpsimd.iota(m.rng[0:EP, 7, 0:PAIRQ], pattern=[[-1, PAIRQ]], base=NPAIR, channel_multiplier=-PAIRQ,
                           allow_small_or_imprecise_dtypes=True).then_inc(found, 1)
            pool.wait_ge(found, 2)
            nc.gpsimd.partition_all_reduce(m.rng[0:EP, 3, :], m.rng[0:EP, 2, :], EP, RMAX).then_inc(ranged, 1)

        @block.vector
        def _(dve):
            dve.wait_ge(row_in, 16)
            nc.vector.tensor_copy(m.dstrowf[0:EP, :, :], m.dstrow[0:EP, :, :].bitcast(I32))
            dve.drain()
            lo, hi = m.rng[0:EP, 0, 0:PAIRQ], m.rng[0:EP, 1, 0:PAIRQ]
            nc.vector.tensor_reduce(lo, m.dstrowf[0:EP, :, :], AX, ALU.min)
            nc.vector.tensor_reduce(hi, m.dstrowf[0:EP, :, :], AX, ALU.max)
            dve.drain()
            for t in range(T):
                nc.vector.tensor_scalar(m.rngh[0:EP, t, 0, :], hi, float(t * TP), None, ALU.is_ge)
            dve.drain()
            for t in range(T):
                nc.vector.scalar_tensor_tensor(m.rngh[0:EP, t, 1, :], lo, float(t * TP + TP - 1),
                                               m.rngh[0:EP, t, 0, :], ALU.is_le, ALU.mult)
            dve.drain()
            dve.wait_ge(found, 1)
            for t in range(T):
                nc.vector.tensor_tensor(m.rngh[0:EP, t, 0, :], m.rngh[0:EP, t, 1, :], m.rng[0:EP, 6, 0:PAIRQ],
                                        ALU.mult)
            dve.drain()
            nc.vector.tensor_reduce(m.rng[0:EP, 2, 0:T], m.rngh[0:EP, :, 0, :], AX, ALU.max)
            for t in range(T):
                nc.vector.tensor_tensor(m.rngh[0:EP, t, 1, :], m.rngh[0:EP, t, 1, :], m.rng[0:EP, 7, 0:PAIRQ],
                                        ALU.mult)
            dve.drain()
            nc.vector.tensor_reduce(m.rng[0:EP, 2, T:2 * T], m.rngh[0:EP, :, 1, :], AX,
                                    ALU.max).then_inc(found, 1)
            dve.wait_ge(ranged, 1)
            end, low = m.rng[0:EP, 3, 0:T], m.rng[0:EP, 3, T:2 * T]
            first, last, count = m.rng[0:EP, 4, 0:T], m.rng[0:EP, 4, T:2 * T], m.rng[0:EP, 5, 0:T]
            nc.vector.tensor_scalar(first, low, -1.0, float(NPAIR), ALU.mult, ALU.add)
            dve.drain()
            nc.vector.tensor_scalar(first, first, float(NPAIR - 1), None, ALU.min)
            dve.drain()
            nc.vector.tensor_tensor(count, end, first, ALU.subtract)
            dve.drain()
            nc.vector.tensor_scalar(count, count, 1.0, None, ALU.max)
            nc.vector.tensor_copy(m.rngi[0:EP, 0, :], first)
            dve.drain()
            nc.vector.tensor_copy(m.rngi[0:EP, 1, :], count)
            nc.vector.tensor_tensor_scan(last, m.onesf[0:EP, 0:T], count, 0.0, ALU.mult, ALU.add)
            dve.drain()
            nc.vector.tensor_tensor(last, last, count, ALU.subtract)
            dve.drain()
            nc.vector.tensor_copy(m.rngi[0:EP, 2, :], last).then_inc(bounds, 1)
            dve.drain()
            dve.wait_ge(e_in, 32)
            nc.vector.tensor_copy(srcf[0:CE, :], esrc[0:CE, :].bitcast(I32))
            nc.vector.tensor_copy(dstf[0:CE, :], edst[0:CE, :].bitcast(I32))
            dve.drain()
            with dve.Fori(0, T) as t:
                first_pair = dve.value_load(m.rngi[0:1, 0, bass.ds(t, 1)], min_val=0, max_val=NPAIR - 1)
                pairs = dve.value_load(m.rngi[0:1, 1, bass.ds(t, 1)], min_val=1, max_val=NPAIR)
                before = dve.value_load(m.rngi[0:1, 2, bass.ds(t, 1)], min_val=0, max_val=(T - 1) * NPAIR)
                with dve.Fori(0, pairs) as j:
                    pair = dve.snap(nc.s_assert_within(
                        first_pair + j, 0, NPAIR - 1,
                        skip_runtime_bounds_check_because="the count ends at the last pair"))
                    done = dve.snap(before + j)
                    for s in range(2):
                        c = pair * 2 + s
                        dve.wait_ge(hot_free, done * 2 + s + 1)
                        nc.vector.tensor_scalar(hots[s], m.iota16[0:CE, 0:N], srcf[0:CE, bass.ds(c, 1)], None,
                                                ALU.is_equal)
                        nc.vector.tensor_scalar(hotd[s], m.iota16[0:CE, bass.ds(t * TP, TP)],
                                                dstf[0:CE, bass.ds(c, 1)], None, ALU.is_equal).then_inc(hot_ready, 1)

        @block.tensor
        def _(pe):
            pe.wait_ge(bounds, 1)
            pe.drain().then_inc(hot_free, 2)
            pe.drain().then_inc(tile_kept, 2)
            with pe.Fori(0, T // 2) as t2:
                for odd in range(2):
                    t = t2 * 2 + odd
                    pairs = pe.value_load(m.rngi[0:1, 1, bass.ds(t, 1)], min_val=1, max_val=NPAIR)
                    before = pe.value_load(m.rngi[0:1, 2, bass.ds(t, 1)], min_val=0, max_val=(T - 1) * NPAIR)
                    pe.wait_ge(tile_kept, t2 * 2 + odd + 1)
                    for b, (s0, n) in enumerate(banks):
                        nc.tensor.matmul(m.ps[0:TP, 3 * odd + b, 0:n * TP], m.zeros[0:CE, 0:TP],
                                         m.zeros[0:CE, 0:n * TP], start=True, stop=False, skip_group_check=True)
                    with pe.Fori(0, pairs) as j:
                        done = pe.snap(before + j)
                        for s in range(2):
                            pe.wait_ge(hot_ready, done * 2 + s + 1)
                            for b, (s0, n) in enumerate(banks):
                                for i in range(n):
                                    mm = nc.tensor.matmul(m.ps[0:TP, 3 * odd + b, i * TP:(i + 1) * TP],
                                                          hots[s][:, (s0 + i) * TP:(s0 + i + 1) * TP], hotd[s],
                                                          start=False, stop=False, skip_group_check=True)
                            mm.then_inc(hot_free, 1)
                    for b, (s0, n) in enumerate(banks):
                        mm = nc.tensor.matmul(m.ps[0:TP, 3 * odd + b, 0:n * TP], m.zeros[0:CE, 0:TP],
                                              m.zeros[0:CE, 0:n * TP], start=False, stop=True,
                                              skip_group_check=True)
                    mm.then_inc(tile_done, 1)

        @block.scalar
        def _(act):
            with act.Fori(0, T // 2) as t2:
                for odd in range(2):
                    act.wait_ge(tile_done, t2 * 2 + odd + 1)
                    for b, (s0, n) in enumerate(banks):
                        a = nc.scalar.activation(m.adjT[0:TP, s0:s0 + n, bass.ds((t2 * 2 + odd) * TP, TP)],
                                                 m.ps[0:TP, 3 * odd + b, 0:n * TP].rearrange("p (s d) -> p s d", s=n),
                                                 ACT.Copy)
                    a.then_inc(tile_kept, 1)

    with ExitStack() as ctx:
        block = ctx.enter_context(nc.Block())

        @block.vector
        def _(dve):
            for s in range(T):
                d = m.adjT[0:TP, s, s * TP:(s + 1) * TP]
                nc.vector.tensor_tensor(d, d, m.ident[0:TP, 0:TP], ALU.add)


def messages(nc, m, wa, wb):
    NS = len(SPANS)
    with ExitStack() as ctx:
        def sem(name):
            return ctx.enter_context(nc.semaphore(name))
        w_in, mm_done, kept, zz_done, zz_kept = sem("w_in"), sem("mm_done"), sem("kept"), sem("zz_done"), sem("zz_kept")
        var_ready, root_done, h_ready = sem("mvar_ready"), sem("mroot_done"), sem("h_ready")
        groups = [(f, s) for f in range(BC) for s in range(NS)]
        G = len(groups)
        block = ctx.enter_context(nc.Block())

        @block.sync
        def _(sp):
            sp.dma_start(m.wab[:, 0:LAYERS * BC, :], wa.rearrange("l (c p) n -> p (l c) n", p=P)).then_inc(w_in, 16)
            sp.dma_start(m.wab[:, LAYERS * BC:, :], wb.rearrange("l (c p) n -> p (l c) n", p=P)).then_inc(w_in, 16)

        @block.tensor
        def _(pe):
            pe.wait_ge(w_in, 32)
            for i in range(LAYERS):
                if i:
                    pe.wait_ge(h_ready, i)
                for g, (f, s) in enumerate(groups):
                    at, n = SPANS[s]
                    k = 2 * G * i + g
                    if k >= 4:
                        pe.wait_ge(kept, k - 3)
                    for c in range(T):
                        mm = nc.tensor.matmul(m.ps[:, k % 4, 0:n], m.h[0:TP, c, f * P:(f + 1) * P],
                                              m.adjT[0:TP, c, at:at + n], start=(c == 0), stop=(c == T - 1))
                    mm.then_inc(mm_done, 1)
                for g, (f, s) in enumerate(groups):
                    at, n = SPANS[s]
                    k = 2 * G * i + G + g
                    pe.wait_ge(kept, max(k - 3, 2 * G * i + G))
                    for c in range(BC):
                        mm = nc.tensor.matmul(m.ps[:, k % 4, 0:n], m.wab[:, i * BC + c, f * P:(f + 1) * P],
                                              m.zT[:, c, at:at + n], start=(c == 0), stop=(c == BC - 1))
                    mm.then_inc(mm_done, 1)
                pe.wait_ge(kept, 2 * G * (i + 1))
                for t in range(T):
                    k = T * i + t
                    if k >= 4:
                        pe.wait_ge(zz_kept, k - 3)
                    for c in range(BC):
                        mm = nc.tensor.matmul(m.ps[0:TP, 4 + k % 4, 0:DB], m.aT[:, c, t * TP:(t + 1) * TP],
                                              m.wab[:, (LAYERS + i) * BC + c, :], start=(c == 0), stop=(c == BC - 1))
                    mm.then_inc(zz_done, 1)

        @block.scalar
        def _(act):
            for i in range(LAYERS):
                for g, (f, s) in enumerate(groups):
                    at, n = SPANS[s]
                    k = 2 * G * i + g
                    act.wait_ge(mm_done, k + 1)
                    nc.scalar.activation(m.zT[:, f, at:at + n], m.ps[:, k % 4, 0:n], ACT.Copy).then_inc(kept, 1)
                for g, (f, s) in enumerate(groups):
                    at, n = SPANS[s]
                    k = 2 * G * i + G + g
                    act.wait_ge(mm_done, k + 1)
                    nc.scalar.activation(m.aT[:, f, at:at + n], m.ps[:, k % 4, 0:n], ACT.Relu,
                                         bias=col(m, "ba", i * BC + f)).then_inc(kept, 1)
                act.wait_ge(var_ready, i + 1)
                nc.scalar.activation(m.rs[0:TP, :], m.ve[0:TP, :], ACT.Sqrt).then_inc(root_done, 1)

        @block.vector
        def _(dve):
            for i in range(LAYERS):
                for t in range(T):
                    k = T * i + t
                    dve.wait_ge(zz_done, k + 1)
                    nc.vector.tensor_tensor(m.zz[0:TP, t, :], m.ps[0:TP, 4 + k % 4, 0:DB], row(m, "bb", i, DB),
                                            ALU.add).then_inc(zz_kept, 1)
                    dve.drain()
                    nc.vector.bn_stats(m.stats[0:TP, 0:6], m.zz[0:TP, t, :])
                    dve.drain()
                    nc.vector.bn_aggr(m.mv[0:TP, 2, t, :], m.stats[0:TP, 0:6])
                dve.drain()
                inverse_root(nc.vector, var_ready, root_done, i + 1, m.mv[0:TP, 2, :, 1], m.ve[0:TP, :],
                             m.rs[0:TP, :], m.nt[0:TP, :])
                for t in range(T):
                    nc.vector.tensor_scalar(m.zz[0:TP, t, :], m.zz[0:TP, t, :], m.mv[0:TP, 2, t, 0:1],
                                            m.rs[0:TP, t:t + 1], ALU.subtract, ALU.mult)
                dve.drain()
                z = m.zz[0:TP, :, :]
                nc.vector.tensor_tensor(z, z, row(m, "ng", i, DB).unsqueeze(1).to_broadcast([TP, T, DB]), ALU.mult)
                dve.drain()
                nc.vector.tensor_tensor(z, z, row(m, "nb", i, DB).unsqueeze(1).to_broadcast([TP, T, DB]), ALU.add)
                dve.drain()
                nc.vector.scalar_tensor_tensor(m.h[0:TP, :, :], z, 0.0, m.h[0:TP, :, :], ALU.max,
                                               ALU.add).then_inc(h_ready, 1)
                dve.drain()


def combine(nc, m, w, x, wd1, wd2, wout, xn2, acc):
    NS = len(SPANS)
    groups = [(f, s) for f in range(HC) for s in range(NS)]
    with ExitStack() as ctx:
        def sem(name):
            return ctx.enter_context(nc.semaphore(name))
        wd1_in, wbig_in, h_turned, h_kept, d_done, d_kept = (sem(n) for n in (
            "wd1_in", "wbig_in", "h_turned", "hT_kept", "d_done", "d_kept"))
        x_in, delta_done, mix_done, delta_used, mix_used = (sem(n) for n in (
            "cx_in", "delta_done", "mix_done", "delta_used", "mix_used"))
        var_ready, root_done, x1_ready, xn_ready, stored, xn_stored = (sem(n) for n in (
            "cvar_ready", "croot_done", "x1_ready", "xn2_ready", "stored", "xn_stored"))
        turned, kept, logit_done, logit_kept, pads = (sem(n) for n in (
            "cturned", "ckept", "logit_done", "logit_kept", "pads"))
        xt, u, mx, xo = m.tile
        xT = m.h[:, 0:DC // 2, :].rearrange("p a b -> p (a b)")[:, 0:DC * TP].rearrange("p (c n) -> p c n", c=DC)
        block = ctx.enter_context(nc.Block())

        @block.sync
        def _(sp):
            sp.dma_start(m.wd1, wd1.rearrange("(c p) n -> p c n", p=P)).then_inc(wd1_in, 16)
            sp.dma_start(m.wd2, wd2.rearrange("(c p) n -> p c n", p=P)).then_inc(wbig_in, 16)
            sp.dma_start(m.wout, wout.rearrange("(c p) n -> p c n", p=P)).then_inc(wbig_in, 16)
            sp.wait_ge(pads, 1)
            sp.dma_start(xn2[N:N + PADROWS, 0:512], m.zeros.bitcast(F32).unsqueeze(1).to_broadcast([P, 2, 256])
                         ).then_inc(stored, 16)
            sp.dma_start(xn2[N:N + PADROWS, 512:1024], m.zeros.bitcast(F32).unsqueeze(1).to_broadcast([P, 2, 256])
                         ).then_inc(stored, 16)
            sp.dma_start(acc[N:N + PADROWS, 0:512], m.zeros.bitcast(F32).unsqueeze(1).to_broadcast([P, 2, 256])
                         ).then_inc(stored, 16)
            sp.dma_start(acc[N:N + PADROWS, 512:1024], m.zeros.bitcast(F32).unsqueeze(1).to_broadcast([P, 2, 256])
                         ).then_inc(stored, 16)
            for t in range(T):
                sp.wait_ge(x1_ready, t + 1)
                sp.dma_start(acc[t * TP:(t + 1) * TP, :], mx[0:TP, :]).then_inc(stored, 16)
                sp.wait_ge(xn_ready, t + 1)
                sp.dma_start(xn2[t * TP:(t + 1) * TP, :], xo[0:TP, :]).then_inc(xn_stored, 16)
            sp.wait_ge(stored, 16 * (T + 4))
            sp.wait_ge(xn_stored, 16 * T)

        @block.gpsimd
        def _(pool):
            pool.drain().then_inc(pads, 1)
            for t in range(T):
                if t:
                    pool.wait_ge(x1_ready, t)
                pool.dma_start(xt[0:TP, :], x[t * TP:(t + 1) * TP, :]).then_inc(x_in, 16)

        @block.tensor
        def _(pe):
            for t in range(T):
                if t >= 4:
                    pe.wait_ge(h_kept, t - 3)
                for f in range(BC):
                    mm = nc.tensor.transpose(m.ps[:, t % 4, f * TP:(f + 1) * TP], m.h[0:TP, t, f * P:(f + 1) * P],
                                             m.ident[0:TP, 0:TP])
                mm.then_inc(h_turned, 1)
            pe.wait_ge(h_kept, T)
            pe.wait_ge(wd1_in, 16)
            for g, (f, s) in enumerate(groups):
                at, n = SPANS[s]
                if g >= 4:
                    pe.wait_ge(d_kept, g - 3)
                for c in range(BC):
                    mm = nc.tensor.matmul(m.ps[:, g % 4, 0:n], m.wd1[:, c, f * P:(f + 1) * P],
                                          m.hT[:, c, at:at + n], start=(c == 0), stop=(c == BC - 1))
                mm.then_inc(d_done, 1)
            pe.wait_ge(d_kept, len(groups))
            pe.wait_ge(wbig_in, 32)

            def router(t):
                pe.wait_ge(xn_ready, t + 1)
                if t:
                    pe.wait_ge(kept, t)
                for c in range(DC):
                    mm = nc.tensor.transpose(m.ps[:, 4 + c // 4, (c % 4) * TP:(c % 4 + 1) * TP],
                                             xo[0:TP, c * P:(c + 1) * P], m.ident[0:TP, 0:TP])
                mm.then_inc(turned, 1)
                pe.wait_ge(kept, t + 1)
                if t:
                    pe.wait_ge(logit_kept, t)
                for c in range(DC):
                    mm = nc.tensor.matmul(m.ps[0:TP, 6, 0:E], xT[:, c, :], m.gatew[:, c, :],
                                          start=(c == 0), stop=(c == DC - 1))
                mm.then_inc(logit_done, 1)

            pe.wait_ge(w.gatew_in, 16)
            for t in range(T):
                if t:
                    pe.wait_ge(delta_used, t)
                for half in range(2):
                    for c in range(HC):
                        mm = nc.tensor.matmul(m.ps[0:TP, half, :], m.dT[:, c, t * TP:(t + 1) * TP],
                                              m.wd2[:, c, half * 512:half * 512 + 512],
                                              start=(c == 0), stop=(c == HC - 1))
                mm.then_inc(delta_done, 1)
                if t:
                    pe.wait_ge(mix_used, t)
                for half in range(2):
                    for c in range(DC):
                        mm = nc.tensor.matmul(m.ps[0:TP, 2 + half, :], m.qT[:, c, t * TP:(t + 1) * TP],
                                              m.wout[:, c, half * 512:half * 512 + 512],
                                              start=(c == 0), stop=(c == DC - 1))
                mm.then_inc(mix_done, 1)
                if t:
                    router(t - 1)
            router(T - 1)

        @block.scalar
        def _(act):
            for t in range(T):
                act.wait_ge(h_turned, t + 1)
                nc.scalar.activation(m.hT[:, :, t * TP:(t + 1) * TP],
                                     m.ps[:, t % 4, 0:BC * TP].rearrange("p (f n) -> p f n", f=BC),
                                     ACT.Copy).then_inc(h_kept, 1)
            for g, (f, s) in enumerate(groups):
                at, n = SPANS[s]
                act.wait_ge(d_done, g + 1)
                nc.scalar.activation(m.dT[:, f, at:at + n], m.ps[:, g % 4, 0:n], ACT.Relu,
                                     bias=col(m, "bd1", f)).then_inc(d_kept, 1)
            for t in range(T):
                for i in range(2):
                    act.wait_ge(var_ready, 2 * t + i + 1)
                    nc.scalar.activation(m.rs[0:TP, t:t + 1], m.ve[0:TP, t:t + 1], ACT.Sqrt).then_inc(root_done, 1)
                act.wait_ge(turned, t + 1)
                if t:
                    act.wait_ge(logit_done, t)
                for i in range(2):
                    a = nc.scalar.activation(xT[:, 4 * i:4 * i + 4, :],
                                             m.ps[:, 4 + i, 0:4 * TP].rearrange("p (c n) -> p c n", c=4), ACT.Copy)
                a.then_inc(kept, 1)
                act.wait_ge(logit_done, t + 1)
                nc.scalar.activation(m.logit[0:TP, t, :], m.ps[0:TP, 6, 0:E], ACT.Copy).then_inc(logit_kept, 1)

        @block.vector
        def _(dve):
            for t in range(T):
                dve.wait_ge(x_in, 16 * (t + 1))
                xt_, u_, mx_, xo_ = (v[0:TP, :] for v in (xt, u, mx, xo))
                nc.vector.tensor_scalar(u_, xt_, m.mr[0:TP, t, 0:1], m.mr[0:TP, t, 1:2], ALU.subtract, ALU.mult)
                dve.drain()
                nc.vector.tensor_tensor(u_, u_, row(m, "bd2"), ALU.add)
                dve.drain()
                dve.wait_ge(delta_done, t + 1)
                nc.vector.tensor_tensor(u_, m.ps[0:TP, 0:2, :].rearrange("p a b -> p (a b)"), u_,
                                        ALU.add).then_inc(delta_used, 1)
                dve.drain()
                for i in range(2):
                    nc.vector.bn_stats(m.stats[0:TP, 6 * i:6 * i + 6], u_[:, 512 * i:512 * i + 512])
                dve.drain()
                nc.vector.bn_aggr(m.mv[0:TP, 0, t, :], m.stats[0:TP, :])
                dve.drain()
                inverse_root(nc.vector, var_ready, root_done, 2 * t + 1, m.mv[0:TP, 0, t, 1:2],
                             m.ve[0:TP, t:t + 1], m.rs[0:TP, t:t + 1], m.nt[0:TP, t:t + 1])
                nc.vector.tensor_scalar(u_, u_, m.mv[0:TP, 0, t, 0:1], m.rs[0:TP, t:t + 1], ALU.subtract, ALU.mult)
                dve.drain()
                nc.vector.tensor_tensor(u_, u_, row(m, "og"), ALU.mult)
                dve.drain()
                nc.vector.tensor_tensor(u_, u_, row(m, "ob"), ALU.add)
                dve.drain()
                nc.vector.tensor_tensor(u_, u_, xt_, ALU.add)
                dve.drain()
                nc.vector.tensor_tensor(u_, u_, row(m, "bo"), ALU.add)
                dve.drain()
                dve.wait_ge(mix_done, t + 1)
                dve.wait_ge(stored, 16 * (t + 4 if t else 0))
                nc.vector.tensor_tensor(mx_, m.ps[0:TP, 2:4, :].rearrange("p a b -> p (a b)"), u_,
                                        ALU.add).then_inc(mix_used, 1)
                dve.drain()
                nc.vector.bn_stats(m.stats[0:TP, 0:6], mx_[:, 0:512]).then_inc(x1_ready, 1)
                nc.vector.bn_stats(m.stats[0:TP, 6:12], mx_[:, 512:1024])
                dve.drain()
                nc.vector.bn_aggr(m.mv[0:TP, 1, t, :], m.stats[0:TP, :])
                dve.drain()
                inverse_root(nc.vector, var_ready, root_done, 2 * t + 2, m.mv[0:TP, 1, t, 1:2],
                             m.ve[0:TP, t:t + 1], m.rs[0:TP, t:t + 1], m.nt[0:TP, t:t + 1])
                if t:
                    dve.wait_ge(xn_stored, 16 * t)
                    dve.wait_ge(turned, t)
                nc.vector.tensor_scalar(xo_, mx_, m.mv[0:TP, 1, t, 0:1], m.rs[0:TP, t:t + 1], ALU.subtract,
                                        ALU.mult).then_inc(xn_ready, 1)
                dve.drain()


def route(nc, m, tabd):
    with ExitStack() as ctx:
        def sem(name):
            return ctx.enter_context(nc.semaphore(name))
        shifted, exped, masked, ranked, tabled, tab_out, tab_in = (sem(n) for n in (
            "shifted", "rexped", "masked", "ranked", "tabled", "tab_out", "tab_in"))
        HT = T // 2
        block = ctx.enter_context(nc.Block())

        def per_tile(v):
            return v[0:TP, :].unsqueeze(2).to_broadcast([TP, T, E])

        @block.scalar
        def _(act):
            act.wait_ge(shifted, 1)
            nc.scalar.activation(m.score[0:TP, :, :], m.logit[0:TP, :, :], ACT.Exp).then_inc(exped, 1)

        @block.vector
        def _(dve):
            logit, score, rep = (v[0:TP, :, :] for v in (m.logit, m.score, m.rep))
            top1, total, inv, topsum = (m.sc[:, i, :] for i in range(4))
            nc.vector.tensor_reduce(top1[0:TP, :], logit, AX, ALU.max)
            dve.drain()
            nc.vector.tensor_tensor(logit, logit, per_tile(top1), ALU.subtract).then_inc(shifted, 1)
            dve.wait_ge(exped, 1)
            nc.vector.tensor_reduce(total[0:TP, :], score, AX, ALU.add)
            dve.drain()
            nc.vector.reciprocal(inv[0:TP, :], total[0:TP, :])
            dve.drain()
            nc.vector.tensor_tensor(score, score, per_tile(inv), ALU.mult)
            dve.drain()
            for t in range(T):
                nc.vector.max(m.top[0:TP, t, :], m.score[0:TP, t, :])
            dve.drain()
            for t in range(T):
                nc.vector.match_replace(m.rep[0:TP, t, :], m.top[0:TP, t, :], m.score[0:TP, t, :], -1.0)
            dve.drain()
            nc.vector.tensor_scalar(m.mask[0:TP, :, :], rep, 0.0, None, ALU.is_lt)
            nc.vector.tensor_reduce(topsum[0:TP, :], m.top[0:TP, :, :], AX, ALU.add)
            nc.vector.memset(m.mprev[0:TP, 0, :], 0.0)
            dve.drain()
            for t in range(T):
                v = nc.vector.tensor_tensor(m.mprev[0:TP, t + 1, :], m.mprev[0:TP, t, :], m.mask[0:TP, t, :], ALU.add)
                if t == T - 1:
                    v.then_inc(masked, 1)
                dve.drain()
            nc.vector.tensor_scalar(topsum[0:TP, :], topsum[0:TP, :], 1e-20, None, ALU.add)
            dve.drain()
            nc.vector.reciprocal(inv[0:TP, :], topsum[0:TP, :])
            dve.drain()
            nc.vector.tensor_tensor(score, score, m.mask[0:TP, :, :], ALU.mult)
            dve.drain()
            nc.vector.tensor_tensor(score, score, per_tile(inv), ALU.mult)
            for t in range(T):
                nc.vector.memset(m.sel[0:TP, t, :, 0], float(t))
            nc.vector.memset(m.sel[0:TP, :, :, 2], 1.0)
            nc.vector.tensor_scalar(m.sel[0:TP, :, :, 1], m.onesf[0:TP, 0:1].unsqueeze(1).to_broadcast([TP, T, E]),
                                    m.pos[0:TP, 0:1], None, ALU.mult)
            dve.drain()
            nc.vector.tensor_copy(m.sel[0:TP, :, :, 3], score)
            dve.drain()
            nc.vector.tensor_tensor(score, score, m.sel[0:TP, :, :, 3], ALU.subtract)
            dve.drain()
            nc.vector.tensor_copy(m.sel[0:TP, :, :, 4], score)
            dve.drain()
            nc.vector.tensor_tensor(score, score, m.sel[0:TP, :, :, 4], ALU.subtract)
            dve.drain()
            nc.vector.tensor_copy(m.sel[0:TP, :, :, 5], score)
            dve.wait_ge(ranked, 1)
            for i in range(2):
                nc.vector.scalar_tensor_tensor(
                    m.place[0:TP, i * HT:(i + 1) * HT, :],
                    m.ps[0:TP, i, 0:HT * E].rearrange("p (t e) -> p t e", t=HT), 1.0,
                    m.mask[0:TP, i * HT:(i + 1) * HT, :], ALU.add, ALU.mult)
            n, nb, end, before, cmp, prod = (m.cnt[:, i, :] for i in range(6))
            nc.vector.tensor_copy(n, m.ps[:, 2, 0:E])
            dve.drain()
            nc.vector.tensor_scalar(m.place[0:TP, :, :], m.place[0:TP, :, :], -1.0, None, ALU.add)
            nc.vector.memset(nb, 1.0)
            dve.drain()
            for j in range(1, BMAX):
                nc.vector.scalar_tensor_tensor(nb, n, float(P * j), nb, ALU.is_gt, ALU.add)
                dve.drain()
            nc.vector.tensor_tensor_scan(end, m.onesf[:, 0:E], nb, 0.0, ALU.mult, ALU.add)
            dve.drain()
            nc.vector.tensor_tensor(before, end, nb, ALU.subtract)
            dve.drain()
            nc.vector.tensor_copy(m.nbi[:, 0, :], nb)
            nc.vector.tensor_copy(m.nbi[:, 1, :], before)
            nc.vector.tensor_scalar(m.nbi[:, 2, :], nb, -1.0, None, ALU.add)
            nc.vector.tensor_scalar(m.nbi[:, 3, :], end, -1.0, None, ALU.add)
            nc.vector.tensor_copy(m.tot[:], end[:, E - 1:E])
            for h in range(2):
                a, s = m.cnt[:, 6, 0:1], m.cnt[:, 6, 1:2]
                dve.drain()
                nc.vector.tensor_scalar(cmp, end, m.pos[:, h:h + 1], None, ALU.is_le)
                dve.drain()
                nc.vector.tensor_reduce(a, cmp, AX, ALU.add)
                nc.vector.tensor_tensor(prod, cmp, nb, ALU.mult)
                dve.drain()
                nc.vector.tensor_reduce(s, prod, AX, ALU.add)
                nc.vector.tensor_scalar(a, a, float(E - 1), None, ALU.min)
                dve.drain()
                nc.vector.tensor_tensor(s, m.pos[:, h:h + 1], s, ALU.subtract)
                nc.vector.tensor_copy(m.tabp[:, h, 0:1], a)
                dve.drain()
                nc.vector.tensor_scalar(s, s, float(BMAX - 1), float(P), ALU.min, ALU.mult)
                dve.drain()
                nc.vector.tensor_copy(m.tabp[:, h, 1:2], s).then_inc(tabled, 1)

        @block.tensor
        def _(pe):
            pe.wait_ge(masked, 1)
            for t in range(T):
                o = m.ps[0:TP, t // HT, (t % HT) * E:(t % HT + 1) * E]
                nc.tensor.matmul(o, m.before[0:TP, 0:TP], m.mask[0:TP, t, :], start=(t % HT == 0), stop=False,
                                 skip_group_check=True)
                nc.tensor.matmul(o, m.ones[0:TP, 0:TP], m.mprev[0:TP, t, :], start=False, stop=True,
                                 skip_group_check=True)
            nc.tensor.matmul(m.ps[:, 2, 0:E], m.ones[0:TP, :], m.mprev[0:TP, T, :], start=True,
                             stop=True).then_inc(ranked, 1)

        @block.sync
        def _(sp):
            sp.wait_ge(tabled, 2)
            for h in range(2):
                sp.dma_start(tabd[h * P:(h + 1) * P, :], m.tabp[:, h, :]).then_inc(tab_out, 16)
            sp.wait_ge(tab_out, 32)
            sp.dma_start(m.tab[:], tabd[0:TAB, :].rearrange("b k -> (b k)").unsqueeze(0)).then_inc(tab_in, 16)
            sp.wait_ge(tab_in, 16)


def experts(nc, m, weights, xn2, acc, out):
    with ExitStack() as ctx:
        def sem(name):
            return ctx.enter_context(nc.semaphore(name))
        raw_in = [sem(f"raw_in{i}") for i in range(RAW)]
        hi_done, lo_done = sem("hi_done"), sem("lo_done")
        hot_ready, listed, meta_ready, gathered = sem("ehot_ready"), sem("listed"), sem("meta_ready"), sem("gathered")
        x_turned, xhi_ready, xT_ready, gu_done, silu_ready = (sem(n) for n in (
            "x_turned", "xhi_ready", "xT_ready", "gu_done", "silu_ready"))
        taken = sem("taken")
        h_ready, h_turned, hhi_ready, hT_ready, down_done, y_ready, added, landed, copied = (sem(n) for n in (
            "eh_ready", "eh_turned", "hhi_ready", "ehT_ready", "down_done", "y_ready", "added", "landed", "copied"))
        block = ctx.enter_context(nc.Block())

        def piece(v, q):
            return v[:, q * PIECE:(q + 1) * PIECE]

        @block.sync
        def _(sp):
            for q in range(PIECES):
                if q >= RAW:
                    sp.wait_ge(lo_done, q - RAW + 1)
                sp.dma_start(m.raw[q % RAW], weights[0, q]).then_inc(raw_in[q % RAW], 16)
            with sp.Fori(1, E) as e:
                for q in range(PIECES):
                    sp.wait_ge(lo_done, e * PIECES + (q - RAW + 1))
                    sp.dma_start(m.raw[q % RAW], weights[bass.ds(e, 1), q].rearrange("o p n -> (o p) n")
                                 ).then_inc(raw_in[q % RAW], 16)
            total = sp.value_load(m.tot[0:1, 0:1], min_val=E, max_val=MAXB)
            sp.wait_ge(added, total * 16)
            sp.dma_start(out.rearrange("n d -> (n d)").rearrange("(a b) -> a b", b=1000),
                         acc[0:N, :].rearrange("n d -> (n d)").rearrange("(a b) -> a b", b=1000)
                         ).then_inc(copied, 16)
            sp.wait_ge(copied, 16)

        @block.tensor
        def _(pe):
            def make_list():
                for t in range(T):
                    mm = nc.tensor.matmul(m.ps[:, 1, 2 * P:2 * P + 6], m.oh[0:TP, t, :], m.sw[0:TP, t, :],
                                          start=(t == 0), stop=(t == T - 1))
                mm.then_inc(listed, 1)

            def turn_x(first, last):
                for c in range(first, last):
                    mm = nc.tensor.transpose(m.ps[:, 6 + c // 4, (c % 4) * P:(c % 4 + 1) * P],
                                             m.xg[:, c * P:(c + 1) * P], m.ident[:])
                return mm

            def product(to, left, right, chunks, width, part=None):
                for c in part or range(chunks):
                    for half, o in enumerate(to):
                        for n, (i, j) in enumerate(((0, 0), (0, 1), (1, 0))):
                            mm = nc.tensor.matmul(o, left[i][:, c, :], right[j][:, c, half * width:(half + 1) * width],
                                                  start=(c == 0 and n == 0), stop=(c == chunks - 1 and n == 2))
                return mm

            for b in range(2):
                pe.wait_ge(hot_ready, b + 1)
                if b:
                    pe.wait_ge(taken, b)
                make_list()
            pe.wait_ge(gathered, 16)
            turn_x(0, DC).then_inc(x_turned, 1)
            with pe.Fori(0, E) as e:
                blocks = pe.value_load(m.nbi[0:1, 0, bass.ds(e, 1)], min_val=1, max_val=BMAX)
                before = pe.value_load(m.nbi[0:1, 1, bass.ds(e, 1)], min_val=0, max_val=MAXB)
                with pe.Fori(0, blocks) as j:
                    k = pe.snap(before + j)
                    pe.wait_ge(xT_ready, k * 2 + 2)
                    pe.wait_ge(lo_done, e * PIECES + MP)
                    product([m.ps[:, i, 0:FH] for i in range(2)], m.xT, m.gate, DC, FH).then_inc(gu_done, 1)
                    pe.wait_ge(lo_done, e * PIECES + 2 * MP)
                    product([m.ps[:, 2 + i, 0:FH] for i in range(2)], m.xT, m.up, DC, FH).then_inc(gu_done, 1)
                    pe.wait_ge(gathered, k * 16 + 32)
                    turn_x(0, DC // 2)
                    pe.wait_ge(hot_ready, k + 3)
                    pe.wait_ge(silu_ready, k * 2 + 2)
                    make_list()
                    pe.wait_ge(h_ready, k + 1)
                    for c in range(FC):
                        mm = nc.tensor.transpose(m.ps[:, c // 4, (c % 4) * P:(c % 4 + 1) * P],
                                                 m.ex[:, c * P:(c + 1) * P], m.ident[:])
                    mm.then_inc(h_turned, 1)
                    turn_x(DC // 2, DC).then_inc(x_turned, 1)
                    pe.wait_ge(lo_done, e * PIECES + 3 * MP)
                    pe.wait_ge(y_ready, k * 2 + 2)
                    y = [m.ps[:, 4 + i, :] for i in range(2)]
                    pe.wait_ge(hT_ready, k * 2 + 1)
                    product(y, m.hxT, m.down, FC, 512, range(4))
                    pe.wait_ge(hT_ready, k * 2 + 2)
                    product(y, m.hxT, m.down, FC, 512, range(4, FC)).then_inc(down_done, 1)

        @block.scalar
        def _(act):
            def high(e, q):
                act.wait_ge(raw_in[q % RAW], e * (16 * PIECES // RAW) + 16 * (q // RAW) + 16)
                nc.scalar.activation(piece(m.whi, q), m.raw[q % RAW], ACT.Copy).then_inc(hi_done, 1)

            def keep_x(b):
                act.wait_ge(x_turned, b + 1)
                for i in range(2):
                    nc.scalar.activation(m.xT[0][:, 4 * i:4 * i + 4, :],
                                         m.ps[:, 6 + i, :].rearrange("p (c n) -> p c n", c=4),
                                         ACT.Copy).then_inc(xhi_ready, 1)

            def take_list():
                nc.scalar.activation(m.selc[:], m.ps[:, 1, 2 * P:2 * P + 6], ACT.Copy).then_inc(taken, 1)

            def block_work(k, more, e):
                act.wait_ge(gu_done, k * 2 + 1)
                for half in range(2):
                    nc.scalar.activation(m.ex[:, half * FH:(half + 1) * FH], m.ps[:, half, 0:FH],
                                         ACT.Silu).then_inc(silu_ready, 1)
                if more:
                    for q in range(MP):
                        high(e + 1, q)
                act.wait_ge(h_turned, k + 1)
                nc.scalar.activation(m.hxT[0][:, 0:4, :], m.ps[:, 0, :].rearrange("p (c n) -> p c n", c=4),
                                     ACT.Copy).then_inc(hhi_ready, 1)
                take_list()
                nc.scalar.activation(m.hxT[0][:, 4:6, :], m.ps[:, 1, 0:2 * P].rearrange("p (c n) -> p c n", c=2),
                                     ACT.Copy).then_inc(hhi_ready, 1)
                keep_x(k + 1)
                if more:
                    for q in range(MP, 2 * MP):
                        high(e + 1, q)
                act.wait_ge(meta_ready, k + 3)
                act.wait_ge(landed, k + 1)
                act.wait_ge(down_done, k + 1)
                for half in range(2):
                    nc.scalar.activation(m.yo[:, half * 512:half * 512 + 512], m.ps[:, 4 + half, :], ACT.Copy,
                                         scale=m.meta[:, 2, 2:3]).then_inc(y_ready, 1)
                if more:
                    for q in range(2 * MP, 3 * MP):
                        high(e + 1, q)

            act.wait_ge(listed, 1)
            take_list()
            act.wait_ge(meta_ready, 1)
            act.wait_ge(listed, 2)
            take_list()
            for q in range(PIECES):
                high(0, q)
                if q == MP - 1:
                    keep_x(0)
            with act.Fori(0, E - 1) as e:
                before = act.value_load(m.nbi[0:1, 1, bass.ds(e, 1)], min_val=0, max_val=MAXB)
                others = act.value_load(m.nbi[0:1, 2, bass.ds(e, 1)], min_val=0, max_val=BMAX - 1)
                with act.If(others > 0):
                    with act.Fori(0, others) as j:
                        block_work(act.snap(before + j), False, e)
                last = act.value_load(m.nbi[0:1, 3, bass.ds(e, 1)], min_val=0, max_val=MAXB)
                block_work(last, True, e)
            blocks = act.value_load(m.nbi[0:1, 0, E - 1:E], min_val=1, max_val=BMAX)
            before = act.value_load(m.nbi[0:1, 1, E - 1:E], min_val=0, max_val=MAXB)
            with act.Fori(0, blocks) as j:
                block_work(act.snap(before + j), False, None)

        @block.vector
        def _(dve):
            def low(e, q):
                dve.wait_ge(hi_done, e * PIECES + q + 1)
                nc.vector.tensor_tensor(piece(m.wlo, q), m.raw[q % RAW], piece(m.whi, q).bitcast(F32),
                                        ALU.subtract).then_inc(lo_done, 1)

            def one_hot(b):
                e = dve.value_load(m.tab[0:1, bass.ds(b * 2, 1)], min_val=0, max_val=E - 1)
                at = dve.value_load(m.tab[0:1, bass.ds(b * 2 + 1, 1)], min_val=0, max_val=(BMAX - 1) * P)
                nc.vector.tensor_tensor(m.oh[0:TP, :, :],
                                        m.place[0:TP, :, bass.ds(e, 1)].to_broadcast([TP, T, P]),
                                        m.iota16[0:TP, bass.ds(at, P)].unsqueeze(1).to_broadcast([TP, T, P]),
                                        ALU.is_equal)
                nc.vector.tensor_copy(m.sw[0:TP, :, :].unsqueeze(2),
                                      m.sel[0:TP, :, bass.ds(e, 1), :]).then_inc(hot_ready, 1)

            def low_x(b):
                for i in range(2):
                    dve.wait_ge(xhi_ready, b * 2 + i + 1)
                    nc.vector.tensor_tensor(m.xT[1][:, 4 * i:4 * i + 4, :],
                                            m.ps[:, 6 + i, :].rearrange("p (c n) -> p c n", c=4),
                                            m.xT[0][:, 4 * i:4 * i + 4, :].bitcast(F32),
                                            ALU.subtract).then_inc(xT_ready, 1)

            def block_work(k, more, e):
                if more:
                    for q in range(MP - 1):
                        low(e + 1, q)
                dve.wait_ge(silu_ready, k * 2 + 2)
                dve.wait_ge(gu_done, k * 2 + 2)
                for half in range(2):
                    ex = m.ex[:, half * FH:(half + 1) * FH]
                    v = nc.vector.tensor_tensor(ex, m.ps[:, 2 + half, 0:FH], ex, ALU.mult)
                v.then_inc(h_ready, 1)
                if more:
                    low(e + 1, MP - 1)
                for a, b, bank in ((0, 4, 0), (4, 6, 1)):
                    dve.wait_ge(hhi_ready, k * 2 + bank + 1)
                    nc.vector.tensor_tensor(m.hxT[1][:, a:b, :],
                                            m.ps[:, bank, 0:(b - a) * P].rearrange("p (c n) -> p c n", c=b - a),
                                            m.hxT[0][:, a:b, :].bitcast(F32), ALU.subtract).then_inc(hT_ready, 1)
                low_x(k + 1)
                dve.wait_ge(listed, k + 3)
                one_hot(k + 3)
                if more:
                    for q in range(MP, 3 * MP):
                        low(e + 1, q)

            dve.drain().then_inc(y_ready, 2)
            one_hot(0)
            for b in range(1, 3):
                dve.wait_ge(listed, b)
                one_hot(b)
            for q in range(PIECES):
                low(0, q)
                if q == MP - 1:
                    low_x(0)
            with dve.Fori(0, E - 1) as e:
                before = dve.value_load(m.nbi[0:1, 1, bass.ds(e, 1)], min_val=0, max_val=MAXB)
                others = dve.value_load(m.nbi[0:1, 2, bass.ds(e, 1)], min_val=0, max_val=BMAX - 1)
                with dve.If(others > 0):
                    with dve.Fori(0, others) as j:
                        block_work(dve.snap(before + j), False, e)
                last = dve.value_load(m.nbi[0:1, 3, bass.ds(e, 1)], min_val=0, max_val=MAXB)
                block_work(last, True, e)
            blocks = dve.value_load(m.nbi[0:1, 0, E - 1:E], min_val=1, max_val=BMAX)
            before = dve.value_load(m.nbi[0:1, 1, E - 1:E], min_val=0, max_val=MAXB)
            with dve.Fori(0, blocks) as j:
                block_work(dve.snap(before + j), False, None)

        @block.gpsimd
        def _(pool):
            total = pool.value_load(m.tot[0:1, 0:1], min_val=E, max_val=MAXB)

            def meta(first):
                c = m.selc
                nc.gpsimd.tensor_tensor(m.wpart[:], c[:, 3:4], c[:, 4:5], ALU.add)
                if not first:
                    nc.gpsimd.tensor_copy(m.metai[:, 2, :], m.metai[:, 1, :])
                    pool.drain()
                    nc.gpsimd.tensor_copy(m.metai[:, 1, :], m.metai[:, 0, :])
                pool.drain()
                nc.gpsimd.tensor_scalar(m.metai[:, 0, 0:1], c[:, 0:1], float(TP), c[:, 1:2], ALU.mult, ALU.add)
                nc.gpsimd.tensor_scalar(m.metai[:, 0, 1:2], c[:, 2:3], m.pos[:, 3:4], m.pos[:, 2:3], ALU.mult, ALU.add)
                nc.gpsimd.tensor_tensor(m.meta[:, 0, 2:3], m.wpart[:], c[:, 5:6], ALU.add).then_inc(meta_ready, 1)
                pool.drain()

            def gather():
                nc.gpsimd.tensor_tensor(m.idx[:, 0:1], m.metai[:, 0, 0:1], m.metai[:, 0, 1:2], ALU.add)
                pool.drain()
                pool.indirect_dma_start(out=m.xg, out_offset=None, in_=xn2,
                                        in_offset=bass.IndirectOffsetOnAxis(ap=m.idx[:, 0:1], axis=0)
                                        ).then_inc(gathered, 16)

            pool.sem_inc(landed, 1)
            nc.gpsimd.memset(m.meta[:], 0.0)
            pool.wait_ge(taken, 1)
            meta(first=True)
            gather()
            pool.wait_ge(taken, 2)
            meta(first=False)
            pool.wait_ge(x_turned, 1)
            gather()
            with pool.Fori(0, total) as k:
                pool.wait_ge(taken, k + 3)
                meta(first=False)
                pool.wait_ge(x_turned, k + 2)
                gather()
                pool.wait_ge(y_ready, k * 2 + 4)
                nc.gpsimd.tensor_tensor(m.idx[:, 1:2], m.metai[:, 2, 0:1], m.metai[:, 2, 1:2], ALU.add)
                pool.drain()
                pool.indirect_dma_start(out=acc, out_offset=bass.IndirectOffsetOnAxis(ap=m.idx[:, 1:2], axis=0),
                                        in_=m.yo, in_offset=None, compute_op=ALU.add).then_inc(added, 16)
                pool.wait_ge(added, k * 16 + 16)
                pool.sem_inc(landed, 1)
            pool.wait_ge(gathered, total * 16 + 32)


def kernel(x, src, dst, L0_gnn_ln_in_g, L0_gnn_ln_in_b, L0_gnn_W1, L0_gnn_b1, L0_gnn_W2, L0_gnn_b2,
           L0_gnn_layer_Wa, L0_gnn_layer_ba, L0_gnn_layer_Wb, L0_gnn_layer_bb, L0_gnn_layer_ng,
           L0_gnn_layer_nb, L0_gnn_Wd1, L0_gnn_bd1, L0_gnn_Wd2, L0_gnn_bd2, L0_gnn_out_g, L0_gnn_out_b,
           L0_mix_w_qkv, L0_mix_w_out, L0_mix_b_out, L0_ffn_gate_w, L0_ffn_w_gate, L0_ffn_w_up,
           L0_ffn_w_down):
    import numpy as np
    import concourse.bacc as bacc
    from concourse.bass_utils import run_bass_kernel_spmd

    def arr(a):
        return np.ascontiguousarray(a)

    def on_partitions(v):
        return np.asarray(v).reshape(-1, P).T

    def chunked(wt):
        wt = np.asarray(wt)
        e, n, k = wt.shape
        return arr(wt.reshape(e, n, k // P, P).transpose(0, 3, 2, 1)).reshape(e, P, k // P * n)

    cols = arr(np.concatenate([on_partitions(v) for v in (
        L0_gnn_ln_in_g, L0_gnn_ln_in_b, L0_gnn_b1, L0_gnn_layer_ba, L0_gnn_bd1)], axis=1))
    rows = arr(np.concatenate([np.asarray(v).reshape(1, -1) for v in (
        L0_gnn_b2, L0_gnn_layer_bb, L0_gnn_layer_ng, L0_gnn_layer_nb, L0_gnn_bd2, L0_gnn_out_g,
        L0_gnn_out_b, L0_mix_b_out)], axis=1))
    pieces = arr(np.concatenate([chunked(v) for v in (L0_ffn_w_gate, L0_ffn_w_up, L0_ffn_w_down)], axis=2)
                 .reshape(E, P, PIECES, PIECE).transpose(0, 2, 1, 3))
    arrays = {
        "x": arr(x), "srcT": arr(np.asarray(src).reshape(CHUNKS, CE).T),
        "dstT": arr(np.asarray(dst).reshape(CHUNKS, CE).T), "dst": arr(dst), "cols": cols, "rows": rows,
        "w1": arr(L0_gnn_W1), "w2": arr(L0_gnn_W2), "wa": arr(L0_gnn_layer_Wa), "wb": arr(L0_gnn_layer_Wb),
        "wd1": arr(L0_gnn_Wd1), "wd2": arr(L0_gnn_Wd2), "wqkv": arr(L0_mix_w_qkv), "wout": arr(L0_mix_w_out),
        "gatew": chunked(np.asarray(L0_ffn_gate_w)[None])[0],
        "weights": pieces,
    }
    nc = bacc.Bacc("TRN2", target_bir_lowering=False, num_devices=1)
    args = {n: nc.dram_tensor("in_" + n, a.shape, mybir.dt.from_np(a.dtype), kind="ExternalInput").ap()
            for n, a in arrays.items()}
    out = nc.dram_tensor("out", (N, D), F32, kind="ExternalOutput").ap()
    build(nc, **args, out=out)
    r = run_bass_kernel_spmd(nc, [{"in_" + n: a for n, a in arrays.items()}], core_ids=[0])
    return r.results[0]["out"]
```

```python
from contextlib import ExitStack

import concourse.bass as bass
from concourse import mybir

F32 = mybir.dt.float32
F32R = mybir.dt.float32r
BF16 = mybir.dt.bfloat16
I32 = mybir.dt.int32
I16 = mybir.dt.int16
ALU = mybir.AluOpType
ACT = mybir.ActivationFunctionType
AX = mybir.AxisListType.X
RMAX = bass.bass_isa.ReduceOp.max

P = 128
N, D = 1250, 1024
TP = 125
T = N // TP
HT = T // 2
DC = D // P
HID, DB = 512, 256
HC, BC = HID // P, DB // P
LAYERS = 3
HEADS, DH = 16, 64
PAIRS = HEADS // 2
E, TOPK, F = 64, 8, 768
FC, FH = F // P, F // 2
EDGES = 40000
CE = 125
CHUNKS = EDGES // CE
EP = 16
CG = 4
NGROUP = CHUNKS // CG
GROUPQ = NGROUP // EP
PARTS = ((0, 0), (0, 1), (1, 0))
SPANS = ((0, 418), (418, 416), (834, 416))
UNIT = 256
QU = D // UNIT
UNITS = QU + PAIRS
UP = 4
UCH = DC // UP
URAW = 3
MAXB = E + (N * TOPK - E) // P + 1
BMAX = (N + P - 1) // P
TAB = MAXB + BMAX + 3
WCOLS = 3 * DC * F
PIECE = 768
PIECES = WCOLS // PIECE
MP = PIECES // 3
RAW = 6
XFIRST = 5
AHEAD = 6
PADROWS = P
EPS = 1e-5

ROWS = {}
_at = 0
for _name, _n in (("b2", DB), ("bb", LAYERS * DB), ("ng", LAYERS * DB), ("nb", LAYERS * DB),
                  ("bd2", D), ("og", D), ("ob", D), ("bo", D)):
    ROWS[_name] = (_at, _n)
    _at += _n
ROWLEN = _at
COLS = {}
_at = 0
for _name, _n in (("g", DC), ("b", DC), ("b1", HC), ("ba", LAYERS * BC), ("bd1", HC)):
    COLS[_name] = (_at, _n)
    _at += _n
COLLEN = _at


class Names:
    pass


def memory(nc, ctx):
    def sb(name, shape, dt=F32):
        return ctx.enter_context(nc.sbuf_tensor(name, shape, dt))

    m = Names()
    m.ps = ctx.enter_context(nc.psum_tensor("ps", [P, 8, 512], F32))
    arena_at = (nc.sbuf_base + 31) // 32 * 32
    arena = sb("arena", [P, 2 * WCOLS])
    r0, r1, r2, r3 = 0, 12500, 22500, 30692

    def view(at, *shape):
        n = 1
        for s in shape:
            n *= s
        v = arena[:, at:at + n]
        if len(shape) == 2:
            return v.rearrange("p (a b) -> p a b", a=shape[0])
        if len(shape) == 3:
            return v.rearrange("p (a b c) -> p a b c", a=shape[0], b=shape[1])
        return v

    m.xnT = view(r0, DC, N)
    m.adjT = view(r0, T, N)
    m.wout = view(r0, DC, D)
    m.wd2 = view(r0 + DC * D, HC, D)
    m.h0T = view(r1, DC, N)
    m.qT = view(r1, DC, N)
    m.w1 = view(r2, DC, HID)
    m.w2 = view(r2 + DC * HID, HC, DB)
    m.wab = view(r2, 2 * LAYERS * BC, DB)
    m.zz = view(r2 + 4096, T, DB)
    m.zstats = view(r2 + 4096 + T * DB, T, 6)
    m.hT = view(r2, BC, N)
    m.wd1 = view(r2 + 2500, BC, HID)
    m.tile = [view(r2 + 2500 + 1024 + i * D, D) for i in range(4)]
    m.h1T = view(r3, HC, N)
    m.uraw = [view(32504 + i * UCH * UNIT, UCH, UNIT) for i in range(URAW)]
    m.kvm = view(34040, PAIRS, P)
    m.z16 = view(35064, PAIRS, HEADS)
    m.kv = [view(35192 + i * 257, 257) for i in range(3)]
    m.tmp = [view(35963 + i * 418, 418) for i in range(2)]
    m.tmpk = [view(12048 + i * P, P) for i in range(3)]
    m.zT = view(r3, BC, N)
    m.aT = view(r3 + 2500, BC, N)
    m.dT = view(r3, HC, N)
    m.edge = [view(r3 + i * CHUNKS, CHUNKS) for i in range(4)]
    m.dstrow = view(r2, GROUPQ, CG * CE)
    m.dstrowf = view(r2 + GROUPQ * CG * CE, GROUPQ, CG * CE)
    m.hot = [view(r3 + 4 * CHUNKS + i * N // 2, N // 2) for i in range(CG)]
    m.hotd = [view(r3 + 4 * CHUNKS + CG * N // 2 + i * 64, 63) for i in range(CG)]
    def placed(name, at, n):
        return nc.alloc_sbuf_tensor_at(name, [P, n], F32R, offset=at)

    def matrices(v):
        q = DC * F
        return (v[:, 0:q].rearrange("p (c f) -> p c f", c=DC), v[:, q:2 * q].rearrange("p (c f) -> p c f", c=DC),
                v[:, 2 * q:3 * q].rearrange("p (c d) -> p c d", c=FC))

    m.whi = placed("whi", arena_at, WCOLS)
    m.wlo = placed("wlo", arena_at + 4 * WCOLS, WCOLS)
    m.gate, m.up, m.down = zip(matrices(m.whi), matrices(m.wlo))
    late_at = (nc.sbuf_base + 31) // 32 * 32
    late = sb("late", [P, 11648])
    lat = [ROWLEN]

    def small(*shape, dt=F32):
        n = 1
        for q in shape:
            n *= q
        words = n // (2 if dt == BF16 else 1)
        v = late[:, lat[0]:lat[0] + words]
        lat[0] += words
        if dt != F32:
            v = v.bitcast(dt)
        if len(shape) == 2:
            return v.rearrange("p (a b) -> p a b", a=shape[0])
        if len(shape) == 3:
            return v.rearrange("p (a b c) -> p a b c", a=shape[0], b=shape[1])
        return v

    m.rows = late[:, 0:ROWLEN]
    m.xt = ([view(r3 + i * D, D) for i in range(6)]
            + [late[:, DB + i * D:DB + (i + 1) * D] for i in range(T - 6)])
    m.xstats = view(r2 + DC * HID + HC * DB, T, 12)
    m.xhi = placed("xhi", arena_at + 4 * (r2 + 4), DC * N)[:, :].rearrange("p (c n) -> p c n", c=DC)
    m.xlo = placed("xlo", arena_at + 4 * r0, DC * N)[:, :].rearrange("p (c n) -> p c n", c=DC)
    upl = [late_at + 4 * (DB + i * DC * UNIT) for i in range(3)] + [arena_at + 4 * DC * N]
    m.uhi, m.ulo = ([placed(f"unit_{name}{i}", upl[2 * j + i], DC * UNIT)[:, :].rearrange("p (c n) -> p c n", c=DC)
                     for i in range(2)] for j, name in enumerate(("high", "low")))
    m.den = late[:, DB:DB + N]
    m.pick = late[:, DB + N:DB + N + PAIRS * P].rearrange("p (a b) -> p a b", a=PAIRS)
    m.h = sb("h", [P, T, DB])
    m.xg = late[:, 0:1024]
    m.ex = late[:, 1024:1792]
    m.yo = late[:, 1792:2816]
    m.oh = late[:, 2816:3456].bitcast(BF16).rearrange("p (t s) -> p t s", t=T)
    m.raw = [late[:, 3456 + i * PIECE:3456 + (i + 1) * PIECE] for i in range(RAW)]
    part = 3456 + RAW * PIECE
    m.xT = [placed(f"xT{i}", late_at + 4 * (part + i * D), D)[:, :].rearrange("p (c n) -> p c n", c=DC)
            for i in range(2)]
    m.hxT = [placed(f"hxT{i}", late_at + 4 * (part + 2 * D + i * F), F)[:, :].rearrange("p (c n) -> p c n", c=FC)
             for i in range(2)]
    m.cols = sb("cols", [P, COLLEN])
    m.ident = sb("ident", [P, P])
    m.before = sb("before", [P, TP], BF16)
    m.ones = sb("ones", [P, P], BF16)
    m.onesf = sb("onesf", [P, P])
    m.zeros = small(512, dt=BF16)
    m.iota16 = sb("iota16", [P, BMAX * P], I16)
    m.pos = sb("pos", [P, 4])
    m.stats = sb("stats", [P, 12])
    m.mv = small(3, T, 2)
    m.ve = sb("ve", [P, T])
    m.rs = sb("rs", [P, T])
    m.mr = sb("mr", [P, T, 2])
    m.nt = sb("nt", [P, T])
    m.gatew = small(DC, E)
    m.logit = small(T, E)
    m.score = view(0, T, E)
    m.rep = view(T * E, T, E)
    m.top = sb("top", [P, T, TOPK])
    m.sc = sb("sc", [P, 4, T])
    m.mask = small(T, E, dt=BF16)
    m.mprev = small(T + 1, E, dt=BF16)
    hs = m.h[:, :, :].rearrange("p t f -> p (t f)")
    m.place = hs[:, 0:T * E].rearrange("p (t e) -> p t e", t=T)
    m.sel = hs[:, T * E:4 * T * E].bitcast(BF16).rearrange("p (t e k) -> p t e k", t=T, e=E)
    m.cnt = small(8, E)
    m.tabp = sb("tabp", [P, 2, 2], I32)
    m.tab = sb("tab", [1, 2 * TAB], I32)
    m.nbi = sb("nbi", [P, 4, E], I32)
    m.tot = sb("tot", [P, 1], I32)
    m.rng = small(8, 2 * T)
    m.rngh = small(T, 2, GROUPQ)
    m.rngi = small(3, T, dt=I32)
    m.sw = sb("sw", [P, T, 6], BF16)
    m.selc = sb("selc", [P, 6])
    m.wpart = sb("wpart", [P, 1])
    m.meta = sb("meta", [P, 3, 3])
    m.metai = m.meta[:, :, :].bitcast(I32)
    m.idx = sb("idx", [P, 2], I32)
    return m


def build(nc, x, srcT, dstT, dst, cols, rows, w1, w2, wa, wb, wd1, wd2, wqkv, wout, gatew,
          weights, out):
    ctx = ExitStack()
    with ctx:
        m = memory(nc, ctx)
        xn2 = nc.dram_tensor("xn2", [N + PADROWS, D], F32, kind="Internal").ap()
        tabd = nc.dram_tensor("tabd", [2 * P, 2], I32, kind="Internal").ap()
        w = Names()
        w.w1_in, w.w2_in, w.rows_in, w.cols_in, w.gatew_in, w.made = (
            ctx.enter_context(nc.semaphore(n)) for n in ("w1_in", "w2_in", "rows_in", "cols_in", "gatew_in", "made"))
        normalise(nc, m, w, x, cols, rows, w1, w2, gatew)
        encode(nc, m, w)
        attention(nc, m, wqkv)
        adjacency(nc, m, w, srcT, dstT, dst, rows)
        messages(nc, m, wa, wb)
        combine(nc, m, w, x, wd1, wd2, wout, xn2, out)
        route(nc, m, tabd)
        experts(nc, m, weights, xn2, out)


def row(m, name, i=0, n=None):
    at, size = ROWS[name]
    n = n or size
    return m.rows[0:TP, at + i * n:at + (i + 1) * n]


def col(m, name, i):
    return m.cols[:, COLS[name][0] + i:COLS[name][0] + i + 1]


def inverse_root(dve, act_ready, act_done, n, var, ve, y, t):
    dve.tensor_scalar(ve, var, EPS, None, ALU.add).then_inc(act_ready, 1)
    dve.wait_ge(act_done, n)
    dve.reciprocal(y, y)
    dve.drain()
    dve.tensor_tensor(t, y, y, ALU.mult)
    dve.drain()
    dve.tensor_tensor(t, t, ve, ALU.mult)
    dve.drain()
    dve.tensor_scalar(t, t, -0.5, 1.5, ALU.mult, ALU.add)
    dve.drain()
    dve.tensor_tensor(y, y, t, ALU.mult)
    dve.drain()


def normalise(nc, m, w, x, cols, rows, w1, w2, gatew):
    with ExitStack() as ctx:
        def sem(name):
            return ctx.enter_context(nc.semaphore(name))
        x_in = [sem(f"x_in{t}") for t in range(T)]
        var_ready, root_done, xn_ready, xh_ready = sem("var_ready"), sem("root_done"), sem("xn_ready"), sem("xh_ready")
        turned, kept = sem("turned"), sem("kept")
        turns = [(which, t) for half in range(2) for which in range(2) for t in range(half * HT, (half + 1) * HT)]
        block = ctx.enter_context(nc.Block())

        @block.sync
        def _(sp):
            for t in range(T):
                sp.dma_start(m.xt[t][0:TP, :], x[t * TP:(t + 1) * TP, :]).then_inc(x_in[t], 16)
            sp.dma_start(m.cols[:], cols).then_inc(w.cols_in, 16)
            sp.dma_start(m.w1, w1.rearrange("(c p) n -> p c n", p=P)).then_inc(w.w1_in, 16)
            sp.dma_start(m.w2, w2.rearrange("(c p) n -> p c n", p=P)).then_inc(w.w2_in, 16)
            sp.dma_start(m.rows[0:TP, 0:DB], rows[:, 0:DB].to_broadcast([TP, DB])).then_inc(w.rows_in, 16)
            sp.dma_start(m.gatew, gatew.rearrange("p (c e) -> p c e", c=DC)).then_inc(w.gatew_in, 16)

        @block.gpsimd
        def _(pool):
            nc.gpsimd.memset(m.ident[:], 0.0)
            nc.gpsimd.memset(m.before[:], 1.0)
            nc.gpsimd.memset(m.ones[:], 1.0)
            nc.gpsimd.memset(m.onesf[:], 1.0)
            nc.gpsimd.memset(m.zeros, 0.0)
            pool.drain()
            nc.gpsimd.affine_select(out=m.ident[:], in_=m.ident[:], compare_op=ALU.not_equal, fill=1.0,
                                    base=0, pattern=[[-1, P]], channel_multiplier=1)
            nc.gpsimd.affine_select(out=m.before[:], in_=m.before[:], compare_op=ALU.is_gt, fill=0.0,
                                    base=0, pattern=[[1, TP]], channel_multiplier=-1)
            nc.gpsimd.iota(m.iota16[:], pattern=[[1, BMAX * P]], base=0, channel_multiplier=0,
                           allow_small_or_imprecise_dtypes=True)
            nc.gpsimd.iota(m.pos[:, 0:1], pattern=[[1, 1]], base=0, channel_multiplier=1,
                           allow_small_or_imprecise_dtypes=True)
            nc.gpsimd.iota(m.pos[:, 1:2], pattern=[[1, 1]], base=P, channel_multiplier=1,
                           allow_small_or_imprecise_dtypes=True)
            nc.gpsimd.iota(m.pos[:, 2:3], pattern=[[1, 1]], base=N, channel_multiplier=1,
                           allow_small_or_imprecise_dtypes=True)
            nc.gpsimd.iota(m.pos[:, 3:4], pattern=[[1, 1]], base=-N, channel_multiplier=-1,
                           allow_small_or_imprecise_dtypes=True).then_inc(w.made, 1)

        @block.vector
        def _(dve):
            def moments(which, half):
                tiles = range(half * HT, (half + 1) * HT)
                for t in tiles:
                    if which == 0:
                        dve.wait_ge(x_in[t], 16)
                    for i in range(2):
                        nc.vector.bn_stats(m.xstats[0:TP, t, 6 * i:6 * i + 6], m.xt[t][0:TP, 512 * i:512 * i + 512])
                dve.drain()
                for t in tiles:
                    nc.vector.bn_aggr(m.mv[0:TP, which, t, :], m.xstats[0:TP, t, :])
                dve.drain()

            def root(which, half, n):
                a, b = half * HT, (half + 1) * HT
                inverse_root(nc.vector, var_ready, root_done, n, m.mv[0:TP, which, a:b, 1],
                             m.ve[0:TP, a:b], m.rs[0:TP, a:b], m.nt[0:TP, a:b])
                if which == 0:
                    nc.vector.tensor_copy(m.mr[0:TP, a:b, 0], m.mv[0:TP, 0, a:b, 0])
                    nc.vector.tensor_copy(m.mr[0:TP, a:b, 1], m.rs[0:TP, a:b])

            def apply(which, half):
                for t in range(half * HT, (half + 1) * HT):
                    if which == 1:
                        dve.wait_ge(turned, turns.index((0, t)) + 1)
                    nc.vector.tensor_scalar(m.xt[t][0:TP, :], m.xt[t][0:TP, :], m.mv[0:TP, which, t, 0:1],
                                            m.rs[0:TP, t:t + 1], ALU.subtract, ALU.mult
                                            ).then_inc(xh_ready if which else xn_ready, 1)
                dve.drain()

            moments(0, 0)
            root(0, 0, 1)
            apply(0, 0)
            moments(0, 1)
            root(0, 1, 2)
            moments(1, 0)
            root(1, 0, 3)
            apply(1, 0)
            apply(0, 1)
            moments(1, 1)
            root(1, 1, 4)
            apply(1, 1)

        @block.tensor
        def _(pe):
            pe.wait_ge(w.made, 1)
            for k, (which, t) in enumerate(turns):
                pe.wait_ge(xh_ready if which else xn_ready, t + 1)
                if k >= 4:
                    pe.wait_ge(kept, k - 3)
                for c in range(DC):
                    mm = nc.tensor.transpose(m.ps[:, 2 * (k % 4) + c // 4, (c % 4) * TP:(c % 4 + 1) * TP],
                                             m.xt[t][0:TP, c * P:(c + 1) * P], m.ident[0:TP, 0:TP])
                mm.then_inc(turned, 1)

        @block.scalar
        def _(act):
            def root(half, which):
                act.wait_ge(var_ready, {(0, 0): 1, (1, 0): 2, (0, 1): 3, (1, 1): 4}[half, which])
                v = slice(half * HT, (half + 1) * HT)
                nc.scalar.activation(m.rs[0:TP, v], m.ve[0:TP, v], ACT.Sqrt).then_inc(root_done, 1)

            def keep(half, which):
                for t in range(half * HT, (half + 1) * HT):
                    k = turns.index((which, t))
                    b = 2 * (k % 4)
                    act.wait_ge(turned, k + 1)
                    if which == 0:
                        for i in range(2):
                            a = nc.scalar.activation(m.xnT[:, 4 * i:4 * i + 4, t * TP:(t + 1) * TP],
                                                     m.ps[:, b + i, 0:4 * TP].rearrange("p (c n) -> p c n", c=4),
                                                     ACT.Copy)
                    else:
                        for c in range(DC):
                            a = nc.scalar.activation(m.h0T[:, c, t * TP:(t + 1) * TP],
                                                     m.ps[:, b + c // 4, (c % 4) * TP:(c % 4 + 1) * TP],
                                                     ACT.Identity, bias=col(m, "b", c), scale=col(m, "g", c))
                    a.then_inc(kept, 1)

            root(0, 0)
            keep(0, 0)
            root(1, 0)
            root(0, 1)
            act.wait_ge(w.cols_in, 16)
            keep(0, 1)
            keep(1, 0)
            root(1, 1)
            keep(1, 1)


def encode(nc, m, w):
    with ExitStack() as ctx:
        def sem(name):
            return ctx.enter_context(nc.semaphore(name))
        h1_done, h1_kept, h_done, h_kept = sem("h1_done"), sem("h1_kept"), sem("h_done"), sem("h_kept")
        groups = [(hb, s) for hb in range(HC) for s in range(len(SPANS))]
        block = ctx.enter_context(nc.Block())

        @block.tensor
        def _(pe):
            pe.wait_ge(w.w1_in, 16)
            for g, (hb, s) in enumerate(groups):
                at, n = SPANS[s]
                if g >= 4:
                    pe.wait_ge(h1_kept, g - 3)
                for c in range(DC):
                    mm = nc.tensor.matmul(m.ps[:, g % 4, 0:n], m.w1[:, c, hb * P:(hb + 1) * P],
                                          m.h0T[:, c, at:at + n], start=(c == 0), stop=(c == DC - 1))
                mm.then_inc(h1_done, 1)
            pe.wait_ge(w.w2_in, 16)
            pe.wait_ge(h1_kept, len(groups))
            for t in range(T):
                if t >= 4:
                    pe.wait_ge(h_kept, t - 3)
                for c in range(HC):
                    mm = nc.tensor.matmul(m.ps[0:TP, 4 + t % 4, 0:DB], m.h1T[:, c, t * TP:(t + 1) * TP],
                                          m.w2[:, c, :], start=(c == 0), stop=(c == HC - 1))
                mm.then_inc(h_done, 1)

        @block.scalar
        def _(act):
            for g, (hb, s) in enumerate(groups):
                at, n = SPANS[s]
                act.wait_ge(h1_done, g + 1)
                nc.scalar.activation(m.h1T[:, hb, at:at + n], m.ps[:, g % 4, 0:n], ACT.Relu,
                                     bias=col(m, "b1", hb)).then_inc(h1_kept, 1)

        @block.vector
        def _(dve):
            dve.wait_ge(w.rows_in, 16)
            for t in range(T):
                dve.wait_ge(h_done, t + 1)
                nc.vector.tensor_tensor(m.h[0:TP, t, :], m.ps[0:TP, 4 + t % 4, 0:DB], row(m, "b2"),
                                        ALU.add).then_inc(h_kept, 1)


def attention(nc, m, wqkv):
    NS = len(SPANS)
    q_groups = [(u, cb, s) for u in range(QU) for cb in range(UNIT // P) for s in range(NS)]
    G = len(q_groups)
    GU = G // QU
    BANKS = 6
    steps = [(i, t) for i in range(PAIRS) for t in range(T)]

    with ExitStack() as ctx:
        def sem(name):
            return ctx.enter_context(nc.semaphore(name))
        raw_in = [sem(f"unit_in{s}") for s in range(URAW)]
        uhi_done, ulo_done, xhi_done, xlo_done = sem("uhi_done"), sem("ulo_done"), sem("axhi_done"), sem("axlo_done")
        unit_used, proj_done, cut, exped = sem("unit_used"), sem("proj_done"), sem("cut"), sem("exped")
        q_kept, k_kept, v_kept = sem("q_kept"), sem("k_kept"), sem("v_kept")
        kv_step, kv_kept = sem("kv_step"), sem("kv_kept")
        spread = sem("spread")
        den_done, den_ready, nd_done, nd_kept = sem("den_done"), sem("den_ready"), sem("nd_done"), sem("nd_kept")
        block = ctx.enter_context(nc.Block())

        @block.sync
        def _(sp):
            for p in range(UNITS * UP):
                if p >= URAW:
                    sp.wait_ge(ulo_done, p - URAW + 1)
                sp.dma_start(m.uraw[p % URAW], wqkv[p // UP, p % UP].rearrange("p (c n) -> p c n", c=UCH)
                             ).then_inc(raw_in[p % URAW], 16)

        def part_of(v, p):
            return v[p // UP % 2][:, p % UP * UCH:(p % UP + 1) * UCH, :]

        @block.tensor
        def _(pe):
            xs, us = (m.xhi, m.xlo), (m.uhi, m.ulo)
            for g, (u, cb, s) in enumerate(q_groups):
                at, n = SPANS[s]
                pe.wait_ge(ulo_done, (u + 1) * UP)
                if u == 0 and cb == 0:
                    pe.wait_ge(xlo_done, s + 1)
                if g >= BANKS:
                    pe.wait_ge(q_kept, g - BANKS + 1)
                for c in range(DC):
                    for k, (i, j) in enumerate(PARTS):
                        mm = nc.tensor.matmul(m.ps[:, g % BANKS, 0:n], us[i][u % 2][:, c, cb * P:(cb + 1) * P],
                                              xs[j][:, c, at:at + n],
                                              start=(c == 0 and k == 0), stop=(c == DC - 1 and k == 2))
                mm.then_inc(proj_done, 1)
                if cb == UNIT // P - 1 and s == NS - 1:
                    pe.drain().then_inc(unit_used, 1)

            def accumulate(n):
                i, t = steps[n]
                kv = m.kv[n % 3]
                pe.wait_ge(k_kept, n + 1)
                if t == 0 and i >= 2:
                    pe.wait_ge(kv_kept, i - 1)
                nc.tensor.matmul(m.ps[:, 6 + i % 2, 0:P + 1], kv[0:TP, 0:P], kv[0:TP, P:2 * P + 1],
                                 start=(t == 0), stop=(t == T - 1)).then_inc(kv_step, 1)

            for n, (i, t) in enumerate(steps):
                u = QU + i
                if t == 0:
                    pe.wait_ge(ulo_done, (u + 1) * UP)
                bank = (G + n) % BANKS
                if n < BANKS:
                    pe.wait_ge(q_kept, G + n - BANKS + 1)
                else:
                    pe.wait_ge(k_kept, n - BANKS + 1)
                for c in range(DC):
                    for k, (a, b) in enumerate(PARTS):
                        mm = nc.tensor.matmul(m.ps[0:TP, bank, 0:UNIT], xs[a][:, c, t * TP:(t + 1) * TP],
                                              us[b][u % 2][:, c, :],
                                              start=(c == 0 and k == 0), stop=(c == DC - 1 and k == 2))
                mm.then_inc(proj_done, 1)
                if t == T - 1:
                    pe.drain().then_inc(unit_used, 1)
                if n >= 2:
                    accumulate(n - 2)
            accumulate(len(steps) - 2)
            accumulate(len(steps) - 1)
            pe.wait_ge(kv_kept, PAIRS)
            for s, (at, n) in enumerate(SPANS):
                for pr in range(PAIRS):
                    mm = nc.tensor.matmul(m.ps[0:HEADS, s, 0:n], m.z16[:, pr, :], m.qT[:, pr, at:at + n],
                                          start=(pr == 0), stop=(pr == PAIRS - 1))
                mm.then_inc(den_done, 1)
            for g in range(NS * PAIRS):
                s, pr = divmod(g, PAIRS)
                at, n = SPANS[s]
                if pr == 0:
                    pe.wait_ge(den_ready, s + 1)
                if g >= 2:
                    pe.wait_ge(nd_kept, g - 1)
                b = 3 + 2 * (g % 2)
                nc.tensor.matmul(m.ps[:, b, 0:n], m.kvm[:, pr, :], m.qT[:, pr, at:at + n], start=True, stop=True)
                nc.tensor.matmul(m.ps[:, b + 1, 0:n], m.pick[0:HEADS, pr, :], m.den[0:HEADS, at:at + n],
                                 start=True, stop=True).then_inc(nd_done, 1)

        @block.scalar
        def _(act):
            def high(p):
                act.wait_ge(raw_in[p % URAW], 16 * (p // URAW + 1))
                if p // UP >= 2:
                    act.wait_ge(unit_used, p // UP - 1)
                nc.scalar.activation(part_of(m.uhi, p), m.uraw[p % URAW], ACT.Copy).then_inc(uhi_done, 1)

            for p in range(UP):
                high(p)
            for at, n in SPANS:
                nc.scalar.activation(m.xhi[:, :, at:at + n], m.xnT[:, :, at:at + n], ACT.Copy).then_inc(xhi_done, 1)
            for p in range(UP, 2 * UP):
                high(p)
            for g, (u, cb, s) in enumerate(q_groups):
                n = SPANS[s][1]
                act.wait_ge(cut, g + 1)
                nc.scalar.activation(m.tmp[g % 2][:, 0:n], m.tmp[g % 2][:, 0:n], ACT.Exp).then_inc(exped, 1)
                if u and g % GU < UP:
                    high((u + 1) * UP + g % GU)
            for n, (i, t) in enumerate(steps):
                act.wait_ge(cut, G + n + 1)
                nc.scalar.activation(m.tmpk[n % 3][0:TP, :], m.tmpk[n % 3][0:TP, :], ACT.Exp).then_inc(exped, 1)
                if n >= 3:
                    act.wait_ge(kv_step, n - 2)
                nc.scalar.activation(m.kv[n % 3][0:TP, P:2 * P], m.ps[0:TP, (G + n) % BANKS, P:2 * P],
                                     ACT.Copy).then_inc(v_kept, 1)
                if t < UP and QU + i + 1 < UNITS:
                    high((QU + i + 1) * UP + t)
            for g in range(NS * PAIRS):
                n = SPANS[g // PAIRS][1]
                act.wait_ge(nd_done, g + 1)
                if g >= 2:
                    act.wait_ge(nd_kept, g - 1)
                nc.scalar.activation(m.tmp[g % 2][:, 0:n], m.ps[:, 4 + 2 * (g % 2), 0:n],
                                     ACT.Copy).then_inc(spread, 1)

        @block.vector
        def _(dve):
            def low(p):
                dve.wait_ge(uhi_done, p + 1)
                nc.vector.tensor_tensor(part_of(m.ulo, p), m.uraw[p % URAW], part_of(m.uhi, p).bitcast(F32),
                                        ALU.subtract).then_inc(ulo_done, 1)

            for p in range(UP):
                low(p)
            for s, (at, n) in enumerate(SPANS):
                dve.wait_ge(xhi_done, s + 1)
                nc.vector.tensor_tensor(m.xlo[:, :, at:at + n], m.xnT[:, :, at:at + n],
                                        m.xhi[:, :, at:at + n].bitcast(F32), ALU.subtract).then_inc(xlo_done, 1)
            for p in range(UP, 2 * UP):
                low(p)
            nc.vector.memset(m.kvm, 0.0)
            nc.vector.memset(m.z16, 0.0)
            for v in m.kv:
                nc.vector.memset(v[0:TP, 2 * P:2 * P + 1], 1.0)
            dve.drain()

            def finish_q(g):
                u, cb, s = q_groups[g]
                at, n = SPANS[s]
                dve.wait_ge(exped, g + 1)
                nc.vector.scalar_tensor_tensor(m.qT[:, 2 * u + cb, at:at + n], m.ps[:, g % BANKS, 0:n], 0.0,
                                               m.tmp[g % 2][:, 0:n], ALU.max, ALU.add).then_inc(q_kept, 1)

            for g, (u, cb, s) in enumerate(q_groups):
                n = SPANS[s][1]
                dve.wait_ge(proj_done, g + 1)
                if g >= 2:
                    dve.drain()
                nc.vector.tensor_scalar(m.tmp[g % 2][:, 0:n], m.ps[:, g % BANKS, 0:n], 0.0, None,
                                        ALU.min).then_inc(cut, 1)
                if g:
                    finish_q(g - 1)
                if u and g % GU < UP:
                    low((u + 1) * UP + g % GU)
            finish_q(G - 1)

            def finish_k(n):
                i, t = steps[n]
                dve.wait_ge(v_kept, n + 1)
                nc.vector.scalar_tensor_tensor(m.kv[n % 3][0:TP, 0:P], m.ps[0:TP, (G + n) % BANKS, 0:P], 0.0,
                                               m.tmpk[n % 3][0:TP, :], ALU.max, ALU.add).then_inc(k_kept, 1)

            def keep_pair(i):
                dve.wait_ge(kv_step, (i + 1) * T)
                bank = 6 + i % 2
                for hd in range(2):
                    a, b = hd * DH, (hd + 1) * DH
                    nc.vector.tensor_copy(m.kvm[a:b, i, a:b], m.ps[a:b, bank, a:b])
                    v = nc.vector.tensor_copy(m.z16[a:b, i, 2 * i + hd:2 * i + hd + 1], m.ps[a:b, bank, P:P + 1])
                v.then_inc(kv_kept, 1)

            for n, (i, t) in enumerate(steps):
                dve.wait_ge(proj_done, G + n + 1)
                if n >= 3:
                    dve.drain()
                nc.vector.tensor_scalar(m.tmpk[n % 3][0:TP, :], m.ps[0:TP, (G + n) % BANKS, 0:P],
                                        0.0, None, ALU.min).then_inc(cut, 1)
                if n:
                    finish_k(n - 1)
                if t == 3 and i:
                    keep_pair(i - 1)
                if t < UP and QU + i + 1 < UNITS:
                    low((QU + i + 1) * UP + t)
            finish_k(len(steps) - 1)
            keep_pair(PAIRS - 1)
            nc.vector.tensor_copy(m.pick[0:HEADS, :, :].rearrange("p r (h d) -> p (r h) d", h=2),
                                  m.ident[0:HEADS, 0:HEADS].unsqueeze(2).to_broadcast([HEADS, HEADS, DH]))
            for s, (at, n) in enumerate(SPANS):
                den = m.den[0:HEADS, at:at + n]
                dve.wait_ge(den_done, s + 1)
                nc.vector.tensor_scalar(den, m.ps[0:HEADS, s, 0:n], 1e-6, None, ALU.add)
                dve.drain()
                nc.vector.reciprocal(den, den).then_inc(den_ready, 1)
            for g in range(NS * PAIRS):
                s, pr = divmod(g, PAIRS)
                at, n = SPANS[s]
                b = 3 + 2 * (g % 2)
                dve.wait_ge(spread, g + 1)
                nc.vector.tensor_tensor(m.qT[:, pr, at:at + n], m.ps[:, b, 0:n], m.tmp[g % 2][:, 0:n],
                                        ALU.mult).then_inc(nd_kept, 1)


def adjacency(nc, m, w, srcT, dstT, dst, rows):
    with ExitStack() as ctx:
        def sem(name):
            return ctx.enter_context(nc.semaphore(name))
        e_in, row_in, found, ranged = sem("e_in"), sem("row_in"), sem("found"), sem("ranged")
        bounds, hot_ready, hot_free = sem("bounds"), sem("hot_ready"), sem("hot_free")
        tile_done, tile_kept, zeroed = sem("tile_done"), sem("tile_kept"), sem("zeroed")
        esrc, edst, srcf, dstf = m.edge
        hots = [v[:, :].bitcast(BF16)[0:TP, 0:N] for v in m.hot]
        hotd = [v[:, :].bitcast(BF16)[0:TP, 0:TP] for v in m.hotd]
        banks = ((0, 4), (4, 4), (8, 2))
        block = ctx.enter_context(nc.Block())

        @block.sync
        def _(sp):
            sp.dma_start(m.dstrow[0:EP, :, :].bitcast(I32),
                         dst.rearrange("(p q e) -> p q e", p=EP, q=GROUPQ)).then_inc(row_in, 16)
            sp.dma_start(esrc[0:CE, :].bitcast(I32), srcT).then_inc(e_in, 16)
            sp.dma_start(edst[0:CE, :].bitcast(I32), dstT).then_inc(e_in, 16)
            sp.dma_start(m.rows[0:TP, DB:ROWLEN],
                         rows[:, DB:ROWLEN].to_broadcast([TP, ROWLEN - DB])).then_inc(w.rows_in, 16)
            sp.wait_ge(w.rows_in, 32)

        @block.gpsimd
        def _(pool):
            nc.gpsimd.iota(m.rng[0:EP, 6, 0:GROUPQ], pattern=[[1, GROUPQ]], base=1, channel_multiplier=GROUPQ,
                           allow_small_or_imprecise_dtypes=True)
            nc.gpsimd.iota(m.rng[0:EP, 7, 0:GROUPQ], pattern=[[-1, GROUPQ]], base=NGROUP, channel_multiplier=-GROUPQ,
                           allow_small_or_imprecise_dtypes=True).then_inc(found, 1)
            pool.wait_ge(found, 2)
            nc.gpsimd.partition_all_reduce(m.rng[0:EP, 3, :], m.rng[0:EP, 2, :], EP, RMAX).then_inc(ranged, 1)

        @block.vector
        def _(dve):
            dve.wait_ge(row_in, 16)
            nc.vector.tensor_copy(m.dstrowf[0:EP, :, :], m.dstrow[0:EP, :, :].bitcast(I32))
            dve.drain()
            lo, hi = m.rng[0:EP, 0, 0:GROUPQ], m.rng[0:EP, 1, 0:GROUPQ]
            nc.vector.tensor_reduce(lo, m.dstrowf[0:EP, :, :], AX, ALU.min)
            nc.vector.tensor_reduce(hi, m.dstrowf[0:EP, :, :], AX, ALU.max)
            dve.drain()
            for t in range(T):
                nc.vector.tensor_scalar(m.rngh[0:EP, t, 0, :], hi, float(t * TP), None, ALU.is_ge)
            dve.drain()
            for t in range(T):
                nc.vector.scalar_tensor_tensor(m.rngh[0:EP, t, 1, :], lo, float(t * TP + TP - 1),
                                               m.rngh[0:EP, t, 0, :], ALU.is_le, ALU.mult)
            dve.drain()
            dve.wait_ge(found, 1)
            for t in range(T):
                nc.vector.tensor_tensor(m.rngh[0:EP, t, 0, :], m.rngh[0:EP, t, 1, :], m.rng[0:EP, 6, 0:GROUPQ],
                                        ALU.mult)
            dve.drain()
            nc.vector.tensor_reduce(m.rng[0:EP, 2, 0:T], m.rngh[0:EP, :, 0, :], AX, ALU.max)
            for t in range(T):
                nc.vector.tensor_tensor(m.rngh[0:EP, t, 1, :], m.rngh[0:EP, t, 1, :], m.rng[0:EP, 7, 0:GROUPQ],
                                        ALU.mult)
            dve.drain()
            nc.vector.tensor_reduce(m.rng[0:EP, 2, T:2 * T], m.rngh[0:EP, :, 1, :], AX,
                                    ALU.max).then_inc(found, 1)
            dve.wait_ge(ranged, 1)
            end, low = m.rng[0:EP, 3, 0:T], m.rng[0:EP, 3, T:2 * T]
            first, last, count = m.rng[0:EP, 4, 0:T], m.rng[0:EP, 4, T:2 * T], m.rng[0:EP, 5, 0:T]
            nc.vector.tensor_scalar(first, low, -1.0, float(NGROUP), ALU.mult, ALU.add)
            dve.drain()
            nc.vector.tensor_scalar(first, first, float(NGROUP - 1), None, ALU.min)
            dve.drain()
            nc.vector.tensor_tensor(count, end, first, ALU.subtract)
            dve.drain()
            nc.vector.tensor_scalar(count, count, 1.0, None, ALU.max)
            nc.vector.tensor_copy(m.rngi[0:EP, 0, :], first)
            dve.drain()
            nc.vector.tensor_copy(m.rngi[0:EP, 1, :], count)
            nc.vector.tensor_tensor_scan(last, m.onesf[0:EP, 0:T], count, 0.0, ALU.mult, ALU.add)
            dve.drain()
            nc.vector.tensor_tensor(last, last, count, ALU.subtract)
            dve.drain()
            nc.vector.tensor_copy(m.rngi[0:EP, 2, :], last).then_inc(bounds, 1)
            dve.drain()
            dve.wait_ge(e_in, 32)
            nc.vector.tensor_copy(srcf[0:CE, :], esrc[0:CE, :].bitcast(I32))
            nc.vector.tensor_copy(dstf[0:CE, :], edst[0:CE, :].bitcast(I32))
            dve.drain()
            with dve.Fori(0, T) as t:
                first_group = dve.value_load(m.rngi[0:1, 0, bass.ds(t, 1)], min_val=0, max_val=NGROUP - 1)
                groups = dve.value_load(m.rngi[0:1, 1, bass.ds(t, 1)], min_val=1, max_val=NGROUP)
                before = dve.value_load(m.rngi[0:1, 2, bass.ds(t, 1)], min_val=0, max_val=(T - 1) * NGROUP)
                nodes = m.iota16[0:CE, bass.ds(t * TP, TP)]
                with dve.Fori(0, groups) as j:
                    group = dve.snap(nc.s_assert_within(
                        first_group + j, 0, NGROUP - 1,
                        skip_runtime_bounds_check_because="the count ends at the last group"))
                    done = dve.snap(before + j)
                    srcs, dsts = srcf[0:CE, bass.ds(group * CG, CG)], dstf[0:CE, bass.ds(group * CG, CG)]
                    for half in range(2):
                        dve.wait_ge(hot_free, done * 2 + half + 1)
                        for s in range(half * CG // 2, (half + 1) * CG // 2):
                            nc.vector.tensor_scalar(hots[s], m.iota16[0:CE, 0:N], srcs[:, s:s + 1], None, ALU.is_equal)
                            v = nc.vector.tensor_scalar(hotd[s], nodes, dsts[:, s:s + 1], None, ALU.is_equal)
                        v.then_inc(hot_ready, 1)

        @block.tensor
        def _(pe):
            pe.wait_ge(bounds, 1)
            pe.drain().then_inc(hot_free, 2)
            pe.drain().then_inc(tile_kept, 2)
            with pe.Fori(0, T // 2) as t2:
                for odd in range(2):
                    t = t2 * 2 + odd
                    groups = pe.value_load(m.rngi[0:1, 1, bass.ds(t, 1)], min_val=1, max_val=NGROUP)
                    before = pe.value_load(m.rngi[0:1, 2, bass.ds(t, 1)], min_val=0, max_val=(T - 1) * NGROUP)
                    pe.wait_ge(tile_kept, t2 * 2 + odd + 1)
                    for b, (s0, n) in enumerate(banks):
                        nc.tensor.matmul(m.ps[0:TP, 3 * odd + b, 0:n * TP], m.zeros[0:CE, 0:TP],
                                         m.zeros[0:CE, 0:n * TP], start=True, stop=False, skip_group_check=True)
                    with pe.Fori(0, groups) as j:
                        done = pe.snap(before + j)
                        for s in range(CG):
                            if s % (CG // 2) == 0:
                                pe.wait_ge(hot_ready, done * 2 + s // (CG // 2) + 1)
                            for b, (s0, n) in enumerate(banks):
                                for i in range(n):
                                    mm = nc.tensor.matmul(m.ps[0:TP, 3 * odd + b, i * TP:(i + 1) * TP],
                                                          hots[s][:, (s0 + i) * TP:(s0 + i + 1) * TP], hotd[s],
                                                          start=False, stop=False, skip_group_check=True)
                            if s % (CG // 2) == CG // 2 - 1:
                                mm.then_inc(hot_free, 1)
                    for b, (s0, n) in enumerate(banks):
                        mm = nc.tensor.matmul(m.ps[0:TP, 3 * odd + b, 0:n * TP], m.zeros[0:CE, 0:TP],
                                              m.zeros[0:CE, 0:n * TP], start=False, stop=True,
                                              skip_group_check=True)
                    mm.then_inc(tile_done, 1)

        @block.scalar
        def _(act):
            with act.Fori(0, T // 2) as t2:
                for odd in range(2):
                    act.wait_ge(tile_done, t2 * 2 + odd + 1)
                    for b, (s0, n) in enumerate(banks):
                        a = nc.scalar.activation(m.adjT[0:TP, s0:s0 + n, bass.ds((t2 * 2 + odd) * TP, TP)],
                                                 m.ps[0:TP, 3 * odd + b, 0:n * TP].rearrange("p (s d) -> p s d", s=n),
                                                 ACT.Copy)
                    a.then_inc(tile_kept, 1)

    with ExitStack() as ctx:
        block = ctx.enter_context(nc.Block())

        @block.vector
        def _(dve):
            for s in range(T):
                d = m.adjT[0:TP, s, s * TP:(s + 1) * TP]
                nc.vector.tensor_tensor(d, d, m.ident[0:TP, 0:TP], ALU.add)


def messages(nc, m, wa, wb):
    NS = len(SPANS)
    with ExitStack() as ctx:
        def sem(name):
            return ctx.enter_context(nc.semaphore(name))
        w_in, mm_done, kept, zz_done, zz_kept = sem("w_in"), sem("mm_done"), sem("kept"), sem("zz_done"), sem("zz_kept")
        var_ready, root_done, h_ready = sem("mvar_ready"), sem("mroot_done"), sem("h_ready")
        groups = [(f, s) for f in range(BC) for s in range(NS)]
        G = len(groups)
        block = ctx.enter_context(nc.Block())

        @block.sync
        def _(sp):
            sp.dma_start(m.wab[:, 0:LAYERS * BC, :], wa.rearrange("l (c p) n -> p (l c) n", p=P)).then_inc(w_in, 16)
            sp.dma_start(m.wab[:, LAYERS * BC:, :], wb.rearrange("l (c p) n -> p (l c) n", p=P)).then_inc(w_in, 16)

        @block.tensor
        def _(pe):
            pe.wait_ge(w_in, 32)
            for i in range(LAYERS):
                for g, half in ([(g, 0) for g in range(4)] + [(g, 1) for g in range(4)]
                                + [(g, half) for g in range(4, G) for half in range(2)]):
                    f, s = groups[g]
                    at, n = SPANS[s]
                    k = 2 * G * i + g
                    if k >= 4 and half == 0:
                        pe.wait_ge(kept, k - 3)
                    if i and g == 0:
                        pe.wait_ge(h_ready, 2 * i - 1 + half)
                    for c in range(half * HT, (half + 1) * HT):
                        mm = nc.tensor.matmul(m.ps[:, k % 4, 0:n], m.h[0:TP, c, f * P:(f + 1) * P],
                                              m.adjT[0:TP, c, at:at + n], start=(c == 0), stop=(c == T - 1))
                    if half:
                        mm.then_inc(mm_done, 1)
                for g, (f, s) in enumerate(groups):
                    at, n = SPANS[s]
                    k = 2 * G * i + G + g
                    pe.wait_ge(kept, max(k - 3, 2 * G * i + G))
                    for c in range(BC):
                        mm = nc.tensor.matmul(m.ps[:, k % 4, 0:n], m.wab[:, i * BC + c, f * P:(f + 1) * P],
                                              m.zT[:, c, at:at + n], start=(c == 0), stop=(c == BC - 1))
                    mm.then_inc(mm_done, 1)
                pe.wait_ge(kept, 2 * G * (i + 1))
                for t in range(T):
                    k = T * i + t
                    if k >= 4:
                        pe.wait_ge(zz_kept, k - 3)
                    for c in range(BC):
                        mm = nc.tensor.matmul(m.ps[0:TP, 4 + k % 4, 0:DB], m.aT[:, c, t * TP:(t + 1) * TP],
                                              m.wab[:, (LAYERS + i) * BC + c, :], start=(c == 0), stop=(c == BC - 1))
                    mm.then_inc(zz_done, 1)

        @block.scalar
        def _(act):
            for i in range(LAYERS):
                for g, (f, s) in enumerate(groups):
                    at, n = SPANS[s]
                    k = 2 * G * i + g
                    act.wait_ge(mm_done, k + 1)
                    nc.scalar.activation(m.zT[:, f, at:at + n], m.ps[:, k % 4, 0:n], ACT.Copy).then_inc(kept, 1)
                for g, (f, s) in enumerate(groups):
                    at, n = SPANS[s]
                    k = 2 * G * i + G + g
                    act.wait_ge(mm_done, k + 1)
                    nc.scalar.activation(m.aT[:, f, at:at + n], m.ps[:, k % 4, 0:n], ACT.Relu,
                                         bias=col(m, "ba", i * BC + f)).then_inc(kept, 1)
                for half in range(2):
                    v = slice(half * HT, (half + 1) * HT)
                    act.wait_ge(var_ready, 2 * i + half + 1)
                    nc.scalar.activation(m.rs[0:TP, v], m.ve[0:TP, v], ACT.Sqrt).then_inc(root_done, 1)

        @block.vector
        def _(dve):
            for i in range(LAYERS):
                for half in range(2):
                    a, b = half * HT, (half + 1) * HT
                    for t in range(a, b):
                        k = T * i + t
                        dve.wait_ge(zz_done, k + 1)
                        nc.vector.tensor_tensor(m.zz[0:TP, t, :], m.ps[0:TP, 4 + k % 4, 0:DB], row(m, "bb", i, DB),
                                                ALU.add).then_inc(zz_kept, 1)
                    dve.drain()
                    for t in range(a, b):
                        nc.vector.bn_stats(m.zstats[0:TP, t, :], m.zz[0:TP, t, :])
                    dve.drain()
                    for t in range(a, b):
                        nc.vector.bn_aggr(m.mv[0:TP, 2, t, :], m.zstats[0:TP, t, :])
                    dve.drain()
                    inverse_root(nc.vector, var_ready, root_done, 2 * i + half + 1, m.mv[0:TP, 2, a:b, 1],
                                 m.ve[0:TP, a:b], m.rs[0:TP, a:b], m.nt[0:TP, a:b])
                    for t in range(a, b):
                        nc.vector.tensor_scalar(m.zz[0:TP, t, :], m.zz[0:TP, t, :], m.mv[0:TP, 2, t, 0:1],
                                                m.rs[0:TP, t:t + 1], ALU.subtract, ALU.mult)
                    dve.drain()
                    z = m.zz[0:TP, a:b, :]
                    nc.vector.tensor_tensor(z, z, row(m, "ng", i, DB).unsqueeze(1).to_broadcast([TP, HT, DB]), ALU.mult)
                    dve.drain()
                    nc.vector.tensor_tensor(z, z, row(m, "nb", i, DB).unsqueeze(1).to_broadcast([TP, HT, DB]), ALU.add)
                    dve.drain()
                    nc.vector.scalar_tensor_tensor(m.h[0:TP, a:b, :], z, 0.0, m.h[0:TP, a:b, :], ALU.max,
                                                   ALU.add).then_inc(h_ready, 1)
                    dve.drain()


def combine(nc, m, w, x, wd1, wd2, wout, xn2, out):
    NS = len(SPANS)
    groups = [(f, s) for f in range(HC) for s in range(NS)]
    with ExitStack() as ctx:
        def sem(name):
            return ctx.enter_context(nc.semaphore(name))
        wd1_in, wbig_in, h_turned, h_kept, d_done, d_kept = (sem(n) for n in (
            "wd1_in", "wbig_in", "h_turned", "hT_kept", "d_done", "d_kept"))
        x_in, delta_done, mix_done, delta_used, mix_used = (sem(n) for n in (
            "cx_in", "delta_done", "mix_done", "delta_used", "mix_used"))
        var_ready, root_done, x1_ready, xn_ready, stored, xn_stored = (sem(n) for n in (
            "cvar_ready", "croot_done", "x1_ready", "xn2_ready", "stored", "xn_stored"))
        turned, kept, logit_done, logit_kept, pads = (sem(n) for n in (
            "cturned", "ckept", "logit_done", "logit_kept", "pads"))
        xt, u, mx, xo = m.tile
        xT = m.h[:, 0:DC // 2, :].rearrange("p a b -> p (a b)")[:, 0:DC * TP].rearrange("p (c n) -> p c n", c=DC)
        block = ctx.enter_context(nc.Block())

        @block.sync
        def _(sp):
            sp.dma_start(m.wd1, wd1.rearrange("(c p) n -> p c n", p=P)).then_inc(wd1_in, 16)
            sp.dma_start(m.wd2, wd2.rearrange("(c p) n -> p c n", p=P)).then_inc(wbig_in, 16)
            sp.dma_start(m.wout, wout.rearrange("(c p) n -> p c n", p=P)).then_inc(wbig_in, 16)
            sp.wait_ge(pads, 1)
            sp.dma_start(xn2[N:N + PADROWS, 0:512], m.zeros.bitcast(F32).unsqueeze(1).to_broadcast([P, 2, 256])
                         ).then_inc(stored, 16)
            sp.dma_start(xn2[N:N + PADROWS, 512:1024], m.zeros.bitcast(F32).unsqueeze(1).to_broadcast([P, 2, 256])
                         ).then_inc(stored, 16)
            sp.dma_start(out[N:N + PADROWS, 0:512], m.zeros.bitcast(F32).unsqueeze(1).to_broadcast([P, 2, 256])
                         ).then_inc(stored, 16)
            sp.dma_start(out[N:N + PADROWS, 512:1024], m.zeros.bitcast(F32).unsqueeze(1).to_broadcast([P, 2, 256])
                         ).then_inc(stored, 16)
            for t in range(T):
                sp.wait_ge(x1_ready, t + 1)
                sp.dma_start(out[t * TP:(t + 1) * TP, :], mx[0:TP, :]).then_inc(stored, 16)
                sp.wait_ge(xn_ready, t + 1)
                sp.dma_start(xn2[t * TP:(t + 1) * TP, :], xo[0:TP, :]).then_inc(xn_stored, 16)
            sp.wait_ge(stored, 16 * (T + 4))
            sp.wait_ge(xn_stored, 16 * T)

        @block.gpsimd
        def _(pool):
            pool.drain().then_inc(pads, 1)
            for t in range(T):
                if t:
                    pool.wait_ge(x1_ready, t)
                pool.dma_start(xt[0:TP, :], x[t * TP:(t + 1) * TP, :]).then_inc(x_in, 16)

        @block.tensor
        def _(pe):
            for t in range(T):
                if t >= 4:
                    pe.wait_ge(h_kept, t - 3)
                for f in range(BC):
                    mm = nc.tensor.transpose(m.ps[:, t % 4, f * TP:(f + 1) * TP], m.h[0:TP, t, f * P:(f + 1) * P],
                                             m.ident[0:TP, 0:TP])
                mm.then_inc(h_turned, 1)
            pe.wait_ge(h_kept, T)
            pe.wait_ge(wd1_in, 16)
            for g, (f, s) in enumerate(groups):
                at, n = SPANS[s]
                if g >= 4:
                    pe.wait_ge(d_kept, g - 3)
                for c in range(BC):
                    mm = nc.tensor.matmul(m.ps[:, g % 4, 0:n], m.wd1[:, c, f * P:(f + 1) * P],
                                          m.hT[:, c, at:at + n], start=(c == 0), stop=(c == BC - 1))
                mm.then_inc(d_done, 1)
            pe.wait_ge(d_kept, len(groups))
            pe.wait_ge(wbig_in, 32)

            def turn(t):
                pe.wait_ge(xn_ready, t + 1)
                if t:
                    pe.wait_ge(kept, t)
                for c in range(DC):
                    mm = nc.tensor.transpose(m.ps[:, 4 + c // 4, (c % 4) * TP:(c % 4 + 1) * TP],
                                             xo[0:TP, c * P:(c + 1) * P], m.ident[0:TP, 0:TP])
                mm.then_inc(turned, 1)

            def router(t):
                pe.wait_ge(kept, t + 1)
                if t:
                    pe.wait_ge(logit_kept, t)
                for c in range(DC):
                    mm = nc.tensor.matmul(m.ps[0:TP, 6, 0:E], xT[:, c, :], m.gatew[:, c, :],
                                          start=(c == 0), stop=(c == DC - 1))
                mm.then_inc(logit_done, 1)

            pe.wait_ge(w.gatew_in, 16)
            for t in range(T):
                if t:
                    pe.wait_ge(delta_used, t)
                for half in range(2):
                    for c in range(HC):
                        mm = nc.tensor.matmul(m.ps[0:TP, half, :], m.dT[:, c, t * TP:(t + 1) * TP],
                                              m.wd2[:, c, half * 512:half * 512 + 512],
                                              start=(c == 0), stop=(c == HC - 1))
                mm.then_inc(delta_done, 1)
                if t:
                    pe.wait_ge(mix_used, t)
                for half in range(2):
                    if t and half:
                        turn(t - 1)
                    for c in range(DC):
                        mm = nc.tensor.matmul(m.ps[0:TP, 2 + half, :], m.qT[:, c, t * TP:(t + 1) * TP],
                                              m.wout[:, c, half * 512:half * 512 + 512],
                                              start=(c == 0), stop=(c == DC - 1))
                mm.then_inc(mix_done, 1)
                if t:
                    router(t - 1)
            turn(T - 1)
            router(T - 1)

        @block.scalar
        def _(act):
            for t in range(T):
                act.wait_ge(h_turned, t + 1)
                nc.scalar.activation(m.hT[:, :, t * TP:(t + 1) * TP],
                                     m.ps[:, t % 4, 0:BC * TP].rearrange("p (f n) -> p f n", f=BC),
                                     ACT.Copy).then_inc(h_kept, 1)
            for g, (f, s) in enumerate(groups):
                at, n = SPANS[s]
                act.wait_ge(d_done, g + 1)
                nc.scalar.activation(m.dT[:, f, at:at + n], m.ps[:, g % 4, 0:n], ACT.Relu,
                                     bias=col(m, "bd1", f)).then_inc(d_kept, 1)

            def root(t, i):
                act.wait_ge(var_ready, 2 * t + i + 1)
                nc.scalar.activation(m.rs[0:TP, t:t + 1], m.ve[0:TP, t:t + 1], ACT.Sqrt).then_inc(root_done, 1)

            def keep_x(t):
                act.wait_ge(turned, t + 1)
                if t:
                    act.wait_ge(logit_done, t)
                for i in range(2):
                    a = nc.scalar.activation(xT[:, 4 * i:4 * i + 4, :],
                                             m.ps[:, 4 + i, 0:4 * TP].rearrange("p (c n) -> p c n", c=4), ACT.Copy)
                a.then_inc(kept, 1)

            def keep_logit(t):
                act.wait_ge(logit_done, t + 1)
                nc.scalar.activation(m.logit[0:TP, t, :], m.ps[0:TP, 6, 0:E], ACT.Copy).then_inc(logit_kept, 1)

            for t in range(T):
                root(t, 0)
                if t:
                    keep_x(t - 1)
                root(t, 1)
                if t:
                    keep_logit(t - 1)
            keep_x(T - 1)
            keep_logit(T - 1)

        @block.vector
        def _(dve):
            for t in range(T):
                dve.wait_ge(x_in, 16 * (t + 1))
                xt_, u_, mx_, xo_ = (v[0:TP, :] for v in (xt, u, mx, xo))
                nc.vector.tensor_scalar(u_, xt_, m.mr[0:TP, t, 0:1], m.mr[0:TP, t, 1:2], ALU.subtract, ALU.mult)
                dve.drain()
                nc.vector.tensor_tensor(u_, u_, row(m, "bd2"), ALU.add)
                dve.drain()
                dve.wait_ge(delta_done, t + 1)
                nc.vector.tensor_tensor(u_, m.ps[0:TP, 0:2, :].rearrange("p a b -> p (a b)"), u_,
                                        ALU.add).then_inc(delta_used, 1)
                dve.drain()
                for i in range(2):
                    nc.vector.bn_stats(m.stats[0:TP, 6 * i:6 * i + 6], u_[:, 512 * i:512 * i + 512])
                dve.drain()
                nc.vector.bn_aggr(m.mv[0:TP, 0, t, :], m.stats[0:TP, :])
                dve.drain()
                inverse_root(nc.vector, var_ready, root_done, 2 * t + 1, m.mv[0:TP, 0, t, 1:2],
                             m.ve[0:TP, t:t + 1], m.rs[0:TP, t:t + 1], m.nt[0:TP, t:t + 1])
                nc.vector.tensor_scalar(u_, u_, m.mv[0:TP, 0, t, 0:1], m.rs[0:TP, t:t + 1], ALU.subtract, ALU.mult)
                dve.drain()
                nc.vector.tensor_tensor(u_, u_, row(m, "og"), ALU.mult)
                dve.drain()
                nc.vector.tensor_tensor(u_, u_, row(m, "ob"), ALU.add)
                dve.drain()
                nc.vector.tensor_tensor(u_, u_, xt_, ALU.add)
                dve.drain()
                nc.vector.tensor_tensor(u_, u_, row(m, "bo"), ALU.add)
                dve.drain()
                dve.wait_ge(mix_done, t + 1)
                if t:
                    dve.wait_ge(stored, 16 * (t + 4))
                nc.vector.tensor_tensor(mx_, m.ps[0:TP, 2:4, :].rearrange("p a b -> p (a b)"), u_,
                                        ALU.add).then_inc(mix_used, 1)
                dve.drain()
                nc.vector.bn_stats(m.stats[0:TP, 0:6], mx_[:, 0:512]).then_inc(x1_ready, 1)
                nc.vector.bn_stats(m.stats[0:TP, 6:12], mx_[:, 512:1024])
                dve.drain()
                nc.vector.bn_aggr(m.mv[0:TP, 1, t, :], m.stats[0:TP, :])
                dve.drain()
                inverse_root(nc.vector, var_ready, root_done, 2 * t + 2, m.mv[0:TP, 1, t, 1:2],
                             m.ve[0:TP, t:t + 1], m.rs[0:TP, t:t + 1], m.nt[0:TP, t:t + 1])
                if t:
                    dve.wait_ge(xn_stored, 16 * t)
                    dve.wait_ge(turned, t)
                nc.vector.tensor_scalar(xo_, mx_, m.mv[0:TP, 1, t, 0:1], m.rs[0:TP, t:t + 1], ALU.subtract,
                                        ALU.mult).then_inc(xn_ready, 1)
                dve.drain()


def route(nc, m, tabd):
    with ExitStack() as ctx:
        def sem(name):
            return ctx.enter_context(nc.semaphore(name))
        shifted, exped, masked, ranked, tabled, tab_out, tab_in = (sem(n) for n in (
            "shifted", "rexped", "masked", "ranked", "tabled", "tab_out", "tab_in"))
        block = ctx.enter_context(nc.Block())

        def per_tile(v):
            return v[0:TP, :].unsqueeze(2).to_broadcast([TP, T, E])

        @block.scalar
        def _(act):
            act.wait_ge(shifted, 1)
            nc.scalar.activation(m.score[0:TP, :, :], m.logit[0:TP, :, :], ACT.Exp).then_inc(exped, 1)

        @block.vector
        def _(dve):
            logit, score, rep = (v[0:TP, :, :] for v in (m.logit, m.score, m.rep))
            top1, total, inv, topsum = (m.sc[:, i, :] for i in range(4))
            nc.vector.tensor_reduce(top1[0:TP, :], logit, AX, ALU.max)
            dve.drain()
            nc.vector.tensor_tensor(logit, logit, per_tile(top1), ALU.subtract).then_inc(shifted, 1)
            dve.wait_ge(exped, 1)
            nc.vector.tensor_reduce(total[0:TP, :], score, AX, ALU.add)
            dve.drain()
            nc.vector.reciprocal(inv[0:TP, :], total[0:TP, :])
            dve.drain()
            nc.vector.tensor_tensor(score, score, per_tile(inv), ALU.mult)
            dve.drain()
            for t in range(T):
                nc.vector.max(m.top[0:TP, t, :], m.score[0:TP, t, :])
            dve.drain()
            for t in range(T):
                nc.vector.match_replace(m.rep[0:TP, t, :], m.top[0:TP, t, :], m.score[0:TP, t, :], -1.0)
            dve.drain()
            nc.vector.tensor_scalar(m.mask[0:TP, :, :], rep, 0.0, None, ALU.is_lt)
            nc.vector.tensor_reduce(topsum[0:TP, :], m.top[0:TP, :, :], AX, ALU.add)
            nc.vector.memset(m.mprev[0:TP, 0, :], 0.0)
            dve.drain()
            for t in range(T):
                v = nc.vector.tensor_tensor(m.mprev[0:TP, t + 1, :], m.mprev[0:TP, t, :], m.mask[0:TP, t, :], ALU.add)
                if t == T - 1:
                    v.then_inc(masked, 1)
                dve.drain()
            nc.vector.tensor_scalar(topsum[0:TP, :], topsum[0:TP, :], 1e-20, None, ALU.add)
            dve.drain()
            nc.vector.reciprocal(inv[0:TP, :], topsum[0:TP, :])
            dve.drain()
            nc.vector.tensor_tensor(score, score, m.mask[0:TP, :, :], ALU.mult)
            dve.drain()
            nc.vector.tensor_tensor(score, score, per_tile(inv), ALU.mult)
            for t in range(T):
                nc.vector.memset(m.sel[0:TP, t, :, 0], float(t))
            nc.vector.memset(m.sel[0:TP, :, :, 2], 1.0)
            nc.vector.tensor_scalar(m.sel[0:TP, :, :, 1], m.onesf[0:TP, 0:1].unsqueeze(1).to_broadcast([TP, T, E]),
                                    m.pos[0:TP, 0:1], None, ALU.mult)
            dve.drain()
            nc.vector.tensor_copy(m.sel[0:TP, :, :, 3], score)
            dve.drain()
            nc.vector.tensor_tensor(score, score, m.sel[0:TP, :, :, 3], ALU.subtract)
            dve.drain()
            nc.vector.tensor_copy(m.sel[0:TP, :, :, 4], score)
            dve.drain()
            nc.vector.tensor_tensor(score, score, m.sel[0:TP, :, :, 4], ALU.subtract)
            dve.drain()
            nc.vector.tensor_copy(m.sel[0:TP, :, :, 5], score)
            dve.wait_ge(ranked, 1)
            for i in range(2):
                nc.vector.scalar_tensor_tensor(
                    m.place[0:TP, i * HT:(i + 1) * HT, :],
                    m.ps[0:TP, i, 0:HT * E].rearrange("p (t e) -> p t e", t=HT), 1.0,
                    m.mask[0:TP, i * HT:(i + 1) * HT, :], ALU.add, ALU.mult)
            n, nb, end, before, cmp, prod = (m.cnt[:, i, :] for i in range(6))
            nc.vector.tensor_copy(n, m.ps[:, 2, 0:E])
            dve.drain()
            nc.vector.tensor_scalar(m.place[0:TP, :, :], m.place[0:TP, :, :], -1.0, None, ALU.add)
            nc.vector.memset(nb, 1.0)
            dve.drain()
            for j in range(1, BMAX):
                nc.vector.scalar_tensor_tensor(nb, n, float(P * j), nb, ALU.is_gt, ALU.add)
                dve.drain()
            nc.vector.tensor_tensor_scan(end, m.onesf[:, 0:E], nb, 0.0, ALU.mult, ALU.add)
            dve.drain()
            nc.vector.tensor_tensor(before, end, nb, ALU.subtract)
            dve.drain()
            nc.vector.tensor_copy(m.nbi[:, 0, :], nb)
            nc.vector.tensor_copy(m.nbi[:, 1, :], before)
            nc.vector.tensor_scalar(m.nbi[:, 2, :], nb, -1.0, None, ALU.add)
            nc.vector.tensor_scalar(m.nbi[:, 3, :], end, -1.0, None, ALU.add)
            nc.vector.tensor_copy(m.tot[:], end[:, E - 1:E])
            for h in range(2):
                a, s = m.cnt[:, 6, 0:1], m.cnt[:, 6, 1:2]
                dve.drain()
                nc.vector.tensor_scalar(cmp, end, m.pos[:, h:h + 1], None, ALU.is_le)
                dve.drain()
                nc.vector.tensor_reduce(a, cmp, AX, ALU.add)
                nc.vector.tensor_tensor(prod, cmp, nb, ALU.mult)
                dve.drain()
                nc.vector.tensor_reduce(s, prod, AX, ALU.add)
                nc.vector.tensor_scalar(a, a, float(E - 1), None, ALU.min)
                dve.drain()
                nc.vector.tensor_tensor(s, m.pos[:, h:h + 1], s, ALU.subtract)
                nc.vector.tensor_copy(m.tabp[:, h, 0:1], a)
                dve.drain()
                nc.vector.tensor_scalar(s, s, float(BMAX - 1), float(P), ALU.min, ALU.mult)
                dve.drain()
                nc.vector.tensor_copy(m.tabp[:, h, 1:2], s).then_inc(tabled, 1)

        @block.tensor
        def _(pe):
            pe.wait_ge(masked, 1)
            for t in range(T):
                o = m.ps[0:TP, t // HT, (t % HT) * E:(t % HT + 1) * E]
                nc.tensor.matmul(o, m.before[0:TP, 0:TP], m.mask[0:TP, t, :], start=(t % HT == 0), stop=False,
                                 skip_group_check=True)
                nc.tensor.matmul(o, m.ones[0:TP, 0:TP], m.mprev[0:TP, t, :], start=False, stop=True,
                                 skip_group_check=True)
            nc.tensor.matmul(m.ps[:, 2, 0:E], m.ones[0:TP, :], m.mprev[0:TP, T, :], start=True,
                             stop=True).then_inc(ranked, 1)

        @block.sync
        def _(sp):
            sp.wait_ge(tabled, 2)
            for h in range(2):
                sp.dma_start(tabd[h * P:(h + 1) * P, :], m.tabp[:, h, :]).then_inc(tab_out, 16)
            sp.wait_ge(tab_out, 32)
            sp.dma_start(m.tab[:], tabd[0:TAB, :].rearrange("b k -> (b k)").unsqueeze(0)).then_inc(tab_in, 16)
            sp.wait_ge(tab_in, 16)


def experts(nc, m, weights, xn2, out):
    with ExitStack() as ctx:
        def sem(name):
            return ctx.enter_context(nc.semaphore(name))
        raw_in = [sem(f"raw_in{i}") for i in range(RAW)]
        hi_done, lo_done = sem("hi_done"), sem("lo_done")
        hot_ready, listed, meta_ready, gathered = sem("ehot_ready"), sem("listed"), sem("meta_ready"), sem("gathered")
        x_turned, xhi_ready, xT_ready, gu_done, silu_ready = (sem(n) for n in (
            "x_turned", "xhi_ready", "xT_ready", "gu_done", "silu_ready"))
        taken = sem("taken")
        h_ready, h_turned, hhi_ready, hT_ready, down_done, y_ready, added, landed = (sem(n) for n in (
            "eh_ready", "eh_turned", "hhi_ready", "ehT_ready", "down_done", "y_ready", "added", "landed"))
        block = ctx.enter_context(nc.Block())

        def piece(v, q):
            return v[:, q * PIECE:(q + 1) * PIECE]

        @block.sync
        def _(sp):
            for q in range(PIECES):
                if q >= RAW:
                    sp.wait_ge(lo_done, q - RAW + 1)
                sp.dma_start(m.raw[q % RAW], weights[0, q]).then_inc(raw_in[q % RAW], 16)
            with sp.Fori(1, E) as e:
                for q in range(PIECES):
                    sp.wait_ge(lo_done, e * PIECES + (q - RAW + 1))
                    sp.dma_start(m.raw[q % RAW], weights[bass.ds(e, 1), q].rearrange("o p n -> (o p) n")
                                 ).then_inc(raw_in[q % RAW], 16)

        @block.tensor
        def _(pe):
            def make_list():
                for t in range(T):
                    mm = nc.tensor.matmul(m.ps[:, 1, 2 * P:2 * P + 6], m.oh[0:TP, t, :], m.sw[0:TP, t, :],
                                          start=(t == 0), stop=(t == T - 1))
                mm.then_inc(listed, 1)

            def turn_x(first, last):
                for c in range(first, last):
                    mm = nc.tensor.transpose(m.ps[:, 6 + c // 4, (c % 4) * P:(c % 4 + 1) * P],
                                             m.xg[:, c * P:(c + 1) * P], m.ident[:])
                return mm

            def product(to, left, right, chunks, width, parts=PARTS, first=True, last=True, at=0):
                for c in chunks:
                    for half, o in enumerate(to):
                        for i, j in parts:
                            mm = nc.tensor.matmul(o, left[i][:, c, :], right[j][:, c, at + half * width:at + (half + 1) * width],
                                                  start=(first and c == chunks[0] and (i, j) == parts[0]),
                                                  stop=(last and c == chunks[-1] and (i, j) == parts[-1]))
                return mm

            for b in range(2):
                pe.wait_ge(hot_ready, b + 1)
                if b:
                    pe.wait_ge(taken, b)
                make_list()
            pe.wait_ge(gathered, 16)
            turn_x(0, DC).then_inc(x_turned, 1)
            with pe.Fori(0, E) as e:
                blocks = pe.value_load(m.nbi[0:1, 0, bass.ds(e, 1)], min_val=1, max_val=BMAX)
                before = pe.value_load(m.nbi[0:1, 1, bass.ds(e, 1)], min_val=0, max_val=MAXB)
                with pe.Fori(0, blocks) as j:
                    k = pe.snap(before + j)
                    pe.wait_ge(xT_ready, k * 2 + 2)
                    pe.wait_ge(lo_done, e * PIECES + MP)
                    for i in range(2):
                        product([m.ps[:, i, 0:FH]], m.xT, m.gate, range(DC), FH, at=i * FH).then_inc(gu_done, 1)
                    pe.wait_ge(lo_done, e * PIECES + 2 * MP)
                    for i in range(2):
                        product([m.ps[:, 2 + i, 0:FH]], m.xT, m.up, range(DC), FH, at=i * FH).then_inc(gu_done, 1)
                    pe.wait_ge(gathered, k * 16 + 32)
                    turn_x(0, XFIRST)
                    pe.wait_ge(hot_ready, k + 3)
                    pe.wait_ge(silu_ready, k * 2 + 2)
                    make_list()
                    pe.wait_ge(h_ready, k + 1)
                    for c in range(FC):
                        mm = nc.tensor.transpose(m.ps[:, c // 4, (c % 4) * P:(c % 4 + 1) * P],
                                                 m.ex[:, c * P:(c + 1) * P], m.ident[:])
                    mm.then_inc(h_turned, 1)
                    turn_x(XFIRST, DC).then_inc(x_turned, 1)
                    pe.wait_ge(lo_done, e * PIECES + 3 * MP)
                    pe.wait_ge(y_ready, k * 2 + 2)
                    y = [m.ps[:, 4 + i, :] for i in range(2)]
                    pe.wait_ge(hhi_ready, k * 2 + 1)
                    product(y, m.hxT, m.down, range(4), 512, parts=PARTS[:2], last=False)
                    pe.wait_ge(hhi_ready, k * 2 + 2)
                    product(y, m.hxT, m.down, range(4, FC), 512, parts=PARTS[:2], first=False, last=False)
                    pe.wait_ge(hT_ready, k * 2 + 2)
                    product(y, m.hxT, m.down, range(FC), 512, parts=PARTS[2:], first=False).then_inc(down_done, 1)

        @block.scalar
        def _(act):
            def high(e, q):
                act.wait_ge(raw_in[q % RAW], e * (16 * PIECES // RAW) + 16 * (q // RAW) + 16)
                nc.scalar.activation(piece(m.whi, q), m.raw[q % RAW], ACT.Copy).then_inc(hi_done, 1)

            def keep_x(b):
                act.wait_ge(x_turned, b + 1)
                for i in range(2):
                    nc.scalar.activation(m.xT[0][:, 4 * i:4 * i + 4, :],
                                         m.ps[:, 6 + i, :].rearrange("p (c n) -> p c n", c=4),
                                         ACT.Copy).then_inc(xhi_ready, 1)

            def take_list():
                nc.scalar.activation(m.selc[:], m.ps[:, 1, 2 * P:2 * P + 6], ACT.Copy).then_inc(taken, 1)

            def block_work(k, more, e):
                act.wait_ge(gu_done, k * 4 + 2)
                if more:
                    for q in range(AHEAD):
                        high(e + 1, q)
                for half in range(2):
                    nc.scalar.activation(m.ex[:, half * FH:(half + 1) * FH], m.ps[:, half, 0:FH],
                                         ACT.Silu).then_inc(silu_ready, 1)
                if more:
                    for q in range(AHEAD, MP):
                        high(e + 1, q)
                act.wait_ge(h_turned, k + 1)
                nc.scalar.activation(m.hxT[0][:, 0:4, :], m.ps[:, 0, :].rearrange("p (c n) -> p c n", c=4),
                                     ACT.Copy).then_inc(hhi_ready, 1)
                take_list()
                nc.scalar.activation(m.hxT[0][:, 4:6, :], m.ps[:, 1, 0:2 * P].rearrange("p (c n) -> p c n", c=2),
                                     ACT.Copy).then_inc(hhi_ready, 1)
                if more:
                    for q in range(MP, MP + AHEAD):
                        high(e + 1, q)
                keep_x(k + 1)
                if more:
                    for q in range(MP + AHEAD, 2 * MP):
                        high(e + 1, q)
                act.wait_ge(meta_ready, k + 3)
                act.wait_ge(landed, k + 1)
                act.wait_ge(down_done, k + 1)
                for half in range(2):
                    nc.scalar.activation(m.yo[:, half * 512:half * 512 + 512], m.ps[:, 4 + half, :], ACT.Copy,
                                         scale=m.meta[:, 2, 2:3]).then_inc(y_ready, 1)
                if more:
                    for q in range(2 * MP, 3 * MP):
                        high(e + 1, q)

            act.wait_ge(listed, 1)
            take_list()
            act.wait_ge(meta_ready, 1)
            act.wait_ge(listed, 2)
            take_list()
            for q in range(PIECES):
                high(0, q)
                if q == MP - 1:
                    keep_x(0)
            with act.Fori(0, E - 1) as e:
                before = act.value_load(m.nbi[0:1, 1, bass.ds(e, 1)], min_val=0, max_val=MAXB)
                others = act.value_load(m.nbi[0:1, 2, bass.ds(e, 1)], min_val=0, max_val=BMAX - 1)
                with act.If(others > 0):
                    with act.Fori(0, others) as j:
                        block_work(act.snap(before + j), False, e)
                last = act.value_load(m.nbi[0:1, 3, bass.ds(e, 1)], min_val=0, max_val=MAXB)
                block_work(last, True, e)
            blocks = act.value_load(m.nbi[0:1, 0, E - 1:E], min_val=1, max_val=BMAX)
            before = act.value_load(m.nbi[0:1, 1, E - 1:E], min_val=0, max_val=MAXB)
            with act.Fori(0, blocks) as j:
                block_work(act.snap(before + j), False, None)

        @block.vector
        def _(dve):
            def low(e, q):
                dve.wait_ge(hi_done, e * PIECES + q + 1)
                nc.vector.tensor_tensor(piece(m.wlo, q), m.raw[q % RAW], piece(m.whi, q).bitcast(F32),
                                        ALU.subtract).then_inc(lo_done, 1)

            def one_hot(b):
                e = dve.value_load(m.tab[0:1, bass.ds(b * 2, 1)], min_val=0, max_val=E - 1)
                at = dve.value_load(m.tab[0:1, bass.ds(b * 2 + 1, 1)], min_val=0, max_val=(BMAX - 1) * P)
                nc.vector.tensor_tensor(m.oh[0:TP, :, :],
                                        m.place[0:TP, :, bass.ds(e, 1)].to_broadcast([TP, T, P]),
                                        m.iota16[0:TP, bass.ds(at, P)].unsqueeze(1).to_broadcast([TP, T, P]),
                                        ALU.is_equal)
                nc.vector.tensor_copy(m.sw[0:TP, :, :].unsqueeze(2),
                                      m.sel[0:TP, :, bass.ds(e, 1), :]).then_inc(hot_ready, 1)

            def low_x(b):
                for i in range(2):
                    dve.wait_ge(xhi_ready, b * 2 + i + 1)
                    nc.vector.tensor_tensor(m.xT[1][:, 4 * i:4 * i + 4, :],
                                            m.ps[:, 6 + i, :].rearrange("p (c n) -> p c n", c=4),
                                            m.xT[0][:, 4 * i:4 * i + 4, :].bitcast(F32),
                                            ALU.subtract).then_inc(xT_ready, 1)

            def block_work(k, more, e):
                if more:
                    for q in range(AHEAD):
                        low(e + 1, q)
                dve.wait_ge(silu_ready, k * 2 + 2)
                for half in range(2):
                    dve.wait_ge(gu_done, k * 4 + 3 + half)
                    ex = m.ex[:, half * FH:(half + 1) * FH]
                    v = nc.vector.tensor_tensor(ex, m.ps[:, 2 + half, 0:FH], ex, ALU.mult)
                v.then_inc(h_ready, 1)
                if more:
                    for q in range(AHEAD, MP):
                        low(e + 1, q)
                for a, b, bank in ((0, 4, 0), (4, 6, 1)):
                    dve.wait_ge(hhi_ready, k * 2 + bank + 1)
                    nc.vector.tensor_tensor(m.hxT[1][:, a:b, :],
                                            m.ps[:, bank, 0:(b - a) * P].rearrange("p (c n) -> p c n", c=b - a),
                                            m.hxT[0][:, a:b, :].bitcast(F32), ALU.subtract).then_inc(hT_ready, 1)
                if more:
                    for q in range(MP, MP + AHEAD):
                        low(e + 1, q)
                low_x(k + 1)
                dve.wait_ge(listed, k + 3)
                one_hot(k + 3)
                if more:
                    for q in range(MP + AHEAD, 3 * MP):
                        low(e + 1, q)

            dve.drain().then_inc(y_ready, 2)
            one_hot(0)
            for b in range(1, 3):
                dve.wait_ge(listed, b)
                one_hot(b)
            for q in range(PIECES):
                low(0, q)
                if q == MP - 1:
                    low_x(0)
            with dve.Fori(0, E - 1) as e:
                before = dve.value_load(m.nbi[0:1, 1, bass.ds(e, 1)], min_val=0, max_val=MAXB)
                others = dve.value_load(m.nbi[0:1, 2, bass.ds(e, 1)], min_val=0, max_val=BMAX - 1)
                with dve.If(others > 0):
                    with dve.Fori(0, others) as j:
                        block_work(dve.snap(before + j), False, e)
                last = dve.value_load(m.nbi[0:1, 3, bass.ds(e, 1)], min_val=0, max_val=MAXB)
                block_work(last, True, e)
            blocks = dve.value_load(m.nbi[0:1, 0, E - 1:E], min_val=1, max_val=BMAX)
            before = dve.value_load(m.nbi[0:1, 1, E - 1:E], min_val=0, max_val=MAXB)
            with dve.Fori(0, blocks) as j:
                block_work(dve.snap(before + j), False, None)

        @block.gpsimd
        def _(pool):
            total = pool.value_load(m.tot[0:1, 0:1], min_val=E, max_val=MAXB)

            def meta(first):
                c = m.selc
                nc.gpsimd.tensor_tensor(m.wpart[:], c[:, 3:4], c[:, 4:5], ALU.add)
                if not first:
                    nc.gpsimd.tensor_copy(m.metai[:, 2, :], m.metai[:, 1, :])
                    pool.drain()
                    nc.gpsimd.tensor_copy(m.metai[:, 1, :], m.metai[:, 0, :])
                pool.drain()
                nc.gpsimd.tensor_scalar(m.metai[:, 0, 0:1], c[:, 0:1], float(TP), c[:, 1:2], ALU.mult, ALU.add)
                nc.gpsimd.tensor_scalar(m.metai[:, 0, 1:2], c[:, 2:3], m.pos[:, 3:4], m.pos[:, 2:3], ALU.mult, ALU.add)
                nc.gpsimd.tensor_tensor(m.meta[:, 0, 2:3], m.wpart[:], c[:, 5:6], ALU.add).then_inc(meta_ready, 1)
                pool.drain()

            def gather():
                nc.gpsimd.tensor_tensor(m.idx[:, 0:1], m.metai[:, 0, 0:1], m.metai[:, 0, 1:2], ALU.add)
                pool.drain()
                pool.indirect_dma_start(out=m.xg, out_offset=None, in_=xn2,
                                        in_offset=bass.IndirectOffsetOnAxis(ap=m.idx[:, 0:1], axis=0)
                                        ).then_inc(gathered, 16)

            pool.sem_inc(landed, 1)
            nc.gpsimd.memset(m.meta[:], 0.0)
            pool.wait_ge(taken, 1)
            meta(first=True)
            gather()
            pool.wait_ge(taken, 2)
            meta(first=False)
            pool.wait_ge(x_turned, 1)
            gather()
            with pool.Fori(0, total) as k:
                pool.wait_ge(taken, k + 3)
                meta(first=False)
                pool.wait_ge(x_turned, k + 2)
                gather()
                pool.wait_ge(y_ready, k * 2 + 4)
                nc.gpsimd.tensor_tensor(m.idx[:, 1:2], m.metai[:, 2, 0:1], m.metai[:, 2, 1:2], ALU.add)
                pool.drain()
                pool.indirect_dma_start(out=out, out_offset=bass.IndirectOffsetOnAxis(ap=m.idx[:, 1:2], axis=0),
                                        in_=m.yo, in_offset=None, compute_op=ALU.add).then_inc(added, 16)
                pool.wait_ge(added, k * 16 + 16)
                pool.sem_inc(landed, 1)
            pool.wait_ge(gathered, total * 16 + 32)


def kernel(x, src, dst, L0_gnn_ln_in_g, L0_gnn_ln_in_b, L0_gnn_W1, L0_gnn_b1, L0_gnn_W2, L0_gnn_b2,
           L0_gnn_layer_Wa, L0_gnn_layer_ba, L0_gnn_layer_Wb, L0_gnn_layer_bb, L0_gnn_layer_ng,
           L0_gnn_layer_nb, L0_gnn_Wd1, L0_gnn_bd1, L0_gnn_Wd2, L0_gnn_bd2, L0_gnn_out_g, L0_gnn_out_b,
           L0_mix_w_qkv, L0_mix_w_out, L0_mix_b_out, L0_ffn_gate_w, L0_ffn_w_gate, L0_ffn_w_up,
           L0_ffn_w_down):
    import numpy as np
    import concourse.bacc as bacc
    from concourse.bass_utils import run_bass_kernel_spmd

    def arr(a):
        return np.ascontiguousarray(a)

    def on_partitions(v):
        return np.asarray(v).reshape(-1, P).T

    def chunked(wt):
        wt = np.asarray(wt)
        e, n, k = wt.shape
        return arr(wt.reshape(e, n, k // P, P).transpose(0, 3, 2, 1)).reshape(e, P, k // P * n)

    cols = arr(np.concatenate([on_partitions(v) for v in (
        L0_gnn_ln_in_g, L0_gnn_ln_in_b, L0_gnn_b1, L0_gnn_layer_ba, L0_gnn_bd1)], axis=1))
    rows = arr(np.concatenate([np.asarray(v).reshape(1, -1) for v in (
        L0_gnn_b2, L0_gnn_layer_bb, L0_gnn_layer_ng, L0_gnn_layer_nb, L0_gnn_bd2, L0_gnn_out_g,
        L0_gnn_out_b, L0_mix_b_out)], axis=1))
    pieces = arr(np.concatenate([chunked(v) for v in (L0_ffn_w_gate, L0_ffn_w_up, L0_ffn_w_down)], axis=2)
                 .reshape(E, P, PIECES, PIECE).transpose(0, 2, 1, 3))
    wq, wk, wv = np.split(np.asarray(L0_mix_w_qkv), 3, axis=1)
    units = np.concatenate([wq.reshape(D, QU, UNIT),
                            np.stack([wk.reshape(D, PAIRS, P), wv.reshape(D, PAIRS, P)], axis=2)
                            .reshape(D, PAIRS, UNIT)], axis=1)
    units = arr(units.reshape(UP, UCH, P, UNITS, UNIT).transpose(3, 0, 2, 1, 4)).reshape(
        UNITS, UP, P, UCH * UNIT)
    arrays = {
        "x": arr(x), "srcT": arr(np.asarray(src).reshape(CHUNKS, CE).T),
        "dstT": arr(np.asarray(dst).reshape(CHUNKS, CE).T), "dst": arr(dst), "cols": cols, "rows": rows,
        "w1": arr(L0_gnn_W1), "w2": arr(L0_gnn_W2), "wa": arr(L0_gnn_layer_Wa), "wb": arr(L0_gnn_layer_Wb),
        "wd1": arr(L0_gnn_Wd1), "wd2": arr(L0_gnn_Wd2), "wqkv": units, "wout": arr(L0_mix_w_out),
        "gatew": chunked(np.asarray(L0_ffn_gate_w)[None])[0],
        "weights": pieces,
    }
    nc = bacc.Bacc("TRN2", target_bir_lowering=False, num_devices=1)
    args = {n: nc.dram_tensor("in_" + n, a.shape, mybir.dt.from_np(a.dtype), kind="ExternalInput").ap()
            for n, a in arrays.items()}
    out = nc.dram_tensor("out", (N + PADROWS, D), F32, kind="ExternalOutput").ap()
    build(nc, **args, out=out)
    r = run_bass_kernel_spmd(nc, [{"in_" + n: a for n, a in arrays.items()}], core_ids=[0])
    return r.results[0]["out"][0:N]
```
